# Optimizing a Trainium2 kernel written in Bass

```python
import numpy as np
import jax
import jax.numpy as jnp

def _softmax(x, axis=-1):
    return jax.nn.softmax(x, axis=axis)

def _gelu(x):
    return jax.nn.gelu(x, approximate=True)

def _silu(x):
    return jax.nn.silu(x)

def _sigmoid(x):
    return jax.nn.sigmoid(x)

def _layernorm(x, axis=-1, eps=1e-05):
    m = jnp.mean(x, axis=axis, keepdims=True)
    v = jnp.var(x, axis=axis, keepdims=True)
    return (x - m) / jnp.sqrt(v + eps)

def _scatter_add(tgt, idx, src, axis=0):
    return tgt.at[idx].add(src)

def _segment_sum(src, seg, n):
    return jax.ops.segment_sum(src, seg, n)
kernel_name = 'mk_lm_tower_d2_tok_ids256_r4_93718d'

def setup_inputs(seed: int=0):
    np.random.seed(seed)
    _w = jnp.asarray

    def _rec_inputs():
        import jax
        import jax.numpy as jnp
        _rk = jax.random.key(seed)
        x = jax.random.randint(jax.random.fold_in(_rk, 1), (32, 512), 0, 64, jnp.int32)
        return x
    x = _rec_inputs()

    def _L0_tok_setup():
        import jax, jax.numpy as jnp
        import numpy as np
        B, T, D = (32, 1024, 64)
        LN_EPS = 1e-05
        key = jax.random.key(seed)
        k0, k1, k2 = jax.random.split(key, 3)
        byte_ids = jax.random.randint(k0, (B, T), 0, 64, dtype=jnp.int32)
        freq_bands = jnp.ones((D // 2,), jnp.float32)
        w1 = jax.random.normal(k1, (D, 2 * D), jnp.float32) * (1.0 / np.sqrt(D))
        b1 = jnp.zeros((2 * D,), jnp.float32)
        gamma = jnp.ones((2 * D,), jnp.float32)
        beta = jnp.zeros((2 * D,), jnp.float32)
        w2 = jax.random.normal(k2, (2 * D, D), jnp.float32) * (1.0 / np.sqrt(2 * D))
        b2 = jnp.zeros((D,), jnp.float32)
        return dict(byte_ids=byte_ids, freq_bands=freq_bands, w1=w1, b1=b1, gamma=gamma, beta=beta, w2=w2, b2=b2)
    _L0_tok_all = _L0_tok_setup()
    _L0_tok_in = {k: v for k, v in _L0_tok_all.items() if k in ('freq_bands', 'w1', 'b1', 'gamma', 'beta', 'w2', 'b2')}
    del _L0_tok_all

    def _L0_attn_setup():
        import jax, jax.numpy as jnp
        import numpy as np
        B, L, E = (2, 2048, 64)
        H, K, DIL = (8, 31, 2)
        DH = E // H

        def neighbor_indices(length, k, d):
            i = jnp.arange(length)
            g = i % d
            p = i // d
            lg = (length - g + d - 1) // d
            start = jnp.clip(p - k // 2, 0, lg - k)
            t = jnp.arange(k)
            return g[:, None] + (start[:, None] + t[None, :]) * d
        key = jax.random.key(seed)
        k0, k1, k2 = jax.random.split(key, 3)
        s = 0.02
        return {'x': jax.random.normal(k0, (B, L, E), jnp.float32), 'w_qkv': jax.random.normal(k1, (E, 3 * E), jnp.float32) * s, 'b_qkv': jnp.zeros((3 * E,), jnp.float32), 'w_proj': jax.random.normal(k2, (E, E), jnp.float32) * s, 'b_proj': jnp.zeros((E,), jnp.float32)}
    _L0_attn_all = _L0_attn_setup()
    _L0_attn_in = {k: v for k, v in _L0_attn_all.items() if k in ('w_qkv', 'b_qkv', 'w_proj', 'b_proj')}
    del _L0_attn_all

    def _L0_ffn_setup():
        import jax, jax.numpy as jnp
        import numpy as np
        NUM_EXPERTS = 8
        TOP_K = 2
        B, S, D = (8, 2048, 64)

        def _moe(tokens, router_w, w1, b1, w2, b2):
            N = tokens.shape[0]
            E = router_w.shape[0]
            logits = tokens.astype(jnp.float32) @ router_w.astype(jnp.float32).T
            probs = jax.nn.softmax(logits, axis=-1)
            rw, re = jax.lax.top_k(probs, TOP_K)
            if TOP_K > 1:
                rw = rw / jnp.maximum(rw.sum(-1, keepdims=True), 1e-12)
            rw = rw.astype(tokens.dtype)
            combine = jnp.zeros((N, E), tokens.dtype).at[jnp.arange(N)[:, None], re].set(rw)
            out = tokens
            for e in range(E):
                h = jax.nn.gelu(tokens @ w1[e] + b1[e], approximate=False)
                y = h @ w2[e] + b2[e]
                out = out + combine[:, e:e + 1] * y
            return out
        key = jax.random.key(seed)
        ks = jax.random.split(key, 4)
        scale = 1.0 / np.sqrt(D).astype(np.float32)
        return {'input_embeddings': jax.random.normal(ks[0], (B, S, D), jnp.float32), 'router_w': jax.random.normal(ks[1], (NUM_EXPERTS, D), jnp.float32) * scale, 'w1': jax.random.normal(ks[2], (NUM_EXPERTS, D, D), jnp.float32) * scale, 'b1': jnp.zeros((NUM_EXPERTS, D), jnp.float32), 'w2': jax.random.normal(ks[3], (NUM_EXPERTS, D, D), jnp.float32) * scale, 'b2': jnp.zeros((NUM_EXPERTS, D), jnp.float32)}
    _L0_ffn_all = _L0_ffn_setup()
    _L0_ffn_in = {k: v for k, v in _L0_ffn_all.items() if k in ('router_w', 'w1', 'b1', 'w2', 'b2')}
    del _L0_ffn_all

    def _L1_attn_setup():
        import jax, jax.numpy as jnp
        import numpy as np
        EMBED_DIM = 64
        SEQ_LEN = 1024
        BATCH = 8
        ALPHA = 0.99
        key = jax.random.key(seed)
        k_x, k_w, k_b = jax.random.split(key, 3)
        x = jax.random.normal(k_x, (BATCH, SEQ_LEN, EMBED_DIM), dtype=jnp.float32)
        Wqkv = jax.random.normal(k_w, (EMBED_DIM, 3 * EMBED_DIM), dtype=jnp.float32) * EMBED_DIM ** (-0.5)
        bqkv = jax.random.normal(k_b, (3 * EMBED_DIM,), dtype=jnp.float32) * 0.02
        return {'x': x, 'Wqkv': Wqkv, 'bqkv': bqkv}
    _L1_attn_all = _L1_attn_setup()
    _L1_attn_in = {k: v for k, v in _L1_attn_all.items() if k in ('Wqkv', 'bqkv')}
    del _L1_attn_all

    def _L1_ffn_setup():
        import jax, jax.numpy as jnp
        import numpy as np
        BN_EPS = 0.001

        def _bn(h, g, b, m, v):
            return g * (h - m) * jax.lax.rsqrt(v + BN_EPS) + b
        key = jax.random.key(seed)
        ks = jax.random.split(key, 8)
        B, F, Df = (64, 64, 64)
        E, H, D = (8, 64, 64)
        s1 = 1.0 / np.sqrt(Df)
        s2 = 1.0 / np.sqrt(H)
        return {'x': jax.random.normal(ks[0], (B, F, Df), jnp.float32), 'Wr': jax.random.normal(ks[1], (Df, E), jnp.float32) * s1, 'br': jnp.zeros((E,), jnp.float32), 'W1': jax.random.normal(ks[2], (E, Df, H), jnp.float32) * s1, 'b1': jnp.zeros((E, H), jnp.float32), 'g1': jnp.ones((E, H), jnp.float32), 'be1': jnp.zeros((E, H), jnp.float32), 'm1': jnp.zeros((E, H), jnp.float32), 'v1': jnp.ones((E, H), jnp.float32), 'W2': jax.random.normal(ks[3], (E, H, H), jnp.float32) * s2, 'b2': jnp.zeros((E, H), jnp.float32), 'g2': jnp.ones((E, H), jnp.float32), 'be2': jnp.zeros((E, H), jnp.float32), 'm2': jnp.zeros((E, H), jnp.float32), 'v2': jnp.ones((E, H), jnp.float32), 'Wo': jax.random.normal(ks[4], (E, H, D), jnp.float32) * s2, 'bo': jnp.zeros((E, D), jnp.float32)}
    _L1_ffn_all = _L1_ffn_setup()
    _L1_ffn_in = {k: v for k, v in _L1_ffn_all.items() if k in ('Wr', 'br', 'W1', 'b1', 'g1', 'be1', 'm1', 'v1', 'W2', 'b2', 'g2', 'be2', 'm2', 'v2', 'Wo', 'bo')}
    del _L1_ffn_all
    return {'x': x, 'L0_tok_freq_bands': _L0_tok_in['freq_bands'], 'L0_tok_w1': _L0_tok_in['w1'], 'L0_tok_b1': _L0_tok_in['b1'], 'L0_tok_gamma': _L0_tok_in['gamma'], 'L0_tok_beta': _L0_tok_in['beta'], 'L0_tok_w2': _L0_tok_in['w2'], 'L0_tok_b2': _L0_tok_in['b2'], 'L0_attn_w_qkv': _L0_attn_in['w_qkv'], 'L0_attn_b_qkv': _L0_attn_in['b_qkv'], 'L0_attn_w_proj': _L0_attn_in['w_proj'], 'L0_attn_b_proj': _L0_attn_in['b_proj'], 'L0_ffn_router_w': _L0_ffn_in['router_w'], 'L0_ffn_w1': _L0_ffn_in['w1'], 'L0_ffn_b1': _L0_ffn_in['b1'], 'L0_ffn_w2': _L0_ffn_in['w2'], 'L0_ffn_b2': _L0_ffn_in['b2'], 'L1_attn_Wqkv': _L1_attn_in['Wqkv'], 'L1_attn_bqkv': _L1_attn_in['bqkv'], 'L1_ffn_Wr': _L1_ffn_in['Wr'], 'L1_ffn_br': _L1_ffn_in['br'], 'L1_ffn_W1': _L1_ffn_in['W1'], 'L1_ffn_b1': _L1_ffn_in['b1'], 'L1_ffn_g1': _L1_ffn_in['g1'], 'L1_ffn_be1': _L1_ffn_in['be1'], 'L1_ffn_m1': _L1_ffn_in['m1'], 'L1_ffn_v1': _L1_ffn_in['v1'], 'L1_ffn_W2': _L1_ffn_in['W2'], 'L1_ffn_b2': _L1_ffn_in['b2'], 'L1_ffn_g2': _L1_ffn_in['g2'], 'L1_ffn_be2': _L1_ffn_in['be2'], 'L1_ffn_m2': _L1_ffn_in['m2'], 'L1_ffn_v2': _L1_ffn_in['v2'], 'L1_ffn_Wo': _L1_ffn_in['Wo'], 'L1_ffn_bo': _L1_ffn_in['bo']}

def reference(x, L0_tok_freq_bands, L0_tok_w1, L0_tok_b1, L0_tok_gamma, L0_tok_beta, L0_tok_w2, L0_tok_b2, L0_attn_w_qkv, L0_attn_b_qkv, L0_attn_w_proj, L0_attn_b_proj, L0_ffn_router_w, L0_ffn_w1, L0_ffn_b1, L0_ffn_w2, L0_ffn_b2, L1_attn_Wqkv, L1_attn_bqkv, L1_ffn_Wr, L1_ffn_br, L1_ffn_W1, L1_ffn_b1, L1_ffn_g1, L1_ffn_be1, L1_ffn_m1, L1_ffn_v1, L1_ffn_W2, L1_ffn_b2, L1_ffn_g2, L1_ffn_be2, L1_ffn_m2, L1_ffn_v2, L1_ffn_Wo, L1_ffn_bo):
    import jax
    import jax.numpy as jnp

    def _L0_tok_ref(byte_ids, freq_bands, w1, b1, gamma, beta, w2, b2):
        import jax, jax.numpy as jnp
        import numpy as np
        B, T, D = (32, 1024, 64)
        LN_EPS = 1e-05
        Bsz, Tlen = byte_ids.shape
        Dm = w1.shape[0]
        k = min(Dm // 2, Tlen // 2)
        signal = byte_ids.astype(jnp.float32) / 127.5 - 1.0
        X = jnp.fft.fft(signal, axis=1)[:, :k]
        mag = jnp.abs(X) * freq_bands[:k]
        phase0 = jnp.angle(X)
        pos = jnp.arange(Tlen, dtype=jnp.float32)
        f = jnp.arange(k, dtype=jnp.float32)
        shift = 2.0 * np.pi / Tlen * pos[:, None] * f[None, :]
        phase = phase0[:, None, :] + shift[None, :, :]
        mag_bt = jnp.broadcast_to(mag[:, None, :], (Bsz, Tlen, k))
        feats = jnp.concatenate([mag_bt, jnp.sin(phase), jnp.cos(phase)], axis=-1)
        if feats.shape[-1] < Dm:
            feats = jnp.pad(feats, ((0, 0), (0, 0), (0, Dm - feats.shape[-1])))
        else:
            feats = feats[..., :Dm]
        h = feats @ w1 + b1
        mu = jnp.mean(h, axis=-1, keepdims=True)
        var = jnp.var(h, axis=-1, keepdims=True)
        h = (h - mu) * jax.lax.rsqrt(var + LN_EPS) * gamma + beta
        h = jax.nn.gelu(h, approximate=False)
        return h @ w2 + b2

    def _L0_attn_ref(x, w_qkv, b_qkv, w_proj, b_proj):
        import jax, jax.numpy as jnp
        import numpy as np
        B, L, E = (2, 2048, 64)
        H, K, DIL = (8, 31, 2)
        DH = E // H

        def neighbor_indices(length, k, d):
            i = jnp.arange(length)
            g = i % d
            p = i // d
            lg = (length - g + d - 1) // d
            start = jnp.clip(p - k // 2, 0, lg - k)
            t = jnp.arange(k)
            return g[:, None] + (start[:, None] + t[None, :]) * d
        b, l, e = x.shape
        qkv = (x @ w_qkv + b_qkv).reshape(b, l, 3, H, DH)
        q, k, v = (qkv[:, :, 0], qkv[:, :, 1], qkv[:, :, 2])
        nbr = neighbor_indices(l, K, DIL)
        kg = k[:, nbr]
        vg = v[:, nbr]
        scale = DH ** (-0.5)
        attn = jnp.einsum('blhd,blkhd->blhk', q, kg) * scale
        attn = jax.nn.softmax(attn, axis=-1)
        out = jnp.einsum('blhk,blkhd->blhd', attn, vg).reshape(b, l, e)
        return out @ w_proj + b_proj

    def _L0_ffn_ref(input_embeddings, router_w, w1, b1, w2, b2):
        import jax, jax.numpy as jnp
        import numpy as np
        NUM_EXPERTS = 8
        TOP_K = 2
        B, S, D = (8, 2048, 64)

        def _moe(tokens, router_w, w1, b1, w2, b2):
            N = tokens.shape[0]
            E = router_w.shape[0]
            logits = tokens.astype(jnp.float32) @ router_w.astype(jnp.float32).T
            probs = jax.nn.softmax(logits, axis=-1)
            rw, re = jax.lax.top_k(probs, TOP_K)
            if TOP_K > 1:
                rw = rw / jnp.maximum(rw.sum(-1, keepdims=True), 1e-12)
            rw = rw.astype(tokens.dtype)
            combine = jnp.zeros((N, E), tokens.dtype).at[jnp.arange(N)[:, None], re].set(rw)
            out = tokens
            for e in range(E):
                h = jax.nn.gelu(tokens @ w1[e] + b1[e], approximate=False)
                y = h @ w2[e] + b2[e]
                out = out + combine[:, e:e + 1] * y
            return out
        b, s, d = input_embeddings.shape
        tokens = input_embeddings.reshape(b * s, d)
        return _moe(tokens, router_w, w1, b1, w2, b2).reshape(b, s, d)

    def _L1_attn_ref(x, Wqkv, bqkv):
        import jax, jax.numpy as jnp
        import numpy as np
        EMBED_DIM = 64
        SEQ_LEN = 1024
        BATCH = 8
        ALPHA = 0.99
        bs, sl, d = x.shape
        qkv = x @ Wqkv + bqkv
        q, k, v = jnp.split(qkv, 3, axis=-1)
        i = jnp.arange(sl, dtype=jnp.float32)
        M = jnp.where(i[:, None] >= i[None, :], jnp.power(jnp.float32(ALPHA), i[:, None] - i[None, :]), 0.0)
        scores = jnp.einsum('bqd,bkd->bqk', q, k) / jnp.sqrt(jnp.float32(d))
        out = jnp.einsum('bqk,bkd->bqd', scores * M, v)
        return out

    def _L1_ffn_ref(x, Wr, br, W1, b1, g1, be1, m1, v1, W2, b2, g2, be2, m2, v2, Wo, bo):
        import jax, jax.numpy as jnp
        import numpy as np
        BN_EPS = 0.001

        def _bn(h, g, b, m, v):
            return g * (h - m) * jax.lax.rsqrt(v + BN_EPS) + b
        feat = jnp.mean(x, axis=0)
        w = jax.nn.softmax(feat @ Wr + br, axis=-1)
        h = jnp.einsum('bfd,edh->bfeh', x, W1) + b1
        h = jax.nn.relu(_bn(h, g1, be1, m1, v1))
        h = jnp.einsum('bfeh,ehk->bfek', h, W2) + b2
        h = jax.nn.relu(_bn(h, g2, be2, m2, v2))
        y = jnp.einsum('bfeh,ehd->bfed', h, Wo) + bo
        return jnp.einsum('bfed,fe->bfd', y, w)
    h = _L0_tok_ref(x, L0_tok_freq_bands, L0_tok_w1, L0_tok_b1, L0_tok_gamma, L0_tok_beta, L0_tok_w2, L0_tok_b2)
    h = h + _L0_attn_ref(_layernorm(h, axis=-1), L0_attn_w_qkv, L0_attn_b_qkv, L0_attn_w_proj, L0_attn_b_proj)
    h = h + _L0_ffn_ref(_layernorm(h, axis=-1), L0_ffn_router_w, L0_ffn_w1, L0_ffn_b1, L0_ffn_w2, L0_ffn_b2)
    h = h + _L1_attn_ref(_layernorm(h, axis=-1), L1_attn_Wqkv, L1_attn_bqkv)
    h = h + _L1_ffn_ref(_layernorm(h, axis=-1), L1_ffn_Wr, L1_ffn_br, L1_ffn_W1, L1_ffn_b1, L1_ffn_g1, L1_ffn_be1, L1_ffn_m1, L1_ffn_v1, L1_ffn_W2, L1_ffn_b2, L1_ffn_g2, L1_ffn_be2, L1_ffn_m2, L1_ffn_v2, L1_ffn_Wo, L1_ffn_bo)
    return h

_drawn_inputs = setup_inputs


def setup_inputs(seed=0):
    import zlib

    import numpy as np

    out = dict(_drawn_inputs(seed))
    spreads = {'L0_tok_freq_bands': (1.0, 0.6),
     'L0_tok_b1': (0.0, 2.0),
     'L0_tok_gamma': (1.0, 0.2),
     'L0_tok_beta': (0.0, 0.1),
     'L0_tok_b2': (0.0, 0.1),
     'L0_attn_b_qkv': (0.0, 0.1),
     'L0_attn_b_proj': (0.0, 0.1),
     'L0_ffn_b1': (0.0, 0.1),
     'L0_ffn_b2': (0.0, 0.1),
     'L1_ffn_br': (0.0, 0.8),
     'L1_ffn_b1': (0.0, 0.8),
     'L1_ffn_g1': (1.0, 0.6),
     'L1_ffn_be1': (0.0, 0.8),
     'L1_ffn_m1': (0.0, 0.8),
     'L1_ffn_v1': (1.0, 0.6),
     'L1_ffn_b2': (0.0, 2.0),
     'L1_ffn_g2': (1.0, 0.6),
     'L1_ffn_be2': (0.0, 2.0),
     'L1_ffn_m2': (0.0, 2.0),
     'L1_ffn_v2': (1.0, 0.6),
     'L1_ffn_bo': (0.0, 2.0)}
    factors = {'L1_ffn_Wr': 8.0, 'L1_ffn_W1': 8.0, 'L1_ffn_W2': 8.0, 'L1_ffn_Wo': 8.0}
    for name, (base, spread) in spreads.items():
        noise = np.random.default_rng([zlib.crc32(name.encode()), seed]).standard_normal(out[name].shape)
        drawn = base * np.exp(spread * noise) if base else spread * noise
        out[name] = jnp.asarray(drawn.astype(out[name].dtype))
    for name, factor in factors.items():
        out[name] = (out[name] * factor).astype(out[name].dtype)
    return out
```

```python
from contextlib import ExitStack

import numpy as np
import concourse.bass as bass
from concourse import mybir

F32 = mybir.dt.float32
F32R = mybir.dt.float32r
BF16 = mybir.dt.bfloat16
I32 = mybir.dt.int32
ALU = mybir.AluOpType
ACT = mybir.ActivationFunctionType
AX = mybir.AxisListType.X

NB, T, D = 32, 512, 64
NP = NB // 2
HID = 2 * D
NF = D // 2
NE = 8
EP = NE // 2
NH, DH = 8, 8
KW, DIL = 31, 2
TG = T // DIL
QT = 32
NT = TG // QT
WIN = 64
LN_EPS = 1e-5
BN_EPS = 1e-3
NEG = -1.0e30
ALPHA = 0.99


def window_start(t):
    return min(max(t * QT - KW // 2, 0), TG - WIN)


CONST_PARTS = [("ident", 128), ("center", 128), ("mean64", 128), ("mean128", 128), ("dft", 4 * 2 * NF), ("shift", T),
               ("decay", T), ("winmask", 2 * WIN), ("headmask", NH), ("vmask", 18), ("rank", NE),
               ("pick", 2 * EP * 128)]
CONST_AT = {}
_at = 0
for _name, _n in CONST_PARTS:
    CONST_AT[_name] = (_at, _n)
    _at += _n
CONST_COLS = _at


def constants():
    c = {}
    c["ident"] = np.eye(128)
    block = np.kron(np.eye(2), np.full((D, D), 1.0 / D))
    c["center"] = np.eye(128) - block
    c["mean64"] = block
    c["mean128"] = np.full((128, 128), 1.0 / HID)
    t = np.arange(T)[:, None] * np.arange(NF)[None, :] % T * (2 * np.pi / T)
    dft = np.concatenate([np.cos(t), -np.sin(t)], 1)
    c["dft"] = dft.reshape(4, 128, 2 * NF).transpose(1, 0, 2).reshape(128, -1)
    step = np.float32(2.0 * np.pi / T)
    shift = (step * np.arange(T, dtype=np.float32)[None, :]) * np.arange(NF, dtype=np.float32)[:, None]
    shift = shift.astype(np.float64)
    c["shift"] = np.concatenate([np.cos(shift), np.sin(shift)] * 2, 0)
    k, q = np.arange(128)[:, None], np.arange(T)[None, :]
    c["decay"] = np.where(q >= k, np.power(float(np.float32(ALPHA)), np.maximum(q - k, 0)), 0.0) / np.sqrt(D)
    mask = np.full((2, 128, WIN), NEG)
    for half in range(2):
        for r in range(128):
            p = half * 128 + r
            first = min(max(p - KW // 2, 0), TG - KW) - window_start(p // QT)
            mask[half, r, first:first + KW] = 0.0
    c["winmask"] = mask.transpose(1, 0, 2).reshape(128, -1)
    c["headmask"] = np.kron(np.ones((2, 1)), np.kron(np.eye(NH), np.ones((DH, 1))))
    v = np.zeros((128, 18))
    v[:WIN, 0:8] = v[WIN:2 * WIN, 8:16] = 1.0
    v[:WIN, 16] = v[WIN:2 * WIN, 17] = 1.0
    c["vmask"] = v
    c["rank"] = np.broadcast_to(np.arange(NE, 0, -1), (128, NE))
    pick = np.zeros((128, 2, EP, 128))
    for b in range(2):
        for part in range(2):
            for e in range(NE):
                pick[(b * 2 + part) * NE + e, b, e // 2, (e % 2) * 64:(e % 2) * 64 + 64] = 1.0
    c["pick"] = pick.reshape(128, -1)
    return np.ascontiguousarray(np.concatenate([c[n] for n, _ in CONST_PARTS], 1).astype(np.float32))


class Buffers:
    pass


def allocate(nc, ctx):
    s = Buffers()

    def sb(name, shape, dt=F32):
        return ctx.enter_context(nc.sbuf_tensor(name, shape, dt))

    s.const = sb("const", [128, CONST_COLS])
    s.h = sb("h", [128, NP, T])
    s.z = sb("z", [128, NB, T])
    s.pick = sb("pick_r", [128, 2, EP, 128], F32R)
    s.winmask = sb("winmask_b", [128, 2, NH, WIN], BF16)
    s.ident_b = sb("ident_b", [128, 128], BF16)
    s.shift = sb("shift_r", [128, T], F32R)
    s.w1s = sb("tok_w1s", [128, HID])
    s.phase = sb("tok_phase", [128, NB])
    s.tok_bias = sb("tok_bias", [128, NB])
    s.tok_w2 = sb("tok_w2", [128, D])
    s.a0_w = sb("a0_w", [128, 3, 128])
    s.a0_wp = sb("a0_wp", [128, 128])
    s.moe_wr = sb("moe_wr", [128, 128])
    s.moe_w1h = sb("moe_w1h", [128, EP, 128], F32R)
    s.moe_w1l = sb("moe_w1l", [128, EP, 128], F32R)
    s.moe_w2 = sb("moe_w2", [128, EP, D])
    s.moe_b2h = sb("moe_b2h", [128, 128], F32R)
    s.moe_b2l = sb("moe_b2l", [128, 128], F32R)
    s.combine = sb("combine", [128, NP, 4, 2 * 2 * NE], F32R)
    s.a1_qkh = sb("a1_qkh", [128, 2, 128], F32R)
    s.a1_qkl = sb("a1_qkl", [128, 2, 128], F32R)
    s.a1_wv = sb("a1_wv", [128, 128])
    s.a1_bv = sb("a1_bv", [128, 2, D])
    s.f1_wr = sb("f1_wr", [128, 128])
    s.f1_br = sb("f1_br", [128, NE])
    s.f1_w1h = sb("f1_w1h", [128, EP, 128], F32R)
    s.f1_w1l = sb("f1_w1l", [128, EP, 128], F32R)
    s.f1_w2 = sb("f1_w2", [128, EP, 128])
    s.f1_wo = sb("f1_wo", [128, EP, D])
    s.f1_wdup = sb("f1_wdup", [128, EP, 2, D])
    s.f1_w = s.z[:, NP:NP + EP, :]
    s.f1_r = s.z[:, NP + EP, :]
    s.feat = sb("feat", [128, T])
    s.eps = sb("eps", [128, 1])
    s.one = sb("one", [128, 1])
    s.cols = sb("cols", [128, 64])
    return s


COLS = {n: i for i, n in enumerate([
    "gamma", "beta", "tok_b2", "a0_bq", "a0_bk", "a0_bv", "a0_bp", "a1_bq", "a1_bk", "freq"])}
for _k, _n in enumerate(["moe_b1", "f1_b1", "f1_g1", "f1_be1", "f1_m1", "f1_v1", "f1_b2", "f1_g2", "f1_be2", "f1_m2", "f1_v2"]):
    COLS[_n] = 12 + EP * _k


def const(s, name, rows=128):
    at, n = CONST_AT[name]
    return s.const[0:rows, at:at + n]


def col(s, name, k=0):
    return s.cols[:, COLS[name] + k:COLS[name] + k + 1]


def cols4(s, name):
    return s.cols[:, COLS[name]:COLS[name] + EP]


def column(ap):
    return ap.rearrange("(p a) -> p a", a=1)


def prepare(nc, s, a):
    with ExitStack() as ctx:
        def sb(name, shape, dt=F32):
            return ctx.enter_context(nc.sbuf_tensor(name, shape, dt))

        def sem(name):
            return ctx.enter_context(nc.semaphore(name))

        x_in = sb("x_in", [NB, T], I32)
        signal = sb("signal", [NB, T])
        signal_t = sb("signal_t", [128, 4, NB])
        spec = sb("spec", [NB, 2, NF])
        spec_sq = sb("spec_sq", [NB, 2, NF])
        power = sb("power", [NB, NF])
        is_zero = sb("is_zero", [NB, NF])
        mag = sb("mag", [NB, NF])
        inv = sb("inv", [NB, NF])
        sincos = sb("sincos", [NB, 4, NF])
        mag_t = sb("mag_t", [NF + 1, NB])
        w1m = sb("w1m", [NF + 1, HID])
        rowsum = sb("rowsum", [128, 2])
        moe_w1 = sb("moe_w1", [128, NE, D])
        f1_w1 = sb("f1_w1", [128, NE, D])
        moe_b2 = sb("moe_b2", [128, 128])
        a1_qk = sb("a1_qk", [128, 2, 2, D])
        g2row = sb("g2row", [128, NE * D])
        v2row = sb("v2row", [128, NE * D])
        bo = sb("bo", [128, EP, D])
        bn = sb("bn", [128, 4, EP])
        ps = [ctx.enter_context(nc.psum_tensor(f"prep_ps{n}", [128, 512], F32)) for n in range(6)]

        zeroed, x_loaded, const_loaded, loaded = sem("zeroed"), sem("x_loaded"), sem("const_loaded"), sem("loaded")
        turned, dve, act, pe = sem("turned"), sem("prep_dve"), sem("prep_act"), sem("prep_pe")
        block = ctx.enter_context(nc.Block())
        wq = a["L0_attn_w_qkv"].rearrange("d (n e) -> d n e", n=3)
        w1 = a["L0_tok_w1"]
        up = slice(64, 128)
        lo = slice(0, 64)
        half = [lo, up]
        loads = [(s.w1s[32 * n:32 * n + 32, :], w1[NF:D, :]) for n in range(4)]
        loads += [(w1m[0:NF, :], w1[0:NF, :]), (w1m[NF:NF + 1, :], a["L0_tok_b1"].rearrange("(p n) -> p n", p=1)),
                  (s.cols[0:NF, COLS["freq"]:COLS["freq"] + 1], column(a["L0_tok_freq_bands"])),
                  (col(s, "gamma"), column(a["L0_tok_gamma"])), (col(s, "beta"), column(a["L0_tok_beta"])),
                  (s.tok_w2[:], a["L0_tok_w2"])]
        for hf in half:
            def put(name, ap):
                loads.append((s.cols[hf, COLS[name]:COLS[name] + 1], column(ap)))
            put("tok_b2", a["L0_tok_b2"])
            put("a0_bq", a["L0_attn_b_qkv"][0:D])
            put("a0_bk", a["L0_attn_b_qkv"][D:2 * D])
            put("a0_bv", a["L0_attn_b_qkv"][2 * D:3 * D])
            put("a0_bp", a["L0_attn_b_proj"])
            put("a1_bq", a["L1_attn_bqkv"][0:D])
            put("a1_bk", a["L1_attn_bqkv"][D:2 * D])
            n = hf.start
            loads.append((s.a0_w[hf, :, n:n + 64], wq))
            loads.append((s.a0_wp[hf, n:n + 64], a["L0_attn_w_proj"]))
            loads.append((s.moe_wr[hf, n // 8:n // 8 + NE], a["L0_ffn_router_w"].rearrange("e d -> d e")))
            loads.append((moe_w1[hf, :, :], a["L0_ffn_w1"].rearrange("e d h -> d e h")))
            loads.append((f1_w1[hf, :, :], a["L1_ffn_W1"].rearrange("e d h -> d e h")))
            loads.append((s.a1_wv[hf, n:n + 64], a["L1_attn_Wqkv"][:, 2 * D:3 * D]))
            loads.append((s.f1_wr[hf, 0:NE], a["L1_ffn_Wr"]))
            for c in range(2):
                loads.append((a1_qk[hf, :, c, :], a["L1_attn_Wqkv"][:, 0:2 * D].rearrange("d (n e) -> d n e", n=2)))
            e2 = n // 64
            for name, key in [("moe_b1", "L0_ffn_b1"), ("f1_b1", "L1_ffn_b1"), ("f1_g1", "L1_ffn_g1"), ("f1_be1", "L1_ffn_be1"),
                              ("f1_m1", "L1_ffn_m1"), ("f1_v1", "L1_ffn_v1"), ("f1_b2", "L1_ffn_b2"), ("f1_g2", "L1_ffn_g2"),
                              ("f1_be2", "L1_ffn_be2"), ("f1_m2", "L1_ffn_m2"), ("f1_v2", "L1_ffn_v2")]:
                loads.append((s.cols[hf, COLS[name]:COLS[name] + EP], a[key].rearrange("(p two) h -> two h p", two=2)[e2]))
            loads.append((s.moe_w2[hf, :, :], a["L0_ffn_w2"].rearrange("(p two) h d -> two h p d", two=2)[e2]))
            loads.append((s.f1_w2[hf, :, n:n + 64], a["L1_ffn_W2"].rearrange("(p two) h d -> two h p d", two=2)[e2]))
            loads.append((s.f1_wo[hf, :, :], a["L1_ffn_Wo"].rearrange("(p two) h d -> two h p d", two=2)[e2]))
            loads.append((bo[n:n + 1, :, :], a["L1_ffn_bo"].rearrange("(p two) d -> two p d", two=2)[e2:e2 + 1]))
            for part in range(2):
                r = (e2 * 2 + part) * NE
                loads.append((moe_b2[r:r + NE, n:n + 64], a["L0_ffn_b2"]))
        for b in range(2):
            loads.append((s.a1_bv[:, b, :], a["L1_attn_bqkv"][2 * D:3 * D].partition_broadcast(128)))
        loads += [(s.f1_br[:], a["L1_ffn_br"].partition_broadcast(128)),
                  (g2row[:], a["L1_ffn_g2"].rearrange("e h -> (e h)").partition_broadcast(128)),
                  (v2row[:], a["L1_ffn_v2"].rearrange("e h -> (e h)").partition_broadcast(128))]
        cleared = [s.a0_w, s.a0_wp, s.moe_wr, s.a1_wv, s.f1_wr, s.f1_w2, moe_b2, bo, s.cols]

        @block.gpsimd
        def _(pool):
            for t in cleared:
                nc.gpsimd.memset(t[:], 0.0).then_inc(zeroed, 1)

        @block.sync
        def _(sp):
            sp.dma_start(x_in[:], a["x"]).then_inc(x_loaded, 16)
            sp.dma_start(s.const[:], a["const"]).then_inc(const_loaded, 16)
            sp.wait_ge(zeroed, len(cleared))
            for dst, src in loads[0::2]:
                sp.dma_start(dst, src, allow_slow_non_contiguous=True).then_inc(loaded, 16)

        @block.scalar
        def _(sc):
            sc.wait_ge(zeroed, len(cleared))
            for dst, src in loads[1::2]:
                sc.dma_start(dst, src, allow_slow_non_contiguous=True).then_inc(loaded, 16)
            sc.wait_ge(dve, 8)
            nc.scalar.activation(mag[:], power[:], ACT.Sqrt).then_inc(act, 1)
            sc.wait_ge(dve, BN_READY)
            nc.scalar.activation(bn[:, 0:2, :], bn[:, 0:2, :], ACT.Sqrt).then_inc(act, 1)
            nc.scalar.activation(v2row[:], v2row[:], ACT.Sqrt).then_inc(act, 1)

        @block.tensor
        def _(te):
            te.wait_ge(const_loaded, 16)
            te.wait_ge(dve, 1)
            for c in range(4):
                nc.tensor.transpose(ps[0][:, c * NB:(c + 1) * NB], signal[:, c * 128:(c + 1) * 128],
                                    const(s, "ident", NB)[:, 0:NB]).then_inc(pe, 1)
            te.wait_ge(dve, 2)
            dft = const(s, "dft").rearrange("p (c n) -> p c n", c=4)
            for c in range(4):
                nc.tensor.matmul(ps[1][0:NB, 0:2 * NF], signal_t[:, c, :], dft[:, c, :],
                                 start=(c == 0), stop=(c == 3)).then_inc(pe, 1)
            te.wait_ge(dve, 13)
            nc.tensor.transpose(ps[2][:, 0:NB], sincos[:].rearrange("p a b -> p (a b)"),
                                const(s, "ident", NB)[:, 0:NB]).then_inc(pe, 1)
            nc.tensor.transpose(ps[3][0:NF, 0:NB], mag[:], const(s, "ident", NB)[:, 0:NB]).then_inc(pe, 1)
            te.wait_ge(dve, 21)
            nc.tensor.matmul(ps[4][:, 0:NB], w1m[:], mag_t[:], start=True, stop=True).then_inc(pe, 1)
            te.wait_ge(loaded, 16 * len(loads))
            nc.tensor.matmul(ps[5][:, 0:1], s.a0_wp[:], col(s, "a0_bv"), start=True, stop=True).then_inc(pe, 1)

        @block.vector
        def _(ve):
            n = [0]

            def step(ins):
                ins.then_inc(dve, 1)
                n[0] += 1
                ve.wait_ge(dve, n[0])

            v = nc.vector
            ve.wait_ge(x_loaded, 16)
            step(v.tensor_scalar(signal[:], x_in[:], 1.0 / 127.5, -1.0, ALU.mult, ALU.add))
            ve.wait_ge(pe, 4)
            step(v.tensor_copy(signal_t[:].rearrange("p c b -> p (c b)"), ps[0][:, 0:4 * NB]))
            ve.wait_ge(pe, 8)
            step(v.tensor_copy(spec[:].rearrange("p a b -> p (a b)"), ps[1][0:NB, 0:2 * NF]))
            re, im = spec[:, 0, :], spec[:, 1, :]
            step(v.tensor_tensor(spec_sq[:], spec[:], spec[:], ALU.mult))
            step(v.tensor_tensor(power[:], spec_sq[:, 0, :], spec_sq[:, 1, :], ALU.add))
            step(v.tensor_scalar(is_zero[:], power[:], 0.0, None, ALU.is_equal))
            step(v.tensor_tensor(re, re, is_zero[:], ALU.add))
            step(v.tensor_tensor(power[:], power[:], is_zero[:], ALU.add))
            assert n[0] == 8
            ve.wait_ge(act, 1)
            step(v.reciprocal(inv[:], mag[:]))
            step(v.tensor_tensor(sincos[:, 0::2, :], im.unsqueeze(1).broadcast_to([NB, 2, NF]),
                                 inv[:].unsqueeze(1).broadcast_to([NB, 2, NF]), ALU.mult))
            step(v.tensor_tensor(sincos[:, 1::2, :], re.unsqueeze(1).broadcast_to([NB, 2, NF]),
                                 inv[:].unsqueeze(1).broadcast_to([NB, 2, NF]), ALU.mult))
            step(v.tensor_tensor(mag[:], mag[:], is_zero[:], ALU.subtract))
            ve.wait_ge(loaded, 16 * len(loads))
            step(v.memset(mag_t[:], 1.0))
            assert n[0] == 13
            ve.wait_ge(pe, 9)
            step(v.tensor_copy(s.phase[:], ps[2][:, 0:NB]))
            ve.wait_ge(pe, 10)
            step(v.tensor_scalar(mag_t[0:NF, :], ps[3][0:NF, 0:NB], s.cols[0:NF, COLS["freq"]:COLS["freq"] + 1], None, ALU.mult))
            step(v.tensor_reduce(rowsum[:, 0:1], s.w1s[:], AX, ALU.add))
            step(v.tensor_reduce(rowsum[0:NF + 1, 1:2], w1m[:], AX, ALU.add))
            step(v.tensor_scalar(rowsum[:, 0:1], rowsum[:, 0:1], 1.0 / HID, None, ALU.mult))
            step(v.tensor_scalar(rowsum[0:NF + 1, 1:2], rowsum[0:NF + 1, 1:2], 1.0 / HID, None, ALU.mult))
            step(v.tensor_scalar(s.w1s[:], s.w1s[:], rowsum[:, 0:1], None, ALU.subtract))
            step(v.tensor_scalar(w1m[:], w1m[:], rowsum[0:NF + 1, 1:2], None, ALU.subtract))
            assert n[0] == 21
            ve.wait_ge(pe, 11)
            step(v.tensor_copy(s.tok_bias[:], ps[4][:, 0:NB]))
            step(v.tensor_copy(s.shift[:], const(s, "shift")))
            step(v.tensor_tensor(s.shift[up, :], const(s, "shift")[up, :], s.shift[up, :].bitcast(F32), ALU.subtract))
            step(v.tensor_copy(s.pick[:].rearrange("p a b c -> p (a b c)"), const(s, "pick")))
            wm = const(s, "winmask").rearrange("p (a w) -> p a w", a=2)
            for hf in range(2):
                step(v.tensor_copy(s.winmask[:, hf, :, :], wm[:, hf, :].unsqueeze(1).broadcast_to([128, NH, WIN])))
            step(v.tensor_copy(s.ident_b[:], const(s, "ident")))
            ve.wait_ge(pe, 12)
            step(v.tensor_tensor(col(s, "a0_bp"), ps[5][:, 0:1], col(s, "a0_bp"), ALU.add))

            def split(high, low, whole):
                step(v.tensor_copy(high, whole))
                step(v.tensor_tensor(low, whole, high.bitcast(F32), ALU.subtract))

            def flat(t):
                return t[:].rearrange("p a b -> p (a b)")

            split(flat(s.moe_w1h), flat(s.moe_w1l), moe_w1[:].rearrange("p a b -> p (a b)"))
            split(flat(s.f1_w1h), flat(s.f1_w1l), f1_w1[:].rearrange("p a b -> p (a b)"))
            split(s.moe_b2h[:], s.moe_b2l[:], moe_b2[:])
            split(flat(s.a1_qkh), flat(s.a1_qkl), a1_qk[:].rearrange("p a b c -> p (a b c)"))
            step(v.tensor_scalar(bn[:, 0, :], cols4(s, "f1_v1"), BN_EPS, None, ALU.add))
            step(v.tensor_scalar(bn[:, 1, :], cols4(s, "f1_v2"), BN_EPS, None, ALU.add))
            step(v.tensor_scalar(v2row[:], v2row[:], BN_EPS, None, ALU.add))
            step(v.reciprocal(bn[:, 0:2, :], bn[:, 0:2, :]))
            step(v.reciprocal(v2row[:], v2row[:]))
            assert n[0] == BN_READY, n
            ve.wait_ge(act, 3)
            for k in range(2):
                m = f"{k + 1}"
                step(v.tensor_tensor(cols4(s, "f1_g" + m), cols4(s, "f1_g" + m), bn[:, k, :], ALU.mult))
                step(v.tensor_tensor(bn[:, 2 + k, :], cols4(s, "f1_b" + m), cols4(s, "f1_m" + m), ALU.subtract))
                step(v.tensor_tensor(bn[:, 2 + k, :], bn[:, 2 + k, :], cols4(s, "f1_g" + m), ALU.mult))
                step(v.tensor_tensor(cols4(s, "f1_be" + m), cols4(s, "f1_be" + m), bn[:, 2 + k, :], ALU.add))
            step(v.tensor_tensor(g2row[:], g2row[:], v2row[:], ALU.mult))
            step(v.tensor_tensor(s.f1_w2[:].rearrange("p a b -> p (a b)"), s.f1_w2[:].rearrange("p a b -> p (a b)"), g2row[:], ALU.mult))
            for ep in range(EP):
                for c in range(2):
                    step(v.scalar_tensor_tensor(out=s.f1_wdup[:, ep, c, :], in0=s.f1_wo[:, ep, :], scalar=s.cols[:, COLS["f1_be2"] + ep:COLS["f1_be2"] + ep + 1],
                                                in1=bo[:, ep, :], op0=ALU.mult, op1=ALU.add))
            step(v.tensor_scalar(cols4(s, "f1_be2"), cols4(s, "f1_be2"), -1.0, None, ALU.mult))
            step(v.memset(s.feat[:], 0.0))
            step(v.memset(s.eps[:], LN_EPS))
            step(v.memset(s.one[:], 1.0))


BN_READY = 42


CREDITS = 16


def done(n):
    return n + (1 + CREDITS)


def give_credits(eng, *semaphores):
    for sem in semaphores:
        eng.sem_inc(sem, CREDITS)


def row(t, n):
    return t[:, bass.ds(n, 1), :].rearrange("p a b -> p (a b)")


class Step:

    def __init__(self, turn, offset, unroll):
        self.turn, self.offset, self.unroll = turn, offset, unroll
        self.n = turn * unroll + offset
        self.k = offset % unroll

    def of(self, size):
        return self.turn * (self.unroll // size) + self.offset // size


def staggered(eng, count, unroll, *stages):
    most = max(lead for lead, _ in stages)
    for n in range(-most, 0):
        for lead, stage in stages:
            if n + lead >= 0:
                stage(Step(0, n + lead, unroll))
    turns = count // unroll - 1
    with eng.Fori(0, turns) as turn:
        for k in range(unroll):
            for lead, stage in stages:
                stage(Step(turn, k + lead, unroll))
    for k in range(unroll):
        for lead, stage in stages:
            if k + lead < unroll:
                stage(Step(turns, k + lead, unroll))


def pool_copy(nc, s, out, in_):
    ones = s.one[:] if len(in_.shape) == 2 else s.one[:].unsqueeze(2)
    return nc.gpsimd.tensor_tensor(out, in_, ones.broadcast_to(in_.shape), ALU.mult)


def spectral_norm(nc, s):
    with ExitStack() as ctx:
        def sb(name, shape, dt=F32):
            return [ctx.enter_context(nc.sbuf_tensor(f"sn_{name}{k}", shape, dt)) for k in range(4)]

        def ps(name):
            return [ctx.enter_context(nc.psum_tensor(f"sn_{name}{k}", [128, T], F32)) for k in range(4)]

        def sem(name):
            return ctx.enter_context(nc.semaphore("sn_" + name))

        wh, wl = sb("wh", [128, HID], F32R), sb("wl", [128, HID], F32R)
        sq, ln, rstd = sb("sq", [128, T]), sb("ln", [128, T]), sb("rstd", [128, T])
        hid, var = ps("hid"), ps("var")
        s_wh, s_wl, s_hid, s_sq, s_var, s_ln, s_rstd, s_z = [sem(x) for x in ("wh", "wl", "hid", "sq", "var", "ln", "rstd", "z")]
        block = ctx.enter_context(nc.Block())

        @block.gpsimd
        def _(pool):
            give_credits(pool, s_wh)

            def weights(at):
                n, k = at.n, at.k
                phase = s.phase[:, bass.ds(n, 1)]
                pool.wait_ge(s_wl, done(n - 4))
                pool.wait_ge(s_hid, done(n - 4))
                nc.gpsimd.tensor_tensor(wh[k][:], s.w1s[:], phase.broadcast_to([128, HID]), ALU.mult).then_inc(s_wh, 1)

            staggered(nc.gpsimd, NB, 4, (0, weights))

        @block.tensor
        def _(te):
            give_credits(te, s_hid, s_var)

            def hidden(at):
                n, k = at.n, at.k
                te.wait_ge(s_wl, done(n))
                te.wait_ge(s_z, done(n - 4))
                nc.tensor.matmul(hid[k][:], wh[k][:], s.shift[:], start=True, stop=False)
                nc.tensor.matmul(hid[k][:], wl[k][:], s.shift[:], start=False, stop=True).then_inc(s_hid, 1)

            def variance(at):
                n, k = at.n, at.k
                te.wait_ge(s_sq, done(n))
                te.wait_ge(s_ln, done(n - 4))
                nc.tensor.matmul(var[k][:], const(s, "mean128"), sq[k][:], start=True, stop=True).then_inc(s_var, 1)

            staggered(nc.tensor, NB, 4, (1, variance), (3, hidden))

        @block.scalar
        def _(sc):
            sc.preload_act_table_set("natural_log_exp_and_others")
            give_credits(sc, s_sq, s_ln, s_rstd)

            def squares(at):
                n, k = at.n, at.k
                sc.wait_ge(s_hid, done(n))
                sc.wait_ge(s_var, done(n - 4))
                nc.scalar.activation(sq[k][:], hid[k][:], ACT.Square, bias=s.tok_bias[:, bass.ds(n, 1)]).then_inc(s_sq, 1)

            def logarithm(at):
                n, k = at.n, at.k
                sc.wait_ge(s_var, done(n))
                sc.wait_ge(s_rstd, done(n - 4))
                nc.scalar.activation(ln[k][:], var[k][:], ACT.Ln, bias=s.eps[:]).then_inc(s_ln, 1)

            def root(at):
                n, k = at.n, at.k
                sc.wait_ge(s_ln, done(n))
                sc.wait_ge(s_z, done(n - 4))
                nc.scalar.activation(rstd[k][:], ln[k][:], ACT.Exp, scale=-0.5).then_inc(s_rstd, 1)

            staggered(nc.scalar, NB, 4, (2, squares), (1, logarithm), (0, root))

        @block.vector
        def _(ve):
            give_credits(ve, s_z, s_wl)

            def low(at):
                n, k = at.n, at.k
                ve.wait_ge(s_wh, done(n))
                ve.wait_ge(s_hid, done(n - 4))
                nc.vector.scalar_tensor_tensor(out=wl[k][:], in0=s.w1s[:], scalar=s.phase[:, bass.ds(n, 1)], in1=wh[k][:].bitcast(F32),
                                               op0=ALU.mult, op1=ALU.subtract).then_inc(s_wl, 1)

            def normalise(at):
                n, k = at.n, at.k
                ve.wait_ge(s_rstd, done(n))
                nc.vector.scalar_tensor_tensor(out=row(s.z, n), in0=hid[k][:], scalar=s.tok_bias[:, bass.ds(n, 1)],
                                               in1=rstd[k][:], op0=ALU.add, op1=ALU.mult).then_inc(s_z, 1)

            staggered(nc.vector, NB, 4, (3, low), (0, normalise))


def tokenizer_output(nc, s):
    with ExitStack() as ctx:
        g = [ctx.enter_context(nc.sbuf_tensor(f"to_g{k}", [128, 2, T], F32)) for k in range(4)]
        y = [ctx.enter_context(nc.psum_tensor(f"to_y{k}", [128, T], F32)) for k in range(4)]
        s_g, s_y, s_h = [ctx.enter_context(nc.semaphore("to_" + x)) for x in ("g", "y", "h")]
        block = ctx.enter_context(nc.Block())

        @block.scalar
        def _(sc):
            give_credits(sc, s_g)

            def gelu(at):
                sc.wait_ge(s_y, done(at.n - 4))
                nc.scalar.activation(g[at.k][:], s.z[:, bass.ds(at.n * 2, 2), :], ACT.Gelu, scale=col(s, "gamma"),
                                     bias=col(s, "beta")).then_inc(s_g, 1)

            staggered(nc.scalar, NP, 4, (0, gelu))

        @block.tensor
        def _(te):
            give_credits(te, s_y)

            def product(at):
                te.wait_ge(s_g, done(at.n))
                te.wait_ge(s_h, done(at.n - 4))
                nc.tensor.matmul(y[at.k][0:64, :], s.tok_w2[:], g[at.k][:, 0, :], start=True, stop=True)
                nc.tensor.matmul(y[at.k][64:128, :], s.tok_w2[:], g[at.k][:, 1, :], start=True, stop=True).then_inc(s_y, 1)

            staggered(nc.tensor, NP, 4, (0, product))

        @block.vector
        def _(ve):
            give_credits(ve, s_h)

            def bias(at):
                ve.wait_ge(s_y, done(at.n))
                nc.vector.tensor_scalar(row(s.h, at.n), y[at.k][:], col(s, "tok_b2"), None, ALU.add).then_inc(s_h, 1)

            staggered(nc.vector, NP, 4, (0, bias))


def layer_norm(nc, s, tag, features=False):
    with ExitStack() as ctx:
        def sb(name):
            return [ctx.enter_context(nc.sbuf_tensor(f"{tag}_{name}{k}", [128, T], F32)) for k in range(4)]

        sq, ln, rstd = sb("sq"), sb("ln"), sb("rstd")
        cen, var = [[ctx.enter_context(nc.psum_tensor(f"{tag}_{x}{k}", [128, T], F32)) for k in range(4)] for x in ("cen", "var")]
        s_cen, s_sq, s_var, s_ln, s_rstd, s_z, s_feat = [ctx.enter_context(nc.semaphore(f"{tag}_s_{x}"))
                                                         for x in ("cen", "sq", "var", "ln", "rstd", "z", "feat")]
        block = ctx.enter_context(nc.Block())

        @block.tensor
        def _(te):
            give_credits(te, s_cen, s_var)

            def centre(at):
                te.wait_ge(s_z, done(at.n - 4))
                nc.tensor.matmul(cen[at.k][:], const(s, "center"), row(s.h, at.n), start=True, stop=True).then_inc(s_cen, 1)

            def variance(at):
                te.wait_ge(s_sq, done(at.n))
                te.wait_ge(s_ln, done(at.n - 4))
                nc.tensor.matmul(var[at.k][:], const(s, "mean64"), sq[at.k][:], start=True, stop=True).then_inc(s_var, 1)

            staggered(nc.tensor, NP, 4, (1, variance), (3, centre))

        @block.scalar
        def _(sc):
            sc.preload_act_table_set("natural_log_exp_and_others")
            give_credits(sc, s_sq, s_ln, s_rstd)

            def squares(at):
                sc.wait_ge(s_cen, done(at.n))
                sc.wait_ge(s_var, done(at.n - 4))
                nc.scalar.activation(sq[at.k][:], cen[at.k][:], ACT.Square).then_inc(s_sq, 1)

            def logarithm(at):
                sc.wait_ge(s_var, done(at.n))
                sc.wait_ge(s_rstd, done(at.n - 4))
                nc.scalar.activation(ln[at.k][:], var[at.k][:], ACT.Ln, bias=s.eps[:]).then_inc(s_ln, 1)

            def root(at):
                sc.wait_ge(s_ln, done(at.n))
                sc.wait_ge(s_z, done(at.n - 4))
                nc.scalar.activation(rstd[at.k][:], ln[at.k][:], ACT.Exp, scale=-0.5).then_inc(s_rstd, 1)

            staggered(nc.scalar, NP, 4, (2, squares), (1, logarithm), (0, root))

        @block.vector
        def _(ve):
            give_credits(ve, s_z)

            def normalise(at):
                ve.wait_ge(s_rstd, done(at.n))
                nc.vector.tensor_tensor(row(s.z, at.n), cen[at.k][:], rstd[at.k][:], ALU.mult).then_inc(s_z, 1)

            staggered(nc.vector, NP, 4, (0, normalise))

        @block.gpsimd
        def _(pool):
            if features:
                give_credits(pool, s_feat)

                def add(at):
                    pool.wait_ge(s_z, done(at.n))
                    pool.wait_ge(s_feat, done(at.n - 1))
                    nc.gpsimd.tensor_tensor(s.feat[:], s.feat[:], row(s.z, at.n), ALU.add).then_inc(s_feat, 1)

                staggered(nc.gpsimd, NP, 4, (0, add))


def neighbourhood_attention(nc, s):
    with ExitStack() as ctx:
        def sb(name, shape, dt=F32, n=2):
            return [ctx.enter_context(nc.sbuf_tensor(f"na_{name}{k}", shape, dt)) for k in range(n)]

        def ps(name, n=1):
            return [ctx.enter_context(nc.psum_tensor(f"na_{name}{k}", [128, 512], F32)) for k in range(n)]

        def sem(name):
            return ctx.enter_context(nc.semaphore("na_" + name))

        zt = sb("zt", [128, T])
        q = sb("q", [128, 2, 2, TG])
        kk = sb("k", [128, 2, TG])
        kblk = [s.z[:, NP + NH * k:NP + NH * k + NH, :].rearrange("p h (two t) -> p h two t", two=2) for k in range(2)]
        v = sb("v", [128, 2 * NT, 2, NH // 2, 18])
        diff, e = sb("diff", [128, NH * WIN]), sb("e", [128, NH * WIN])
        rowmax = sb("rowmax", [128, NH])
        et = sb("et", [128, NH // 2, 128])
        rden = sb("rden", [128, NH // 2, 2])
        on = sb("on", [128, 2, D])
        ot = sb("ot", [128, 2, TG])
        p_s, p_t, p_o, p_prep, p_ot, p_out = ps("ps", 2), ps("pt", 2), ps("po")[0], ps("pprep")[0], ps("pot")[0], ps("pout")[0]
        s_zt, s_prep, s_prepd, s_k, s_score, s_max, s_diff, s_e, s_et, s_etd, s_o, s_rden, s_on, s_ot, s_otd, s_out, s_h, s_zero = [
            sem(x) for x in ("zt", "prep", "prepd", "k", "score", "max", "diff", "e", "et", "etd", "o", "rden", "on", "ot", "otd", "out", "h", "zero")]
        block = ctx.enter_context(nc.Block())
        PREP = 6

        def group(at):
            g = at.k % 8
            return g // 4, g // 2 % 2, g % 2

        def uses(i, part):
            return i * PREP + part

        @block.gpsimd
        def _(pool):
            for t in q:
                nc.gpsimd.memset(t[:], 0.0).then_inc(s_zero, 1)
            for t in v:
                nc.gpsimd.memset(t[:], 0.0).then_inc(s_zero, 1)
            pool.wait_ge(s_zero, 4)
            for t in v:
                nc.gpsimd.tensor_tensor(t[:, :, :, :, 16:18].rearrange("p a b c d -> p (a b c) d"),
                                        t[:, :, :, :, 16:18].rearrange("p a b c d -> p (a b c) d"),
                                        const(s, "vmask")[:, 16:18].unsqueeze(1).broadcast_to([128, 2 * NT * NH, 2]), ALU.add).then_inc(s_zero, 1)
            give_credits(pool, s_zt)

            def copy(at):
                if at.k % 8 == 0:
                    i = at.of(8)
                    pool.wait_ge(s_k, done(i - 2))
                    pool_copy(nc, s, zt[at.k // 8][:], row(s.z, i)).then_inc(s_zt, 1)

            staggered(nc.gpsimd, 8 * NP, 16, (0, copy))

        @block.tensor
        def _(te):
            give_credits(te, s_prep, s_score, s_et, s_o, s_ot, s_out)
            te.wait_ge(s_zero, 6)

            def prepare_pair(at):
                part = at.k % 8
                if part >= PREP:
                    return
                b = at.k // 8
                i = at.of(8)
                if part == 0:
                    te.wait_ge(s_zt, done(i))
                te.wait_ge(s_prepd, done(uses(i, part) - 1))
                if part < 2:
                    mm = nc.tensor.matmul(p_prep[:], s.a0_w[:, part, :], zt[b][:], start=True, stop=True)
                else:
                    for c in range(4):
                        par, t = divmod(4 * (part - 2) + c, NT)
                        first = par + DIL * window_start(t)
                        window = zt[b][:, first:first + DIL * (WIN - 1) + 1:DIL]
                        for head in range(2):
                            mm = nc.tensor.matmul(p_prep[64 * head:64 * head + WIN, c * 128:c * 128 + 128], window, s.a0_w[:, 2, :],
                                                  start=True, stop=True, skip_group_check=True)
                mm.then_inc(s_prep, 1)

            def scores(at):
                par, half, b = group(at)
                te.wait_ge(s_diff, done(at.n - 2))
                if at.k % 8 == 0:
                    te.wait_ge(s_k, done(at.of(8)))
                bank = p_s[at.k % 2]
                nc.tensor.matmul(bank[:, 0:NH * WIN], s.ident_b[:], s.winmask[:, half, :, :], start=True, stop=False, skip_group_check=True)
                for c in range(4):
                    t = 4 * half + c
                    w = window_start(t)
                    mm = nc.tensor.matmul(bank[QT * c:QT * c + QT, 0:NH * WIN], q[at.k // 8][:, b, par, t * QT:t * QT + QT],
                                          kblk[at.k // 8][:, :, par, w:w + WIN], start=False, stop=True, skip_group_check=True)
                mm.then_inc(s_score, 1)

            def transposes(at):
                te.wait_ge(s_e, done(at.n))
                te.wait_ge(s_etd, done(at.n - 2))
                for c in range(NH // 2):
                    mm = nc.tensor.transpose(p_t[at.k % 2][0:2 * WIN, c * 128:c * 128 + 128],
                                             e[at.k % 2][:, c * 2 * WIN:(c + 1) * 2 * WIN], const(s, "ident"))
                mm.then_inc(s_et, 1)

            def values(at):
                par, half, b = group(at)
                te.wait_ge(s_etd, done(at.n))
                te.wait_ge(s_on, done(at.n - 1))
                for c in range(NH // 2):
                    for t in range(4):
                        mm = nc.tensor.matmul(p_o[QT * t:QT * t + QT, c * 18:c * 18 + 18], et[at.k % 2][0:2 * WIN, c, QT * t:QT * t + QT],
                                              v[at.k // 8][0:2 * WIN, par * NT + 4 * half + t, b, c, :], start=True, stop=True)
                mm.then_inc(s_o, 1)

            def turn(at):
                if at.k % 2 == 1:
                    te.wait_ge(s_on, done(at.n))
                    te.wait_ge(s_otd, done(at.of(2) - 1))
                    nc.tensor.transpose(p_ot[:, 0:128], on[at.k // 2 % 2][:].rearrange("p a b -> p (a b)"), const(s, "ident")).then_inc(s_ot, 1)

            def project(at):
                if at.k % 8 == 7:
                    i = at.of(8)
                    te.wait_ge(s_otd, done(at.of(2)))
                    te.wait_ge(s_h, done(i - 1))
                    nc.tensor.matmul(p_out[:], s.a0_wp[:], ot[at.k // 8][:].rearrange("p a b -> p (a b)"), start=True, stop=True).then_inc(s_out, 1)

            staggered(nc.tensor, 8 * NP, 16, (9, scores), (6, transposes), (4, values), (2, turn), (0, project), (16, prepare_pair))

        @block.scalar
        def _(sc):
            sc.preload_act_table_set("natural_log_exp_and_others")
            give_credits(sc, s_e, s_etd, s_otd)
            sc.wait_ge(s_zero, 6)

            def queries(at):
                if at.k % 8 == 0:
                    i = at.of(8)
                    sc.wait_ge(s_prep, done(uses(i, 0)))
                    sc.wait_ge(s_score, done(at.n - 9))
                    for b in range(2):
                        half = slice(64 * b, 64 * b + 64)
                        ins = nc.scalar.activation(q[at.k // 8][half, b, :, :], p_prep[half, :].rearrange("p (t two) -> p two t", two=2), ACT.Identity,
                                                   bias=s.cols[half, COLS["a0_bq"]:COLS["a0_bq"] + 1])
                    ins.then_inc(s_prepd, 1)

            def exponential(at):
                sc.wait_ge(s_diff, done(at.n))
                sc.wait_ge(s_et, done(at.n - 2))
                nc.scalar.activation(e[at.k % 2][:], diff[at.k % 2][:], ACT.Exp, scale=float(DH) ** -0.5).then_inc(s_e, 1)

            def fetch(at):
                sc.wait_ge(s_et, done(at.n))
                sc.wait_ge(s_o, done(at.n - 2))
                nc.scalar.activation(et[at.k % 2][0:2 * WIN, :, :].rearrange("p a b -> p (a b)"), p_t[at.k % 2][0:2 * WIN, :], ACT.Copy).then_inc(s_etd, 1)

            def fetch_output(at):
                if at.k % 2 == 1:
                    par, half, _ = group(at)
                    sc.wait_ge(s_ot, done(at.of(2)))
                    if at.k % 8 == 1:
                        sc.wait_ge(s_out, done(at.of(8) - 2))
                    nc.scalar.activation(ot[at.k // 8][:, par, half * 128:half * 128 + 128], p_ot[:, 0:128], ACT.Copy).then_inc(s_otd, 1)

            staggered(nc.scalar, 8 * NP, 16, (7, exponential), (5, fetch), (1, fetch_output), (15, queries))

        @block.vector
        def _(ve):
            ve.sem_inc(s_prepd, CREDITS)
            give_credits(ve, s_max, s_diff, s_k, s_rden, s_on, s_h)
            ve.wait_ge(s_zero, 6)

            def prepare_pair(at):
                part, i, b = at.k % 8, at.of(8), at.k // 8
                if part == 1:
                    ve.wait_ge(s_prep, done(uses(i, 1)))
                    nc.vector.tensor_scalar(kk[b][:], p_prep[:].rearrange("p (t two) -> p two t", two=2), col(s, "a0_bk"), None, ALU.add)\
                        .then_inc(s_prepd, 1)
                elif 2 <= part < PREP:
                    ve.wait_ge(s_prep, done(uses(i, part)))
                    if part == 2:
                        ve.wait_ge(s_o, done(i * 8 - 9))
                    out = v[b][0:2 * WIN, 4 * (part - 2):4 * (part - 1), :, :, 0:16].rearrange("p a b c d -> p (a b c) d")
                    nc.vector.tensor_tensor(out, p_prep[0:2 * WIN, :].rearrange("p (a d) -> p a d", d=16),
                                            const(s, "vmask", 2 * WIN)[:, 0:16].unsqueeze(1).broadcast_to([2 * WIN, 32, 16]), ALU.mult).then_inc(s_prepd, 1)
                if 2 <= part < 6:
                    if part == 2:
                        ve.wait_ge(s_prepd, done(uses(i, 1)))
                        ve.wait_ge(s_score, done(i * 8 - 9))
                    for h in (2 * part - 4, 2 * part - 3):
                        ins = nc.vector.tensor_scalar(kblk[b][:, h, :, :], kk[b][:], const(s, "headmask")[:, h:h + 1], None, ALU.mult)
                    if part == 5:
                        ins.then_inc(s_k, 1)

            def maximum(at):
                ve.wait_ge(s_score, done(at.n))
                sc_ = p_s[at.k % 2][:, 0:NH * WIN].rearrange("p (h w) -> p h w", h=NH)
                nc.vector.tensor_reduce(rowmax[at.k % 2][:], sc_, AX, ALU.max).then_inc(s_max, 1)
                ve.wait_ge(s_max, done(at.n))
                ve.wait_ge(s_e, done(at.n - 2))
                nc.vector.tensor_tensor(diff[at.k % 2][:].rearrange("p (h w) -> p h w", h=NH), sc_,
                                        rowmax[at.k % 2][:].unsqueeze(2).broadcast_to([128, NH, WIN]), ALU.subtract).then_inc(s_diff, 1)

            def normalise(at):
                _, _, b = group(at)
                ve.wait_ge(s_o, done(at.n))
                o = p_o[:, 0:72].rearrange("p (c d) -> p c d", c=NH // 2)
                nc.vector.reciprocal(rden[at.k % 2][:], o[:, :, 16:18]).then_inc(s_rden, 1)
                ve.wait_ge(s_rden, done(at.n))
                ve.wait_ge(s_ot, done(at.of(2) - 2))
                nc.vector.tensor_tensor(on[at.k // 2 % 2][:, b, :].rearrange("p (c h d) -> p c h d", c=NH // 2, h=2),
                                        o[:, :, 0:16].rearrange("p c (h d) -> p c h d", h=2),
                                        rden[at.k % 2][:].unsqueeze(3).broadcast_to([128, NH // 2, 2, DH]), ALU.mult).then_inc(s_on, 1)

            def residual(at):
                if at.k % 8 == 7:
                    i = at.of(8)
                    ve.wait_ge(s_out, done(i))
                    h = row(s.h, i).rearrange("p (t two) -> p two t", two=2)
                    nc.vector.scalar_tensor_tensor(out=h, in0=p_out[:].rearrange("p (two t) -> p two t", two=2), scalar=col(s, "a0_bp"),
                                                   in1=h, op0=ALU.add, op1=ALU.add).then_inc(s_h, 1)

            staggered(nc.vector, 8 * NP, 16, (8, maximum), (3, normalise), (0, residual), (15, prepare_pair))


def route(nc, s):
    with ExitStack() as ctx:
        def sb(name, shape, dt=F32):
            return ctx.enter_context(nc.sbuf_tensor("ro_" + name, shape, dt))

        groups = NP * 4 * 2
        zt = [sb(f"zt{k}", [128, T]) for k in range(4)]
        logits, best, masked, picked, other = [sb(x, [128, groups, NE]) for x in ("logits", "best", "masked", "picked", "other")]
        first, second, top, total = [sb(x, [128, groups]) for x in ("first", "second", "top", "total")]
        p_l = [ctx.enter_context(nc.psum_tensor(f"ro_p{k}", [128, 4, 128], F32)) for k in range(4)]
        s_zt, s_l, s_ld, s_v, s_e = [ctx.enter_context(nc.semaphore("ro_" + x)) for x in ("s_zt", "s_l", "s_ld", "s_v", "s_e")]
        block = ctx.enter_context(nc.Block())

        def wide(t):
            return t[:].unsqueeze(2).broadcast_to([128, groups, NE])

        @block.gpsimd
        def _(pool):
            give_credits(pool, s_zt)

            def copy(at):
                pool.wait_ge(s_l, done(at.n - 4))
                pool_copy(nc, s, zt[at.k][:], row(s.z, at.n)).then_inc(s_zt, 1)

            staggered(nc.gpsimd, NP, 4, (0, copy))

        @block.tensor
        def _(te):
            give_credits(te, s_l)

            def product(at):
                te.wait_ge(s_zt, done(at.n))
                te.wait_ge(s_ld, done(at.n - 4))
                for c in range(4):
                    mm = nc.tensor.matmul(p_l[at.k][:, c, :], zt[at.k][:, c * 128:c * 128 + 128], s.moe_wr[:], start=True, stop=True)
                mm.then_inc(s_l, 1)

            staggered(nc.tensor, NP, 4, (0, product))

        @block.scalar
        def _(sc):
            sc.preload_act_table_set("natural_log_exp_and_others")
            sc.wait_ge(s_v, 11)
            nc.scalar.activation(masked[:], masked[:], ACT.Exp).then_inc(s_e, 1)

        @block.vector
        def _(ve):
            give_credits(ve, s_ld)
            all_logits = logits[:].rearrange("p (i g) e -> p i (g e)", i=NP)

            def fetch(at):
                ve.wait_ge(s_l, done(at.n))
                nc.vector.tensor_copy(row(all_logits, at.n).rearrange("p (c n) -> p c n", c=4), p_l[at.k][:, :, 0:2 * NE]).then_inc(s_ld, 1)

            staggered(nc.vector, NP, 4, (0, fetch))
            ve.wait_ge(s_ld, done(NP - 1))
            n = [0]

            def step(ins):
                ins.then_inc(s_v, 1)
                n[0] += 1
                ve.wait_ge(s_v, n[0])

            v = nc.vector
            rank = const(s, "rank").unsqueeze(1).broadcast_to([128, groups, NE])
            step(v.tensor_reduce(first[:], logits[:], AX, ALU.max))
            step(v.tensor_tensor(best[:], logits[:], wide(first), ALU.is_equal))
            step(v.tensor_tensor(best[:], best[:], rank, ALU.mult))
            step(v.tensor_reduce(top[:], best[:], AX, ALU.max))
            step(v.tensor_tensor(best[:], best[:], wide(top), ALU.is_equal))
            step(v.scalar_tensor_tensor(out=masked[:], in0=best[:], scalar=-3.0e38, in1=logits[:], op0=ALU.mult, op1=ALU.add))
            step(v.tensor_reduce(second[:], masked[:], AX, ALU.max))
            step(v.tensor_tensor(picked[:], masked[:], wide(second), ALU.is_equal))
            step(v.tensor_tensor(picked[:], picked[:], rank, ALU.mult))
            step(v.tensor_reduce(top[:], picked[:], AX, ALU.max))
            step(v.tensor_tensor(masked[:], logits[:], wide(first), ALU.subtract))
            step(v.tensor_tensor(picked[:], picked[:], wide(top), ALU.is_equal))
            step(v.tensor_tensor(picked[:], picked[:], best[:], ALU.add))
            ve.wait_ge(s_e, 1)
            step(v.tensor_tensor(other[:], picked[:], masked[:], ALU.mult))
            step(v.tensor_reduce(total[:], other[:], AX, ALU.add))
            step(v.reciprocal(total[:], total[:]))
            step(v.tensor_tensor(other[:], other[:], wide(total), ALU.mult))
            parts = s.combine[:].rearrange("p i c (b n) -> p (i c b) n", b=2)
            step(v.tensor_copy(parts[:, :, 0:NE], other[:]))
            step(v.tensor_tensor(parts[:, :, NE:2 * NE], other[:], parts[:, :, 0:NE].bitcast(F32), ALU.subtract))


def stack_high(nc, s, zs, zrow):
    return pool_copy(nc, s, zs[:], zrow.unsqueeze(1).broadcast_to([128, 2, T]))


def stack_low(nc, zs, zrow, b):
    own, other = slice(64 * b, 64 * b + 64), slice(64 - 64 * b, 128 - 64 * b)
    return nc.vector.tensor_tensor(zs[other, b, :], zrow[own, :], zs[own, b, :].bitcast(F32), ALU.subtract)


def mixture_of_experts(nc, s):
    with ExitStack() as ctx:
        def sb(name, shape, dt=F32, n=2):
            return [ctx.enter_context(nc.sbuf_tensor(f"me_{name}{k}", shape, dt)) for k in range(n)]

        def ps(name, n=2):
            return [ctx.enter_context(nc.psum_tensor(f"me_{name}{k}", [128, T], F32)) for k in range(n)]

        zs = sb("zs", [128, 2, T], F32R)
        ct_in, ct = sb("ctin", [128, 4 * 4 * NE]), sb("ct", [128, T], F32R)
        g, gw = sb("g", [128, T], n=4), sb("gw", [128, T], n=4)
        p_1, p_c, p_y, p_t = ps("p1"), ps("pc"), ps("py"), ps("pt", 1)[0]
        s_zero, s_ctin, s_high, s_low, s_hz, s_t, s_ct, s_w1, s_c, s_g, s_gw, s_w2, s_h = [
            ctx.enter_context(nc.semaphore("me_" + x)) for x in ("zero", "ctin", "high", "low", "hz", "t", "ct", "w1", "c", "g", "gw", "w2", "h")]
        block = ctx.enter_context(nc.Block())

        def where(at):
            return at.k % 8 // EP, at.k % EP

        @block.gpsimd
        def _(pool):
            for t in ct:
                nc.gpsimd.memset(t[:].bitcast(F32), 0.0).then_inc(s_zero, 1)
            give_credits(pool, s_ctin, s_high, s_hz)

            def prepare(at):
                if at.k % 8 == 0:
                    i, k = at.of(8), at.k // 8
                    pool.wait_ge(s_t, done(i - 2))
                    pool_copy(nc, s, ct_in[k][:], s.combine[:, bass.ds(i, 1), :, :].rearrange("p a b c -> p (a b c)").bitcast(F32)).then_inc(s_ctin, 1)
                    pool.wait_ge(s_w1, done(at.n - 9))
                    stack_high(nc, s, zs[k], row(s.z, i)).then_inc(s_high, 1)
                    nc.gpsimd.tensor_tensor(row(s.h, i), row(s.h, i), row(s.z, i), ALU.add).then_inc(s_hz, 1)

            staggered(nc.gpsimd, 8 * NP, 16, (0, prepare))

        @block.tensor
        def _(te):
            give_credits(te, s_t, s_w1, s_c, s_w2)
            te.wait_ge(s_zero, 2)

            def turn(at):
                if at.k % 8 == 0:
                    i = at.of(8)
                    te.wait_ge(s_ctin, done(i))
                    te.wait_ge(s_ct, done(i - 1))
                    for c in range(4):
                        mm = nc.tensor.transpose(p_t[0:4 * NE, c * 128:c * 128 + 128], ct_in[at.k // 8][:, c * 4 * NE:(c + 1) * 4 * NE], const(s, "ident"))
                    mm.then_inc(s_t, 1)

            def first(at):
                b, ep = where(at)
                if at.k % 8 == 0:
                    te.wait_ge(s_low, done(at.of(8)))
                te.wait_ge(s_g, done(at.n - 2))
                z = zs[at.k // 8][:, b, :]
                nc.tensor.matmul(p_1[at.k % 2][:], s.moe_w1h[:, ep, :], z, start=True, stop=False)
                nc.tensor.matmul(p_1[at.k % 2][:], s.moe_w1l[:, ep, :], z, start=False, stop=True).then_inc(s_w1, 1)

            def spread(at):
                b, ep = where(at)
                if at.k % 8 == 0:
                    te.wait_ge(s_ct, done(at.of(8)))
                te.wait_ge(s_gw, done(at.n - 2))
                nc.tensor.matmul(p_c[at.k % 2][:], s.pick[:, b, ep, :], ct[at.k // 8][:], start=True, stop=True).then_inc(s_c, 1)

            def bias(at):
                if at.k % 8 == 0:
                    te.wait_ge(s_h, done(at.of(8) - 2))
                    y = p_y[at.k // 8][:]
                    nc.tensor.matmul(y, s.moe_b2h[:], ct[at.k // 8][:], start=True, stop=False, skip_group_check=True)
                    nc.tensor.matmul(y, s.moe_b2l[:], ct[at.k // 8][:], start=False, stop=False, skip_group_check=True)

            def second(at):
                b, ep = where(at)
                te.wait_ge(s_gw, done(at.n))
                nc.tensor.matmul(p_y[at.k // 8][64 * b:64 * b + 64, :], s.moe_w2[:, ep, :], gw[at.k % 4][:], start=False, stop=(ep == EP - 1),
                                 skip_group_check=True).then_inc(s_w2, 1)

            staggered(nc.tensor, 8 * NP, 16, (4, first), (3, spread), (2, bias), (1, second), (10, turn))

        @block.scalar
        def _(sc):
            give_credits(sc, s_ct, s_g)

            def gelu(at):
                _, ep = where(at)
                sc.wait_ge(s_w1, done(at.n))
                sc.wait_ge(s_gw, done(at.n - 4))
                nc.scalar.activation(g[at.k % 4][:], p_1[at.k % 2][:], ACT.Gelu, bias=col(s, "moe_b1", ep)).then_inc(s_g, 1)

            def fetch(at):
                if at.k % 8 == 0:
                    sc.wait_ge(s_t, done(at.of(8)))
                    sc.wait_ge(s_c, done(at.n - 9))
                    sc.wait_ge(s_w2, done(at.n - 9))
                    nc.scalar.activation(ct[at.k // 8][0:4 * NE, :], p_t[0:4 * NE, :], ACT.Copy).then_inc(s_ct, 1)

            sc.wait_ge(s_zero, 2)
            staggered(nc.scalar, 8 * NP, 16, (3, gelu), (9, fetch))

        @block.vector
        def _(ve):
            give_credits(ve, s_low, s_gw, s_h)

            def low(at):
                if at.k % 8 == 0:
                    i = at.of(8)
                    ve.wait_ge(s_high, done(i))
                    stack_low(nc, zs[at.k // 8], row(s.z, i), 0)
                    stack_low(nc, zs[at.k // 8], row(s.z, i), 1).then_inc(s_low, 1)

            def weigh(at):
                ve.wait_ge(s_g, done(at.n))
                ve.wait_ge(s_c, done(at.n))
                ve.wait_ge(s_w2, done(at.n - 4))
                nc.vector.tensor_tensor(gw[at.k % 4][:], p_c[at.k % 2][:], g[at.k % 4][:], ALU.mult).then_inc(s_gw, 1)

            def residual(at):
                if at.k % 8 == 7:
                    i = at.of(8)
                    ve.wait_ge(s_w2, done(at.n))
                    ve.wait_ge(s_hz, done(i))
                    nc.vector.tensor_tensor(row(s.h, i), p_y[at.k // 8][:], row(s.h, i), ALU.add).then_inc(s_h, 1)

            staggered(nc.vector, 8 * NP, 16, (2, weigh), (0, residual), (12, low))


def decayed_attention(nc, s):
    with ExitStack() as ctx:
        def sb(name, shape, dt=F32, n=4):
            return [ctx.enter_context(nc.sbuf_tensor(f"da_{name}{k}", shape, dt)) for k in range(n)]

        def ps(name, n=1):
            return [ctx.enter_context(nc.psum_tensor(f"da_{name}{k}", [128, T], F32)) for k in range(n)]

        zt = sb("zt", [128, T])
        zs = sb("zs", [128, 2, T], F32R)
        qh, ql, kk = sb("qh", [128, T], F32R), sb("ql", [128, T], F32R), sb("k", [128, T], F32R)
        vt = [s.z[:, NP + k, :].rearrange("p (c n) -> p c n", c=4) for k in range(4)]
        width = [T - 128 * j for j in range(4)]
        free = s.z[:, NP + 4:NP + 10, :].rearrange("p a b -> p (a b)")
        sm = [[free[:, 3 * T * k + sum(width[:j]):3 * T * k + sum(width[:j + 1])] for j in range(4)] for k in range(2)]
        p_q, p_k, p_v, p_s, p_o = ps("pq")[0], ps("pk")[0], ps("pv")[0], ps("ps", 3), ps("po", 2)
        bank = [p_s[0][:, 0:width[0]], p_s[1][:, 0:width[1]], p_s[2][:, 0:width[2]], p_s[2][:, width[2]:width[2] + width[3]]]
        s_zt, s_high, s_low, s_qk, s_kh, s_kl, s_v, s_vt, s_s, s_sm, s_o, s_h, s_qh = [
            ctx.enter_context(nc.semaphore("da_" + x)) for x in ("s_zt", "high", "low", "qk", "kh", "kl", "v", "s_vt", "s", "sm", "o", "h", "s_qh")]
        block = ctx.enter_context(nc.Block())

        @block.gpsimd
        def _(pool):
            give_credits(pool, s_zt, s_high)

            def prepare(at):
                i = at.of(2)
                if at.k % 2 == 0:
                    pool.wait_ge(s_v, done(i - 4))
                    pool.wait_ge(s_qk, done(at.n - 7))
                    pool_copy(nc, s, zt[at.k // 2][:], row(s.z, i)).then_inc(s_zt, 1)
                    stack_high(nc, s, zs[at.k // 2], row(s.z, i)).then_inc(s_high, 1)

            staggered(nc.gpsimd, NB, 8, (0, prepare))

        @block.tensor
        def _(te):
            give_credits(te, s_qk, s_v, s_s, s_o)

            def queries_keys(at):
                te.wait_ge(s_low, done(at.n))
                te.wait_ge(s_kl, done(at.n - 1))
                z = zs[at.k // 2][:, at.k % 2, :]
                for c, p in enumerate((p_q, p_k)):
                    nc.tensor.matmul(p[:], s.a1_qkh[:, c, :], z, start=True, stop=False)
                    mm = nc.tensor.matmul(p[:], s.a1_qkl[:, c, :], z, start=False, stop=True)
                mm.then_inc(s_qk, 1)

            def values(at):
                if at.k % 2 == 0:
                    i = at.of(2)
                    te.wait_ge(s_zt, done(i))
                    te.wait_ge(s_vt, done(i - 1))
                    for c in range(4):
                        mm = nc.tensor.matmul(p_v[:, c * 128:c * 128 + 128], zt[at.k // 2][:, c * 128:c * 128 + 128], s.a1_wv[:], start=True, stop=True)
                    mm.then_inc(s_v, 1)

            def scores(at):
                te.wait_ge(s_kl, done(at.n))
                te.wait_ge(s_sm, done(4 * at.n - 1))
                for j in range(4):
                    keys = kk[at.k % 4][:, 128 * j:128 * j + 128]
                    nc.tensor.matmul(bank[j], keys, qh[at.k % 4][:, 128 * j:], start=True, stop=False, skip_group_check=True)
                    mm = nc.tensor.matmul(bank[j], keys, ql[at.k % 4][:, 128 * j:], start=False, stop=True, skip_group_check=True)
                    if j != 2:
                        mm.then_inc(s_s, 1)

            def outputs(at):
                b = at.k % 2
                te.wait_ge(s_sm, done(4 * at.n + 3))
                if b == 0:
                    te.wait_ge(s_vt, done(at.of(2)))
                    te.wait_ge(s_h, done(at.of(2) - 2))
                for j in range(4):
                    mm = nc.tensor.matmul(p_o[at.k // 2 % 2][64 * b:64 * b + 64, 128 * j:], vt[at.k // 2][:, j, 64 * b:64 * b + 64], sm[at.k % 2][j],
                                          start=(j == 0), stop=(j == 3), skip_group_check=True)
                mm.then_inc(s_o, 1)

            staggered(nc.tensor, NB, 8, (6, queries_keys), (6, values), (3, scores), (1, outputs))

        @block.scalar
        def _(sc):
            give_credits(sc, s_qh, s_kh)

            def high(at):
                sc.wait_ge(s_qk, done(at.n))
                sc.wait_ge(s_s, done(3 * at.n - 10))
                nc.scalar.activation(qh[at.k % 4][:], p_q[:], ACT.Identity, bias=col(s, "a1_bq")).then_inc(s_qh, 1)
                nc.scalar.activation(kk[at.k % 4][:], p_k[:], ACT.Identity, bias=col(s, "a1_bk")).then_inc(s_kh, 1)

            staggered(nc.scalar, NB, 8, (5, high))

        @block.vector
        def _(ve):
            give_credits(ve, s_low, s_kl, s_vt, s_sm, s_h)

            def low(at):
                ve.wait_ge(s_high, done(at.of(2)))
                stack_low(nc, zs[at.k // 2], row(s.z, at.of(2)), at.k % 2).then_inc(s_low, 1)

            def split(at):
                up = slice(64, 128)
                ve.wait_ge(s_qh, done(at.n))
                nc.vector.scalar_tensor_tensor(out=ql[at.k % 4][:], in0=p_q[:], scalar=col(s, "a1_bq"), in1=qh[at.k % 4][:].bitcast(F32),
                                               op0=ALU.add, op1=ALU.subtract)
                ve.wait_ge(s_kh, done(at.n))
                nc.vector.scalar_tensor_tensor(out=kk[at.k % 4][up, :], in0=p_k[up, :], scalar=s.cols[up, COLS["a1_bk"]:COLS["a1_bk"] + 1],
                                               in1=kk[at.k % 4][up, :].bitcast(F32), op0=ALU.add, op1=ALU.subtract).then_inc(s_kl, 1)

            def values(at):
                if at.k % 2 == 0:
                    ve.wait_ge(s_v, done(at.of(2)))
                    ve.wait_ge(s_o, done(at.n - 7))
                    nc.vector.tensor_tensor(vt[at.k // 2], p_v[:].rearrange("p (c n) -> p c n", c=4),
                                            s.a1_bv[:].rearrange("p a b -> p (a b)").unsqueeze(1).broadcast_to([128, 4, 128]), ALU.add).then_inc(s_vt, 1)

            def decay(at):
                ve.wait_ge(s_o, done(at.n - 2))
                for j in range(4):
                    ve.wait_ge(s_s, done(3 * at.n + min(j, 2)))
                    nc.vector.tensor_tensor(sm[at.k % 2][j], bank[j], const(s, "decay")[:, 0:width[j]], ALU.mult).then_inc(s_sm, 1)

            def residual(at):
                if at.k % 2 == 1:
                    ve.wait_ge(s_o, done(at.n))
                    h = row(s.h, at.of(2))
                    nc.vector.tensor_tensor(h, p_o[at.k // 2 % 2][:], h, ALU.add).then_inc(s_h, 1)

            staggered(nc.vector, NB, 8, (7, low), (5, split), (5, values), (2, decay), (0, residual))


def soft_router(nc, s):
    with ExitStack() as ctx:
        def sb(name, shape):
            return ctx.enter_context(nc.sbuf_tensor("sr_" + name, shape, F32))

        logits, w = sb("logits", [128, 4, NE]), sb("w", [128, 4, NE])
        top, total = sb("top", [128, 4]), sb("total", [128, 4])
        wide_w = sb("wide", [128, 4, NE, D])
        ps = [ctx.enter_context(nc.psum_tensor(f"sr_p{k}", [128, 4, 128], F32)) for k in range(6)]
        s_p, s_v, s_a = [ctx.enter_context(nc.semaphore("sr_" + x)) for x in ("pe", "dve", "act")]
        block = ctx.enter_context(nc.Block())

        @block.tensor
        def _(te):
            for c in range(4):
                nc.tensor.matmul(ps[0][:, c, :], s.feat[:, c * 128:c * 128 + 128], s.f1_wr[:], start=True, stop=True).then_inc(s_p, 1)
            te.wait_ge(s_v, 8)
            for ep in range(EP):
                for c in range(4):
                    nc.tensor.matmul(ps[1 + ep][:, c, :], wide_w[:, c, 2 * ep:2 * ep + 2, :].rearrange("p a b -> p (a b)"), const(s, "ident"),
                                     start=True, stop=True).then_inc(s_p, 1)
            for ep in range(EP):
                te.wait_ge(s_a, ep + 2)
                nc.tensor.matmul(ps[5][:].rearrange("p a b -> p (a b)"), s.f1_wdup[:, ep, :, :].rearrange("p a b -> p (a b)"), s.f1_w[:, ep, :],
                                 start=(ep == 0), stop=(ep == EP - 1)).then_inc(s_p, 1)

        @block.scalar
        def _(sc):
            sc.preload_act_table_set("natural_log_exp_and_others")
            sc.wait_ge(s_v, 4)
            nc.scalar.activation(w[:], logits[:], ACT.Exp).then_inc(s_a, 1)
            for ep in range(EP):
                sc.wait_ge(s_p, 4 + 4 * (ep + 1))
                nc.scalar.activation(s.f1_w[:, ep, :], ps[1 + ep][:].rearrange("p a b -> p (a b)"), ACT.Copy).then_inc(s_a, 1)
            sc.wait_ge(s_p, 24)
            nc.scalar.activation(s.f1_r, ps[5][:].rearrange("p a b -> p (a b)"), ACT.Copy).then_inc(s_a, 1)

        @block.vector
        def _(ve):
            n = [0]

            def step(ins):
                ins.then_inc(s_v, 1)
                n[0] += 1
                ve.wait_ge(s_v, n[0])

            def wide(t):
                return t[:].unsqueeze(2).broadcast_to([128, 4, NE])

            v = nc.vector
            ve.wait_ge(s_p, 4)
            step(v.tensor_scalar(logits[:], ps[0][:, :, 0:NE], 1.0 / NB, None, ALU.mult))
            step(v.tensor_tensor(logits[:], logits[:], s.f1_br[:].unsqueeze(1).broadcast_to([128, 4, NE]), ALU.add))
            step(v.tensor_reduce(top[:], logits[:], AX, ALU.max))
            step(v.tensor_tensor(logits[:], logits[:], wide(top), ALU.subtract))
            ve.wait_ge(s_a, 1)
            step(v.tensor_reduce(total[:], w[:], AX, ALU.add))
            step(v.reciprocal(total[:], total[:]))
            step(v.tensor_tensor(w[:], w[:], wide(total), ALU.mult))
            step(v.tensor_copy(wide_w[:].rearrange("p a b c -> p (a b) c"), w[:].rearrange("p a b -> p (a b)").unsqueeze(2).broadcast_to([128, 4 * NE, D])))


def soft_experts(nc, s, out):
    with ExitStack() as ctx:
        def sb(name, shape, dt=F32, n=2):
            return [ctx.enter_context(nc.sbuf_tensor(f"se_{name}{k}", shape, dt)) for k in range(n)]

        def ps(name, n=2):
            return [ctx.enter_context(nc.psum_tensor(f"se_{name}{k}", [128, T], F32)) for k in range(n)]

        zs = sb("zs", [128, 2, T], F32R)
        a1, a2 = sb("a1", [128, T], n=4), sb("a2", [128, T], n=4)
        res, rows = sb("res", [128, T]), sb("rows", [128, 2, 4, D])
        p_1, p_2, p_y, p_t = ps("p1"), ps("p2"), ps("py"), ps("pt", 1)[0]
        s_high, s_low, s_hr, s_w1, s_a1, s_w2, s_a2, s_wo, s_res, s_t, s_rows, *s_out = [
            ctx.enter_context(nc.semaphore("se_" + x)) for x in ("high", "low", "hr", "w1", "s_a1", "w2", "s_a2", "wo", "s_res", "t", "s_rows", "out0", "out1")]
        block = ctx.enter_context(nc.Block())

        def where(at):
            return at.k % 8 // EP, at.k % EP

        @block.gpsimd
        def _(pool):
            give_credits(pool, s_high, s_hr)

            def prepare(at):
                if at.k % 8 == 0:
                    i, k = at.of(8), at.k // 8
                    pool.wait_ge(s_w1, done(at.n - 9))
                    stack_high(nc, s, zs[k], row(s.z, i)).then_inc(s_high, 1)
                    nc.gpsimd.tensor_tensor(row(s.h, i), row(s.h, i), s.f1_r, ALU.add).then_inc(s_hr, 1)

            staggered(nc.gpsimd, 8 * NP, 16, (0, prepare))

        @block.tensor
        def _(te):
            give_credits(te, s_w1, s_w2, s_wo, s_t)

            def first(at):
                b, ep = where(at)
                if at.k % 8 == 0:
                    te.wait_ge(s_low, done(at.of(8)))
                te.wait_ge(s_a1, done(at.n - 2))
                z = zs[at.k // 8][:, b, :]
                nc.tensor.matmul(p_1[at.k % 2][:], s.f1_w1h[:, ep, :], z, start=True, stop=False)
                nc.tensor.matmul(p_1[at.k % 2][:], s.f1_w1l[:, ep, :], z, start=False, stop=True).then_inc(s_w1, 1)

            def second(at):
                _, ep = where(at)
                te.wait_ge(s_a1, done(at.n))
                te.wait_ge(s_a2, done(at.n - 2))
                nc.tensor.matmul(p_2[at.k % 2][:], s.f1_w2[:, ep, :], a1[at.k % 4][:], start=True, stop=True).then_inc(s_w2, 1)

            def third(at):
                b, ep = where(at)
                te.wait_ge(s_a2, done(at.n))
                if at.k % 8 == 0:
                    te.wait_ge(s_res, done(at.of(8) - 2))
                nc.tensor.matmul(p_y[at.k // 8][64 * b:64 * b + 64, :], s.f1_wo[:, ep, :], a2[at.k % 4][:], start=(ep == 0), stop=(ep == EP - 1),
                                 skip_group_check=True).then_inc(s_wo, 1)

            def turn(at):
                if at.k % 8 == 7:
                    i = at.of(8)
                    te.wait_ge(s_res, done(i))
                    te.wait_ge(s_rows, done(i - 1))
                    for c in range(4):
                        mm = nc.tensor.transpose(p_t[:, c * 128:c * 128 + 128], res[at.k // 8][:, c::4], const(s, "ident"))
                    mm.then_inc(s_t, 1)

            staggered(nc.tensor, 8 * NP, 16, (7, first), (5, second), (3, third), (1, turn))

        @block.scalar
        def _(sc):
            give_credits(sc, s_a1, s_rows)

            def relu(at):
                _, ep = where(at)
                sc.wait_ge(s_w1, done(at.n))
                sc.wait_ge(s_w2, done(at.n - 4))
                nc.scalar.activation(a1[at.k % 4][:], p_1[at.k % 2][:], ACT.Relu, scale=col(s, "f1_g1", ep), bias=col(s, "f1_be1", ep)).then_inc(s_a1, 1)

            def fetch(at):
                if at.k % 8 == 7:
                    i = at.of(8)
                    sc.wait_ge(s_t, done(i))
                    sc.wait_ge(s_out[at.k // 8], at.of(16) * 16 + 16)
                    nc.scalar.activation(rows[at.k // 8][:].rearrange("p b t c -> p t b c"), p_t[:].rearrange("p (t b c) -> p t b c", t=4, b=2),
                                         ACT.Copy).then_inc(s_rows, 1)

            staggered(nc.scalar, 8 * NP, 16, (6, relu), (0, fetch))

        @block.vector
        def _(ve):
            give_credits(ve, s_low, s_a2, s_res)

            def low(at):
                if at.k % 8 == 0:
                    i = at.of(8)
                    ve.wait_ge(s_high, done(i))
                    stack_low(nc, zs[at.k // 8], row(s.z, i), 0)
                    stack_low(nc, zs[at.k // 8], row(s.z, i), 1).then_inc(s_low, 1)

            def weigh(at):
                _, ep = where(at)
                ve.wait_ge(s_w2, done(at.n))
                ve.wait_ge(s_wo, done(at.n - 4))
                nc.vector.scalar_tensor_tensor(out=a2[at.k % 4][:], in0=p_2[at.k % 2][:], scalar=col(s, "f1_be2", ep), in1=s.f1_w[:, ep, :],
                                               op0=ALU.max, op1=ALU.mult).then_inc(s_a2, 1)

            def residual(at):
                if at.k % 8 == 7:
                    i = at.of(8)
                    ve.wait_ge(s_wo, done(at.n))
                    ve.wait_ge(s_hr, done(i))
                    ve.wait_ge(s_t, done(i - 2))
                    nc.vector.tensor_tensor(res[at.k // 8][:], p_y[at.k // 8][:], row(s.h, i), ALU.add).then_inc(s_res, 1)

            staggered(nc.vector, 8 * NP, 16, (4, weigh), (2, residual), (12, low))

        @block.sync
        def _(sp):
            for x in s_out:
                sp.sem_inc(x, 16)

            def store(at):
                sp.wait_ge(s_rows, done(at.n))
                sp.dma_start(out[bass.ds(at.n * 2, 2), :, :].rearrange("b (p t) c -> p b (t c)", t=4),
                             rows[at.k][:].rearrange("p b t c -> p b (t c)")).then_inc(s_out[at.k], 16)

            staggered(nc.sync, NP, 2, (0, store))
            for x in s_out:
                sp.wait_ge(x, 16 * (1 + NP // 2))





def build(nc, a, out):
    with ExitStack() as ctx:
        s = allocate(nc, ctx)
        prepare(nc, s, a)
        spectral_norm(nc, s)
        tokenizer_output(nc, s)
        layer_norm(nc, s, "ln0")
        neighbourhood_attention(nc, s)
        layer_norm(nc, s, "ln1")
        route(nc, s)
        mixture_of_experts(nc, s)

        layer_norm(nc, s, "ln2")
        decayed_attention(nc, s)

        layer_norm(nc, s, "ln3", features=True)
        soft_router(nc, s)
        soft_experts(nc, s, out)


_INS = ['x', 'L0_tok_freq_bands', 'L0_tok_w1', 'L0_tok_b1', 'L0_tok_gamma', 'L0_tok_beta', 'L0_tok_w2', 'L0_tok_b2',
        'L0_attn_w_qkv', 'L0_attn_b_qkv', 'L0_attn_w_proj', 'L0_attn_b_proj', 'L0_ffn_router_w', 'L0_ffn_w1', 'L0_ffn_b1',
        'L0_ffn_w2', 'L0_ffn_b2', 'L1_attn_Wqkv', 'L1_attn_bqkv', 'L1_ffn_Wr', 'L1_ffn_br', 'L1_ffn_W1', 'L1_ffn_b1',
        'L1_ffn_g1', 'L1_ffn_be1', 'L1_ffn_m1', 'L1_ffn_v1', 'L1_ffn_W2', 'L1_ffn_b2', 'L1_ffn_g2', 'L1_ffn_be2',
        'L1_ffn_m2', 'L1_ffn_v2', 'L1_ffn_Wo', 'L1_ffn_bo']


def kernel(**inputs):
    import concourse.bacc as bacc
    from concourse.bass_utils import run_bass_kernel_spmd

    nc = bacc.Bacc("TRN2", target_bir_lowering=False, num_devices=1)
    arrays, aps = {}, {}
    for name in _INS + ["const"]:
        array = constants() if name == "const" else np.ascontiguousarray(inputs[name])
        arrays[f"in_{name}"] = array
        aps[name] = nc.dram_tensor(f"in_{name}", array.shape, mybir.dt.from_np(array.dtype), kind="ExternalInput").ap()
    out = nc.dram_tensor("out", (NB, T, D), F32, kind="ExternalOutput").ap()
    build(nc, aps, out)
    r = run_bass_kernel_spmd(nc, [arrays], core_ids=[0])
    return r.results[0]["out"]
```

```python
from contextlib import ExitStack

import numpy as np
import concourse.bass as bass
from concourse import mybir

F32 = mybir.dt.float32
F32R = mybir.dt.float32r
BF16 = mybir.dt.bfloat16
I32 = mybir.dt.int32
ALU = mybir.AluOpType
ACT = mybir.ActivationFunctionType
AX = mybir.AxisListType.X

NB, T, D = 32, 512, 64
NP = NB // 2
HID = 2 * D
NF = D // 2
NE = 8
EP = NE // 2
NH, DH = 8, 8
KW, DIL = 31, 2
TG = T // DIL
QT = 32
NT = TG // QT
WIN = 64
LN_EPS = 1e-5
BN_EPS = 1e-3
NEG = -1.0e30
ALPHA = 0.99


def window_start(t):
    return min(max(t * QT - KW // 2, 0), TG - WIN)


CONST_PARTS = [("ident", 128), ("dft", 4 * 2 * NF), ("shift", T), ("center", 128), ("mean64", 128), ("mean128", 128),
               ("decay", T), ("winmask", 2 * WIN), ("headmask", NH), ("vmask", 18), ("rank", NE),
               ("pick", 2 * EP * 128)]
CONST_AT = {}
_at = 0
for _name, _n in CONST_PARTS:
    CONST_AT[_name] = (_at, _n)
    _at += _n
CONST_COLS = _at
FIRST_CONST = CONST_AT["center"][0]


def constants():
    c = {}
    c["ident"] = np.eye(128)
    block = np.kron(np.eye(2), np.full((D, D), 1.0 / D))
    c["center"] = np.eye(128) - block
    c["mean64"] = block
    c["mean128"] = np.full((128, 128), 1.0 / HID)
    t = np.arange(T)[:, None] * np.arange(NF)[None, :] % T * (2 * np.pi / T)
    dft = np.concatenate([np.cos(t), -np.sin(t)], 1)
    c["dft"] = dft.reshape(4, 128, 2 * NF).transpose(1, 0, 2).reshape(128, -1)
    step = np.float32(2.0 * np.pi / T)
    shift = (step * np.arange(T, dtype=np.float32)[None, :]) * np.arange(NF, dtype=np.float32)[:, None]
    shift = shift.astype(np.float64)
    c["shift"] = np.concatenate([np.cos(shift), np.sin(shift)] * 2, 0)
    k, q = np.arange(128)[:, None], np.arange(T)[None, :]
    c["decay"] = np.where(q >= k, np.power(float(np.float32(ALPHA)), np.maximum(q - k, 0)), 0.0) / np.sqrt(D)
    mask = np.full((2, 128, WIN), NEG)
    for half in range(2):
        for r in range(128):
            p = half * 128 + r
            first = min(max(p - KW // 2, 0), TG - KW) - window_start(p // QT)
            mask[half, r, first:first + KW] = 0.0
    c["winmask"] = mask.transpose(1, 0, 2).reshape(128, -1)
    c["headmask"] = np.kron(np.ones((2, 1)), np.kron(np.eye(NH), np.ones((DH, 1))))
    v = np.zeros((128, 18))
    v[:WIN, 0:8] = v[WIN:2 * WIN, 8:16] = 1.0
    v[:WIN, 16] = v[WIN:2 * WIN, 17] = 1.0
    c["vmask"] = v
    c["rank"] = np.broadcast_to(np.arange(NE, 0, -1), (128, NE))
    pick = np.zeros((128, 2, EP, 128))
    for b in range(2):
        for part in range(2):
            for e in range(NE):
                pick[(b * 2 + part) * NE + e, b, e // 2, (e % 2) * 64:(e % 2) * 64 + 64] = 1.0
    c["pick"] = pick.reshape(128, -1)
    return np.ascontiguousarray(np.concatenate([c[n] for n, _ in CONST_PARTS], 1).astype(np.float32))


class Buffers:
    pass


def allocate(nc, ctx):
    s = Buffers()

    def sb(name, shape, dt=F32):
        return ctx.enter_context(nc.sbuf_tensor(name, shape, dt))

    s.const = sb("const", [128, CONST_COLS])
    s.h = sb("h", [128, NP, T])
    s.z = sb("z", [128, NB, T])
    s.pick = sb("pick_r", [128, 2, EP, 128], F32R)
    s.winmask = sb("winmask_b", [128, 2, NH, WIN], BF16)
    s.ident_b = sb("ident_b", [128, 128], BF16)
    s.shift = sb("shift_r", [128, T], F32R)
    s.w1s = sb("tok_w1s", [128, HID])
    s.phase = sb("tok_phase", [128, NB])
    s.tok_bias = sb("tok_bias", [128, NB])
    s.tok_w2 = sb("tok_w2", [128, D])
    s.a0_w = sb("a0_w", [128, 3, 128])
    s.a0_wp = sb("a0_wp", [128, 128])
    s.moe_wr = sb("moe_wr", [128, 128])
    s.moe_w1h = sb("moe_w1h", [128, EP, 128], F32R)
    s.moe_w1l = sb("moe_w1l", [128, EP, 128], F32R)
    s.moe_w2 = sb("moe_w2", [128, EP, D])
    s.moe_b2h = sb("moe_b2h", [128, 128], F32R)
    s.moe_b2l = sb("moe_b2l", [128, 128], F32R)
    s.combine = sb("combine", [128, NP, 4, 2 * 2 * NE], F32R)
    s.a1_qkh = sb("a1_qkh", [128, 2, 128], F32R)
    s.a1_qkl = sb("a1_qkl", [128, 2, 128], F32R)
    s.a1_wv = sb("a1_wv", [128, 128])
    s.a1_bv = sb("a1_bv", [128, 2, D])
    s.f1_wr = sb("f1_wr", [128, 128])
    s.f1_br = sb("f1_br", [128, NE])
    s.f1_w1h = sb("f1_w1h", [128, EP, 128], F32R)
    s.f1_w1l = sb("f1_w1l", [128, EP, 128], F32R)
    s.f1_w2 = sb("f1_w2", [128, EP, 128])
    s.f1_wo = sb("f1_wo", [128, EP, D])
    s.f1_wdup = sb("f1_wdup", [128, EP, 2, D])
    s.f1_w = s.z[:, NP:NP + EP, :]
    s.f1_r = s.z[:, NP + EP, :]
    s.feat = sb("feat", [128, T])
    s.bn_diag = s.feat[:].rearrange("p (e n) -> p e n", e=EP)
    raw = s.combine[:].rearrange("p a b c -> p (a b c)").bitcast(F32)
    at = 0

    def part(*shape):
        nonlocal at
        n = int(np.prod(shape))
        at += n
        return raw[:, at - n:at]

    s.raw_moe_w1, s.raw_f1_w1, s.raw_moe_b2, s.raw_a1_qk = part(NE, D), part(NE, D), part(128), part(2, 2, D)
    s.raw_bo = part(EP, D)
    s.bn_var, s.bn_scale, s.bn_shift = [part(2, EP).rearrange("p (k e) -> p k e", k=2) for _ in range(3)]
    s.loaded = ctx.enter_context(nc.semaphore("loaded"))
    s.bn_ready = ctx.enter_context(nc.semaphore("bn_ready"))
    s.eps = sb("eps", [128, 1])
    s.one = sb("one", [128, 1])
    s.cols = sb("cols", [128, 64])
    return s


COLS = {n: i for i, n in enumerate([
    "gamma", "beta", "tok_b2", "a0_bq", "a0_bk", "a0_bv", "a0_bp", "a1_bq", "a1_bk", "freq"])}
for _k, _n in enumerate(["moe_b1", "f1_b1", "f1_g1", "f1_be1", "f1_m1", "f1_v1", "f1_b2", "f1_g2", "f1_be2", "f1_m2", "f1_v2"]):
    COLS[_n] = 12 + EP * _k


def const(s, name, rows=128):
    at, n = CONST_AT[name]
    return s.const[0:rows, at:at + n]


def col(s, name, k=0):
    return s.cols[:, COLS[name] + k:COLS[name] + k + 1]


def cols4(s, name):
    return s.cols[:, COLS[name]:COLS[name] + EP]


def column(ap):
    return ap.rearrange("(p a) -> p a", a=1)


def later_loads(s, a):
    wq = a["L0_attn_w_qkv"].rearrange("d (n e) -> d n e", n=3)
    experts = lambda t, e: t.rearrange("p (e d) -> p e d", e=e)
    loads = []
    for e2 in range(2):
        n = 64 * e2
        hf = slice(n, n + 64)
        for name, src in [("tok_b2", a["L0_tok_b2"]), ("a0_bq", a["L0_attn_b_qkv"][0:D]), ("a0_bk", a["L0_attn_b_qkv"][D:2 * D]),
                          ("a0_bv", a["L0_attn_b_qkv"][2 * D:3 * D]), ("a0_bp", a["L0_attn_b_proj"]), ("a1_bq", a["L1_attn_bqkv"][0:D]),
                          ("a1_bk", a["L1_attn_bqkv"][D:2 * D])]:
            loads.append((s.cols[hf, COLS[name]:COLS[name] + 1], column(src)))
        for name, key in [("f1_v1", "L1_ffn_v1"), ("f1_v2", "L1_ffn_v2"), ("moe_b1", "L0_ffn_b1"), ("f1_b1", "L1_ffn_b1"), ("f1_g1", "L1_ffn_g1"),
                          ("f1_be1", "L1_ffn_be1"), ("f1_m1", "L1_ffn_m1"), ("f1_b2", "L1_ffn_b2"), ("f1_g2", "L1_ffn_g2"),
                          ("f1_be2", "L1_ffn_be2"), ("f1_m2", "L1_ffn_m2")]:
            loads.append((s.cols[hf, COLS[name]:COLS[name] + EP], a[key].rearrange("(p two) h -> two h p", two=2)[e2]))
        loads.append((s.a0_w[hf, :, hf], wq))
        loads.append((s.a0_wp[hf, hf], a["L0_attn_w_proj"]))
        loads.append((s.moe_wr[hf, NE * e2:NE * e2 + NE], a["L0_ffn_router_w"].rearrange("e d -> d e")))
        loads.append((experts(s.raw_moe_w1[hf, :], NE), a["L0_ffn_w1"].rearrange("e d h -> d e h")))
        loads.append((experts(s.raw_f1_w1[hf, :], NE), a["L1_ffn_W1"].rearrange("e d h -> d e h")))
        loads.append((s.a1_wv[hf, hf], a["L1_attn_Wqkv"][:, 2 * D:3 * D]))
        loads.append((s.f1_wr[hf, 0:NE], a["L1_ffn_Wr"]))
        qk = s.raw_a1_qk[hf, :].rearrange("p (n c e) -> p n c e", n=2, c=2)
        for c in range(2):
            loads.append((qk[:, :, c, :], a["L1_attn_Wqkv"][:, 0:2 * D].rearrange("d (n e) -> d n e", n=2)))
        loads.append((s.moe_w2[hf, :, :], a["L0_ffn_w2"].rearrange("(p two) h d -> two h p d", two=2)[e2]))
        loads.append((s.f1_w2[hf, :, hf], a["L1_ffn_W2"].rearrange("(p two) h d -> two h p d", two=2)[e2]))
        loads.append((s.f1_wo[hf, :, :], a["L1_ffn_Wo"].rearrange("(p two) h d -> two h p d", two=2)[e2]))
        loads.append((experts(s.raw_bo[n:n + 1, :], EP), a["L1_ffn_bo"].rearrange("(p two) d -> two p d", two=2)[e2:e2 + 1]))
        for part in range(2):
            r = (e2 * 2 + part) * NE
            loads.append((s.raw_moe_b2[r:r + NE, hf], a["L0_ffn_b2"]))
        loads.append((s.a1_bv[:, e2, :], a["L1_attn_bqkv"][2 * D:3 * D].partition_broadcast(128)))
    loads.append((s.f1_br[:], a["L1_ffn_br"].partition_broadcast(128)))
    return loads


def prepare(nc, s, a):
    with ExitStack() as ctx:
        def sb(name, shape, dt=F32):
            return ctx.enter_context(nc.sbuf_tensor(name, shape, dt))

        def sem(name):
            return ctx.enter_context(nc.semaphore(name))

        x_in = sb("x_in", [NB, T], I32)
        signal = sb("signal", [NB, T])
        signal_t = sb("signal_t", [128, 4, NB])
        spec = sb("spec", [NB, 2, NF])
        spec_sq = sb("spec_sq", [NB, 2, NF])
        power = sb("power", [NB, NF])
        is_zero = sb("is_zero", [NB, NF])
        mag = sb("mag", [NB, NF])
        inv = sb("inv", [NB, NF])
        sincos = sb("sincos", [NB, 4, NF])
        mag_t = sb("mag_t", [NF + 1, NB])
        w1m = sb("w1m", [NF + 1, HID])
        rowsum = sb("rowsum", [128, 2])
        ps = [ctx.enter_context(nc.psum_tensor(f"prep_ps{n}", [128, 512], F32)) for n in range(5)]

        zeroed, x_loaded, const_loaded, w1_loaded = sem("zeroed"), sem("x_loaded"), sem("const_loaded"), sem("w1_loaded")
        other_loaded = sem("other_loaded")
        dve, act, pe = sem("prep_dve"), sem("prep_act"), sem("prep_pe")
        block = ctx.enter_context(nc.Block())
        w1 = a["L0_tok_w1"]
        SIGNAL, SIGNAL_T, POWER, SINCOS, MAG_T = 1, 11, 17, 22, 24
        w1_loads = [(w1m[0:NF, :], w1[0:NF, :]), (w1m[NF:NF + 1, :], a["L0_tok_b1"].rearrange("(p n) -> p n", p=1))]
        w1_loads += [(s.w1s[32 * n:32 * n + 32, :], w1[NF:D, :]) for n in range(4)]
        w1_loads += [(s.cols[0:NF, COLS["freq"]:COLS["freq"] + 1], column(a["L0_tok_freq_bands"]))]
        others = [(s.const[:, FIRST_CONST:], a["const"][:, FIRST_CONST:]), (col(s, "gamma"), column(a["L0_tok_gamma"])),
                  (col(s, "beta"), column(a["L0_tok_beta"])), (s.tok_w2[:], a["L0_tok_w2"])]
        cleared = [s.cols, s.a0_w, s.a0_wp, s.moe_wr, s.a1_wv, s.f1_wr, s.f1_w2, s.combine]

        @block.gpsimd
        def _(pool):
            for t in cleared:
                view = t[:] if t is not s.combine else s.combine[:].rearrange("p a b c -> p (a b c)").bitcast(F32)
                nc.gpsimd.memset(view, 0.0).then_inc(zeroed, 1)
            pool.wait_ge(zeroed, len(cleared))

        @block.sync
        def _(sp):
            sp.dma_start(x_in[:], a["x"]).then_inc(x_loaded, 16)
            for dst, src in w1_loads[:-1]:
                sp.dma_start(dst, src).then_inc(w1_loaded, 16)
            sp.wait_ge(other_loaded, 16 * len(others))

        @block.scalar
        def _(sc):
            sc.dma_start(s.const[:, 0:FIRST_CONST], a["const"][:, 0:FIRST_CONST]).then_inc(const_loaded, 16)
            sc.wait_ge(zeroed, 1)
            for dst, src in w1_loads[-1:]:
                sc.dma_start(dst, src, allow_slow_non_contiguous=True).then_inc(w1_loaded, 16)
            for dst, src in others:
                sc.dma_start(dst, src, allow_slow_non_contiguous=True).then_inc(other_loaded, 16)
            sc.preload_act_table_set("sqrt_and_others")
            sc.wait_ge(dve, POWER)
            nc.scalar.activation(mag[:], power[:], ACT.Sqrt).then_inc(act, 1)

        @block.tensor
        def _(te):
            te.wait_ge(const_loaded, 16)
            te.wait_ge(dve, SIGNAL)
            for c in range(4):
                nc.tensor.transpose(ps[0][:, c * NB:(c + 1) * NB], signal[:, c * 128:(c + 1) * 128],
                                    const(s, "ident", NB)[:, 0:NB]).then_inc(pe, 1)
            te.wait_ge(dve, SIGNAL_T)
            dft = const(s, "dft").rearrange("p (c n) -> p c n", c=4)
            for c in range(4):
                nc.tensor.matmul(ps[1][0:NB, 0:2 * NF], signal_t[:, c, :], dft[:, c, :],
                                 start=(c == 0), stop=(c == 3)).then_inc(pe, 1)
            te.wait_ge(dve, SINCOS)
            nc.tensor.transpose(ps[2][:, 0:NB], sincos[:].rearrange("p a b -> p (a b)"),
                                const(s, "ident", NB)[:, 0:NB]).then_inc(pe, 1)
            nc.tensor.transpose(ps[3][0:NF, 0:NB], mag[:], const(s, "ident", NB)[:, 0:NB]).then_inc(pe, 1)
            te.wait_ge(dve, MAG_T)
            nc.tensor.matmul(ps[4][:, 0:NB], w1m[:], mag_t[:], start=True, stop=True).then_inc(pe, 1)

        @block.vector
        def _(ve):
            n = [0]

            def step(ins):
                ins.then_inc(dve, 1)
                n[0] += 1
                ve.wait_ge(dve, n[0])

            v = nc.vector
            up = slice(64, 128)
            ve.wait_ge(x_loaded, 16)
            step(v.tensor_scalar(signal[:], x_in[:], 1.0 / 127.5, -1.0, ALU.mult, ALU.add))
            assert n[0] == SIGNAL
            step(v.memset(mag_t[:], 1.0))
            step(v.memset(s.eps[:], LN_EPS))
            step(v.memset(s.one[:], 1.0))
            ve.wait_ge(w1_loaded, 16 * len(w1_loads))
            step(v.tensor_reduce(rowsum[:, 0:1], s.w1s[:], AX, ALU.add))
            step(v.tensor_reduce(rowsum[0:NF + 1, 1:2], w1m[:], AX, ALU.add))
            step(v.tensor_scalar(rowsum[:, 0:1], rowsum[:, 0:1], 1.0 / HID, None, ALU.mult))
            step(v.tensor_scalar(rowsum[0:NF + 1, 1:2], rowsum[0:NF + 1, 1:2], 1.0 / HID, None, ALU.mult))
            step(v.tensor_scalar(s.w1s[:], s.w1s[:], rowsum[:, 0:1], None, ALU.subtract))
            step(v.tensor_scalar(w1m[:], w1m[:], rowsum[0:NF + 1, 1:2], None, ALU.subtract))
            ve.wait_ge(pe, 4)
            step(v.tensor_copy(signal_t[:].rearrange("p c b -> p (c b)"), ps[0][:, 0:4 * NB]))
            assert n[0] == SIGNAL_T
            ve.wait_ge(pe, 8)
            step(v.tensor_copy(spec[:].rearrange("p a b -> p (a b)"), ps[1][0:NB, 0:2 * NF]))
            re, im = spec[:, 0, :], spec[:, 1, :]
            step(v.tensor_tensor(spec_sq[:], spec[:], spec[:], ALU.mult))
            step(v.tensor_tensor(power[:], spec_sq[:, 0, :], spec_sq[:, 1, :], ALU.add))
            step(v.tensor_scalar(is_zero[:], power[:], 0.0, None, ALU.is_equal))
            step(v.tensor_tensor(re, re, is_zero[:], ALU.add))
            step(v.tensor_tensor(power[:], power[:], is_zero[:], ALU.add))
            assert n[0] == POWER
            step(v.tensor_copy(s.shift[:], const(s, "shift")))
            ve.wait_ge(act, 1)
            step(v.reciprocal(inv[:], mag[:]))
            step(v.tensor_tensor(sincos[:, 0::2, :], im.unsqueeze(1).broadcast_to([NB, 2, NF]),
                                 inv[:].unsqueeze(1).broadcast_to([NB, 2, NF]), ALU.mult))
            step(v.tensor_tensor(sincos[:, 1::2, :], re.unsqueeze(1).broadcast_to([NB, 2, NF]),
                                 inv[:].unsqueeze(1).broadcast_to([NB, 2, NF]), ALU.mult))
            step(v.tensor_tensor(mag[:], mag[:], is_zero[:], ALU.subtract))
            assert n[0] == SINCOS
            ve.wait_ge(pe, 9)
            step(v.tensor_copy(s.phase[:], ps[2][:, 0:NB]))
            ve.wait_ge(pe, 10)
            step(v.tensor_scalar(mag_t[0:NF, :], ps[3][0:NF, 0:NB], s.cols[0:NF, COLS["freq"]:COLS["freq"] + 1], None, ALU.mult))
            assert n[0] == MAG_T
            step(v.tensor_tensor(s.shift[up, :], const(s, "shift")[up, :], s.shift[up, :].bitcast(F32), ALU.subtract))
            ve.wait_ge(pe, 11)
            step(v.tensor_copy(s.tok_bias[:], ps[4][:, 0:NB]))


def derive_weights(nc, s, step):
    p = nc.gpsimd

    def product(out, x, y, op=ALU.mult):
        step(p.tensor_tensor(out, x, y, op))

    def split(high, low, whole):
        step(p.tensor_copy(high, whole))
        product(low, whole, high.bitcast(F32), ALU.subtract)

    def flat(t):
        return t[:].rearrange("p a b -> p (a b)")

    product(s.bn_shift, s.bn_scale, s.bn_scale)
    product(s.bn_shift, s.bn_shift, s.bn_var)
    step(p.tensor_scalar(s.bn_shift, s.bn_shift, -0.5, 1.5, ALU.mult, ALU.add))
    product(s.bn_scale, s.bn_scale, s.bn_shift)
    for k in range(2):
        m = f"{k + 1}"
        product(cols4(s, "f1_g" + m), cols4(s, "f1_g" + m), s.bn_scale[:, k, :])
        product(s.bn_shift[:, k, :], cols4(s, "f1_b" + m), cols4(s, "f1_m" + m), ALU.subtract)
        product(s.bn_shift[:, k, :], s.bn_shift[:, k, :], cols4(s, "f1_g" + m))
        product(cols4(s, "f1_be" + m), cols4(s, "f1_be" + m), s.bn_shift[:, k, :], ALU.add)
    product(s.bn_diag, const(s, "ident").unsqueeze(1).broadcast_to([128, EP, 128]), cols4(s, "f1_g2").unsqueeze(2).broadcast_to([128, EP, 128]))
    for c in range(2):
        product(s.f1_wdup[:, :, c, :], s.f1_wo[:], cols4(s, "f1_be2").unsqueeze(2).broadcast_to([128, EP, D]))
        product(s.f1_wdup[:, :, c, :], s.f1_wdup[:, :, c, :], s.raw_bo.rearrange("p (e d) -> p e d", e=EP), ALU.add)
    step(p.tensor_scalar(cols4(s, "f1_be2"), cols4(s, "f1_be2"), -1.0, None, ALU.mult))
    wm = const(s, "winmask").rearrange("p (a w) -> p a w", a=2)
    for hf in range(2):
        step(p.tensor_copy(s.winmask[:, hf, :, :], wm[:, hf, :].unsqueeze(1).broadcast_to([128, NH, WIN])))
    step(p.tensor_copy(s.ident_b[:], const(s, "ident")))
    split(flat(s.moe_w1h), flat(s.moe_w1l), s.raw_moe_w1)
    split(s.moe_b2h[:], s.moe_b2l[:], s.raw_moe_b2)
    split(flat(s.a1_qkh), flat(s.a1_qkl), s.raw_a1_qk)
    split(flat(s.f1_w1h), flat(s.f1_w1l), s.raw_f1_w1)
    step(p.tensor_copy(s.pick[:].rearrange("p a b c -> p (a b c)"), const(s, "pick")))


BN_DIAG = 13


CREDITS = 16


def done(n):
    return n + (1 + CREDITS)


def give_credits(eng, *semaphores):
    for sem in semaphores:
        eng.sem_inc(sem, CREDITS)


def row(t, n):
    return t[:, bass.ds(n, 1), :].rearrange("p a b -> p (a b)")


class Step:

    def __init__(self, turn, offset, unroll):
        self.turn, self.offset, self.unroll = turn, offset, unroll
        self.n = turn * unroll + offset
        self.k = offset % unroll

    def of(self, size):
        return self.turn * (self.unroll // size) + self.offset // size


def staggered(eng, count, unroll, *stages):
    most = max(lead for lead, _ in stages)
    for n in range(-most, 0):
        for lead, stage in stages:
            if n + lead >= 0:
                stage(Step(0, n + lead, unroll))
    turns = count // unroll - 1
    with eng.Fori(0, turns) as turn:
        for k in range(unroll):
            for lead, stage in stages:
                stage(Step(turn, k + lead, unroll))
    for k in range(unroll):
        for lead, stage in stages:
            if k + lead < unroll:
                stage(Step(turns, k + lead, unroll))


def pool_copy(nc, s, out, in_):
    ones = s.one[:] if len(in_.shape) == 2 else s.one[:].unsqueeze(2)
    return nc.gpsimd.tensor_tensor(out, in_, ones.broadcast_to(in_.shape), ALU.mult)


def spectral_norm(nc, s, a):
    with ExitStack() as ctx:
        def sb(name, shape, dt=F32):
            return [ctx.enter_context(nc.sbuf_tensor(f"sn_{name}{k}", shape, dt)) for k in range(4)]

        def ps(name):
            return [ctx.enter_context(nc.psum_tensor(f"sn_{name}{k}", [128, T], F32)) for k in range(4)]

        def sem(name):
            return ctx.enter_context(nc.semaphore("sn_" + name))

        loads = later_loads(s, a)
        wh, wl = sb("wh", [128, HID], F32R), sb("wl", [128, HID], F32R)
        sq, ln, rstd = sb("sq", [128, T]), sb("ln", [128, T]), sb("rstd", [128, T])
        hid, var = ps("hid"), ps("var")
        s_wh, s_wl, s_hid, s_sq, s_var, s_ln, s_rstd, s_z = [sem(x) for x in ("wh", "wl", "hid", "sq", "var", "ln", "rstd", "z")]
        block = ctx.enter_context(nc.Block())

        @block.gpsimd
        def _(pool):
            give_credits(pool, s_wh)

            def weights(at):
                n, k = at.n, at.k
                phase = s.phase[:, bass.ds(n, 1)]
                pool.wait_ge(s_wl, done(n - 4))
                pool.wait_ge(s_hid, done(n - 4))
                nc.gpsimd.tensor_tensor(wh[k][:], s.w1s[:], phase.broadcast_to([128, HID]), ALU.mult).then_inc(s_wh, 1)

            staggered(nc.gpsimd, NB, 4, (0, weights))
            pool.wait_ge(s.loaded, 16 * len(loads))
            nc.gpsimd.tensor_scalar(s.bn_var[:, 0, :], cols4(s, "f1_v1"), BN_EPS, None, ALU.add).then_inc(s.bn_ready, 1)
            nc.gpsimd.tensor_scalar(s.bn_var[:, 1, :], cols4(s, "f1_v2"), BN_EPS, None, ALU.add).then_inc(s.bn_ready, 1)

        @block.sync
        def _(sp):
            for dst, src in loads:
                sp.dma_start(dst, src, allow_slow_non_contiguous=True).then_inc(s.loaded, 16)

        @block.tensor
        def _(te):
            give_credits(te, s_hid, s_var)

            def hidden(at):
                n, k = at.n, at.k
                te.wait_ge(s_wl, done(n))
                te.wait_ge(s_z, done(n - 4))
                nc.tensor.matmul(hid[k][:], wh[k][:], s.shift[:], start=True, stop=False)
                nc.tensor.matmul(hid[k][:], wl[k][:], s.shift[:], start=False, stop=True).then_inc(s_hid, 1)

            def variance(at):
                n, k = at.n, at.k
                te.wait_ge(s_sq, done(n))
                te.wait_ge(s_ln, done(n - 4))
                nc.tensor.matmul(var[k][:], const(s, "mean128"), sq[k][:], start=True, stop=True).then_inc(s_var, 1)

            staggered(nc.tensor, NB, 4, (1, variance), (3, hidden))

        @block.scalar
        def _(sc):
            sc.preload_act_table_set("natural_log_exp_and_others")
            give_credits(sc, s_sq, s_ln, s_rstd)

            def squares(at):
                n, k = at.n, at.k
                sc.wait_ge(s_hid, done(n))
                sc.wait_ge(s_var, done(n - 4))
                nc.scalar.activation(sq[k][:], hid[k][:], ACT.Square, bias=s.tok_bias[:, bass.ds(n, 1)]).then_inc(s_sq, 1)

            def logarithm(at):
                n, k = at.n, at.k
                sc.wait_ge(s_var, done(n))
                sc.wait_ge(s_rstd, done(n - 4))
                nc.scalar.activation(ln[k][:], var[k][:], ACT.Ln, bias=s.eps[:]).then_inc(s_ln, 1)

            def root(at):
                n, k = at.n, at.k
                sc.wait_ge(s_ln, done(n))
                sc.wait_ge(s_z, done(n - 4))
                nc.scalar.activation(rstd[k][:], ln[k][:], ACT.Exp, scale=-0.5).then_inc(s_rstd, 1)

            staggered(nc.scalar, NB, 4, (2, squares), (1, logarithm), (0, root))
            sc.wait_ge(s.bn_ready, 2)
            nc.scalar.activation(s.bn_scale, s.bn_var, ACT.Ln).then_inc(s.bn_ready, 1)
            sc.wait_ge(s.bn_ready, 3)
            nc.scalar.activation(s.bn_scale, s.bn_scale, ACT.Exp, scale=-0.5).then_inc(s.bn_ready, 1)

        @block.vector
        def _(ve):
            give_credits(ve, s_z, s_wl)

            def low(at):
                n, k = at.n, at.k
                ve.wait_ge(s_wh, done(n))
                ve.wait_ge(s_hid, done(n - 4))
                nc.vector.scalar_tensor_tensor(out=wl[k][:], in0=s.w1s[:], scalar=s.phase[:, bass.ds(n, 1)], in1=wh[k][:].bitcast(F32),
                                               op0=ALU.mult, op1=ALU.subtract).then_inc(s_wl, 1)

            def normalise(at):
                n, k = at.n, at.k
                ve.wait_ge(s_rstd, done(n))
                nc.vector.scalar_tensor_tensor(out=row(s.z, n), in0=hid[k][:], scalar=s.tok_bias[:, bass.ds(n, 1)],
                                               in1=rstd[k][:], op0=ALU.add, op1=ALU.mult).then_inc(s_z, 1)

            staggered(nc.vector, NB, 4, (4, low), (0, normalise))


def tokenizer_output(nc, s):
    with ExitStack() as ctx:
        g = [ctx.enter_context(nc.sbuf_tensor(f"to_g{k}", [128, 2, T], F32)) for k in range(4)]
        y = [ctx.enter_context(nc.psum_tensor(f"to_y{k}", [128, T], F32)) for k in range(4)]
        p_scale, p_bias = [ctx.enter_context(nc.psum_tensor("to_" + x, [128, 512], F32)) for x in ("scale", "bias")]
        s_g, s_y, s_h, s_derived, s_last, s_scaled = [ctx.enter_context(nc.semaphore("to_" + x)) for x in ("g", "y", "h", "derived", "last", "scaled")]
        block = ctx.enter_context(nc.Block())

        @block.scalar
        def _(sc):
            give_credits(sc, s_g)

            def gelu(at):
                sc.wait_ge(s_y, done(at.n - 4))
                nc.scalar.activation(g[at.k][:], s.z[:, bass.ds(at.n * 2, 2), :], ACT.Gelu, scale=col(s, "gamma"),
                                     bias=col(s, "beta")).then_inc(s_g, 1)

            staggered(nc.scalar, NP, 4, (0, gelu))

        @block.gpsimd
        def _(pool):
            n = [0]

            def step(ins):
                ins.then_inc(s_derived, 1)
                n[0] += 1
                pool.wait_ge(s_derived, n[0])

            derive_weights(nc, s, step)

        @block.tensor
        def _(te):
            give_credits(te, s_y)

            def product(at):
                te.wait_ge(s_g, done(at.n))
                te.wait_ge(s_h, done(at.n - 4))
                nc.tensor.matmul(y[at.k][0:64, :], s.tok_w2[:], g[at.k][:, 0, :], start=True, stop=True)
                nc.tensor.matmul(y[at.k][64:128, :], s.tok_w2[:], g[at.k][:, 1, :], start=True, stop=True).then_inc(s_y, 1)

            staggered(nc.tensor, NP, 4, (0, product))
            nc.tensor.matmul(p_bias[:, 0:1], s.a0_wp[:], col(s, "a0_bv"), start=True, stop=True).then_inc(s_last, 1)
            te.wait_ge(s_derived, BN_DIAG)
            nc.tensor.matmul(p_scale[:], const(s, "mean128"), s.feat[:], start=True, stop=True).then_inc(s_last, 1)

        @block.vector
        def _(ve):
            give_credits(ve, s_h)

            def bias(at):
                ve.wait_ge(s_y, done(at.n))
                nc.vector.tensor_scalar(row(s.h, at.n), y[at.k][:], col(s, "tok_b2"), None, ALU.add).then_inc(s_h, 1)

            staggered(nc.vector, NP, 4, (0, bias))
            ve.wait_ge(s_last, 1)
            nc.vector.tensor_tensor(col(s, "a0_bp"), p_bias[:, 0:1], col(s, "a0_bp"), ALU.add)
            ve.wait_ge(s_last, 2)
            w2 = s.f1_w2[:].rearrange("p a b -> p (a b)")
            nc.vector.scalar_tensor_tensor(out=w2, in0=p_scale[:], scalar=float(HID), in1=w2, op0=ALU.mult, op1=ALU.mult)
            nc.vector.memset(s.feat[:], 0.0).then_inc(s_scaled, 1)
            ve.wait_ge(s_scaled, 1)


def layer_norm(nc, s, tag, features=False):
    with ExitStack() as ctx:
        def sb(name):
            return [ctx.enter_context(nc.sbuf_tensor(f"{tag}_{name}{k}", [128, T], F32)) for k in range(4)]

        sq, ln, rstd = sb("sq"), sb("ln"), sb("rstd")
        cen, var = [[ctx.enter_context(nc.psum_tensor(f"{tag}_{x}{k}", [128, T], F32)) for k in range(4)] for x in ("cen", "var")]
        s_cen, s_sq, s_var, s_ln, s_rstd, s_z, s_feat = [ctx.enter_context(nc.semaphore(f"{tag}_s_{x}"))
                                                         for x in ("cen", "sq", "var", "ln", "rstd", "z", "feat")]
        block = ctx.enter_context(nc.Block())

        @block.tensor
        def _(te):
            give_credits(te, s_cen, s_var)

            def centre(at):
                te.wait_ge(s_z, done(at.n - 4))
                nc.tensor.matmul(cen[at.k][:], const(s, "center"), row(s.h, at.n), start=True, stop=True).then_inc(s_cen, 1)

            def variance(at):
                te.wait_ge(s_sq, done(at.n))
                te.wait_ge(s_ln, done(at.n - 4))
                nc.tensor.matmul(var[at.k][:], const(s, "mean64"), sq[at.k][:], start=True, stop=True).then_inc(s_var, 1)

            staggered(nc.tensor, NP, 4, (1, variance), (3, centre))

        @block.scalar
        def _(sc):
            sc.preload_act_table_set("natural_log_exp_and_others")
            give_credits(sc, s_sq, s_ln, s_rstd)

            def squares(at):
                sc.wait_ge(s_cen, done(at.n))
                sc.wait_ge(s_var, done(at.n - 4))
                nc.scalar.activation(sq[at.k][:], cen[at.k][:], ACT.Square).then_inc(s_sq, 1)

            def logarithm(at):
                sc.wait_ge(s_var, done(at.n))
                sc.wait_ge(s_rstd, done(at.n - 4))
                nc.scalar.activation(ln[at.k][:], var[at.k][:], ACT.Ln, bias=s.eps[:]).then_inc(s_ln, 1)

            def root(at):
                sc.wait_ge(s_ln, done(at.n))
                sc.wait_ge(s_z, done(at.n - 4))
                nc.scalar.activation(rstd[at.k][:], ln[at.k][:], ACT.Exp, scale=-0.5).then_inc(s_rstd, 1)

            staggered(nc.scalar, NP, 4, (2, squares), (1, logarithm), (0, root))

        @block.vector
        def _(ve):
            give_credits(ve, s_z)

            def normalise(at):
                ve.wait_ge(s_rstd, done(at.n))
                nc.vector.tensor_tensor(row(s.z, at.n), cen[at.k][:], rstd[at.k][:], ALU.mult).then_inc(s_z, 1)

            staggered(nc.vector, NP, 4, (0, normalise))

        @block.gpsimd
        def _(pool):
            if features:
                give_credits(pool, s_feat)

                def add(at):
                    pool.wait_ge(s_z, done(at.n))
                    pool.wait_ge(s_feat, done(at.n - 1))
                    nc.gpsimd.tensor_tensor(s.feat[:], s.feat[:], row(s.z, at.n), ALU.add).then_inc(s_feat, 1)

                staggered(nc.gpsimd, NP, 4, (0, add))


def neighbourhood_attention(nc, s):
    with ExitStack() as ctx:
        def sb(name, shape, dt=F32, n=2):
            return [ctx.enter_context(nc.sbuf_tensor(f"na_{name}{k}", shape, dt)) for k in range(n)]

        def ps(name, n=1):
            return [ctx.enter_context(nc.psum_tensor(f"na_{name}{k}", [128, 512], F32)) for k in range(n)]

        def sem(name):
            return ctx.enter_context(nc.semaphore("na_" + name))

        zt = sb("zt", [128, T])
        q = sb("q", [128, 2, 2, TG])
        kk = sb("k", [128, 2, TG])
        kblk = [s.z[:, NP + NH * k:NP + NH * k + NH, :].rearrange("p h (two t) -> p h two t", two=2) for k in range(2)]
        v = sb("v", [128, 2 * NT, 2, NH // 2, 18])
        diff, e = sb("diff", [128, NH * WIN]), sb("e", [128, NH * WIN])
        rowmax = sb("rowmax", [128, NH])
        et = sb("et", [128, NH // 2, 128])
        rden = sb("rden", [128, NH // 2, 2])
        on = sb("on", [128, 2, D])
        ot = sb("ot", [128, 2, TG])
        p_s, p_t, p_o, p_prep, p_out = ps("ps", 2), ps("pt", 2), ps("po", 2), ps("pprep")[0], ps("pout")[0]
        p_ot = p_out
        s_zt, s_prep, s_prepd, s_k, s_score, s_max, s_diff, s_e, s_et, s_etd, s_o, s_rden, s_on, s_ot, s_otd, s_out, s_h, s_zero = [
            sem(x) for x in ("zt", "prep", "prepd", "k", "score", "max", "diff", "e", "et", "etd", "o", "rden", "on", "ot", "otd", "out", "h", "zero")]
        block = ctx.enter_context(nc.Block())
        PREP = 4

        def group(at):
            g = at.k % 8
            return g // 4, g // 2 % 2, g % 2

        def product(i, part):
            return i * PREP + part

        @block.gpsimd
        def _(pool):
            for t in q:
                nc.gpsimd.memset(t[:], 0.0).then_inc(s_zero, 1)
            for t in v:
                nc.gpsimd.memset(t[:], 0.0).then_inc(s_zero, 1)
            pool.wait_ge(s_zero, 4)
            for t in v:
                nc.gpsimd.tensor_tensor(t[:, :, :, :, 16:18].rearrange("p a b c d -> p (a b c) d"),
                                        t[:, :, :, :, 16:18].rearrange("p a b c d -> p (a b c) d"),
                                        const(s, "vmask")[:, 16:18].unsqueeze(1).broadcast_to([128, 2 * NT * NH, 2]), ALU.add).then_inc(s_zero, 1)
            give_credits(pool, s_zt)

            def copy(at):
                if at.k % 8 == 0:
                    i = at.of(8)
                    pool.wait_ge(s_prep, done(product(i - 2, PREP - 1)))
                    pool_copy(nc, s, zt[at.k // 8][:], row(s.z, i)).then_inc(s_zt, 1)

            staggered(nc.gpsimd, 8 * NP, 16, (0, copy))

        @block.tensor
        def _(te):
            give_credits(te, s_prep, s_score, s_et, s_o, s_ot, s_out)
            te.wait_ge(s_zero, 6)

            def prepare_pair(at):
                if at.k % 2:
                    return
                part, b = at.k // 2 % PREP, at.k // 8
                i = at.of(8)
                if part == 0:
                    te.wait_ge(s_zt, done(i))
                te.wait_ge(s_prepd, done(product(i, part) - 1))
                bank = p_prep
                if part < 2:
                    mm = nc.tensor.matmul(bank[:], s.a0_w[:, 1 - part, :], zt[b][:], start=True, stop=True)
                else:
                    for c in range(4):
                        for half in range(2):
                            first = part - 2 + DIL * window_start(4 * half + c)
                            window = zt[b][:, first:first + DIL * (WIN - 1) + 1:DIL]
                            mm = nc.tensor.matmul(bank[WIN * half:WIN * half + WIN, c * 128:c * 128 + 128], window, s.a0_w[:, 2, :],
                                                  start=True, stop=True, skip_group_check=True)
                mm.then_inc(s_prep, 1)

            def scores(at):
                par, half, b = group(at)
                te.wait_ge(s_diff, done(at.n - 2))
                if at.k % 8 == 0:
                    te.wait_ge(s_k, done(at.of(8)))
                bank = p_s[at.k % 2]
                nc.tensor.matmul(bank[:, 0:NH * WIN], s.ident_b[:], s.winmask[:, half, :, :], start=True, stop=False, skip_group_check=True)
                for c in range(4):
                    t = 4 * half + c
                    w = window_start(t)
                    mm = nc.tensor.matmul(bank[QT * c:QT * c + QT, 0:NH * WIN], q[at.k // 8][:, b, par, t * QT:t * QT + QT],
                                          kblk[at.k // 8][:, :, par, w:w + WIN], start=False, stop=True, skip_group_check=True)
                mm.then_inc(s_score, 1)

            def transposes(at):
                te.wait_ge(s_e, done(at.n))
                te.wait_ge(s_etd, done(at.n - 2))
                for c in range(NH // 2):
                    mm = nc.tensor.transpose(p_t[at.k % 2][0:2 * WIN, c * 128:c * 128 + 128],
                                             e[at.k % 2][:, c * 2 * WIN:(c + 1) * 2 * WIN], const(s, "ident"))
                mm.then_inc(s_et, 1)

            def values(at):
                par, half, b = group(at)
                te.wait_ge(s_etd, done(at.n))
                te.wait_ge(s_on, done(at.n - 2))
                for c in range(NH // 2):
                    for t in range(4):
                        mm = nc.tensor.matmul(p_o[at.k % 2][QT * t:QT * t + QT, c * 18:c * 18 + 18], et[at.k % 2][0:2 * WIN, c, QT * t:QT * t + QT],
                                              v[at.k // 8][0:2 * WIN, par * NT + 4 * half + t, b, c, :], start=True, stop=True)
                mm.then_inc(s_o, 1)

            def turn(at):
                if at.k % 2 == 1:
                    te.wait_ge(s_on, done(at.n))
                    te.wait_ge(s_otd, done(at.of(2) - 1))
                    if at.k % 8 == 1:
                        te.wait_ge(s_h, done(at.of(8) - 1))
                    nc.tensor.transpose(p_ot[:, 0:128], on[at.k // 2 % 2][:].rearrange("p a b -> p (a b)"), const(s, "ident")).then_inc(s_ot, 1)

            def project(at):
                if at.k % 8 == 7:
                    i = at.of(8)
                    te.wait_ge(s_otd, done(at.of(2)))
                    nc.tensor.matmul(p_out[:], s.a0_wp[:], ot[at.k // 8][:].rearrange("p a b -> p (a b)"), start=True, stop=True).then_inc(s_out, 1)

            staggered(nc.tensor, 8 * NP, 16, (9, scores), (6, transposes), (4, values), (1, project), (2, turn), (16, prepare_pair))

        @block.scalar
        def _(sc):
            sc.preload_act_table_set("natural_log_exp_and_others")
            give_credits(sc, s_e, s_etd, s_otd, s_prepd)
            sc.wait_ge(s_zero, 6)

            def fetch_prepared(at):
                if at.k % 2:
                    return
                part, i, k = at.k // 2 % PREP, at.of(8), at.k // 8
                bank = p_prep
                sc.wait_ge(s_prep, done(product(i, part)))
                if part == 0:
                    sc.wait_ge(s_k, done(i - 2))
                    ins = nc.scalar.activation(kk[k][:], bank[:].rearrange("p (t two) -> p two t", two=2), ACT.Identity, bias=col(s, "a0_bk"))
                elif part == 1:
                    sc.wait_ge(s_score, done(i * 8 - 9))
                    for b in range(2):
                        half = slice(64 * b, 64 * b + 64)
                        ins = nc.scalar.activation(q[k][half, b, :, :], bank[half, :].rearrange("p (t two) -> p two t", two=2), ACT.Identity,
                                                   bias=s.cols[half, COLS["a0_bq"]:COLS["a0_bq"] + 1])
                else:
                    if part == 2:
                        sc.wait_ge(s_o, done(i * 8 - 9))
                    for half in range(2):
                        first = (part - 2) * NT + 4 * half
                        for head in range(2):
                            values = bank[WIN * half:WIN * half + WIN, :].rearrange("p (a d) -> p a d", d=2 * DH)[:, :, DH * head:DH * head + DH]
                            out = v[k][WIN * head:WIN * head + WIN, first:first + 4, :, :, DH * head:DH * head + DH]
                            ins = nc.scalar.activation(out.rearrange("p a b c d -> p (a b c) d"), values, ACT.Copy)
                ins.then_inc(s_prepd, 1)

            def exponential(at):
                sc.wait_ge(s_diff, done(at.n))
                sc.wait_ge(s_et, done(at.n - 2))
                nc.scalar.activation(e[at.k % 2][:], diff[at.k % 2][:], ACT.Exp, scale=float(DH) ** -0.5).then_inc(s_e, 1)

            def fetch(at):
                sc.wait_ge(s_et, done(at.n))
                sc.wait_ge(s_o, done(at.n - 2))
                nc.scalar.activation(et[at.k % 2][0:2 * WIN, :, :].rearrange("p a b -> p (a b)"), p_t[at.k % 2][0:2 * WIN, :], ACT.Copy).then_inc(s_etd, 1)

            def fetch_output(at):
                if at.k % 2 == 1:
                    par, half, _ = group(at)
                    sc.wait_ge(s_ot, done(at.of(2)))
                    if at.k % 8 == 1:
                        sc.wait_ge(s_out, done(at.of(8) - 2))
                    nc.scalar.activation(ot[at.k // 8][:, par, half * 128:half * 128 + 128], p_ot[:, 0:128], ACT.Copy).then_inc(s_otd, 1)

            staggered(nc.scalar, 8 * NP, 16, (7, exponential), (5, fetch), (1, fetch_output), (15, fetch_prepared))

        @block.vector
        def _(ve):
            give_credits(ve, s_max, s_diff, s_k, s_rden, s_on, s_h)
            ve.wait_ge(s_zero, 6)

            def keys_by_head(at):
                part, i, b = at.k % 8, at.of(8), at.k // 8
                if 2 <= part < 6:
                    if part == 2:
                        ve.wait_ge(s_prepd, done(product(i, 0)))
                        ve.wait_ge(s_score, done(i * 8 - 9))
                    for h in (2 * part - 4, 2 * part - 3):
                        ins = nc.vector.tensor_scalar(kblk[b][:, h, :, :], kk[b][:], const(s, "headmask")[:, h:h + 1], None, ALU.mult)
                    if part == 5:
                        ins.then_inc(s_k, 1)

            def maximum(at):
                ve.wait_ge(s_score, done(at.n))
                sc_ = p_s[at.k % 2][:, 0:NH * WIN].rearrange("p (h w) -> p h w", h=NH)
                nc.vector.tensor_reduce(rowmax[at.k % 2][:], sc_, AX, ALU.max).then_inc(s_max, 1)
                ve.wait_ge(s_max, done(at.n))
                ve.wait_ge(s_e, done(at.n - 2))
                nc.vector.tensor_tensor(diff[at.k % 2][:].rearrange("p (h w) -> p h w", h=NH), sc_,
                                        rowmax[at.k % 2][:].unsqueeze(2).broadcast_to([128, NH, WIN]), ALU.subtract).then_inc(s_diff, 1)

            def normalise(at):
                _, _, b = group(at)
                ve.wait_ge(s_o, done(at.n))
                o = p_o[at.k % 2][:, 0:72].rearrange("p (c d) -> p c d", c=NH // 2)
                nc.vector.reciprocal(rden[at.k % 2][:], o[:, :, 16:18]).then_inc(s_rden, 1)
                ve.wait_ge(s_rden, done(at.n))
                ve.wait_ge(s_ot, done(at.of(2) - 2))
                nc.vector.tensor_tensor(on[at.k // 2 % 2][:, b, :].rearrange("p (c h d) -> p c h d", c=NH // 2, h=2),
                                        o[:, :, 0:16].rearrange("p c (h d) -> p c h d", h=2),
                                        rden[at.k % 2][:].unsqueeze(3).broadcast_to([128, NH // 2, 2, DH]), ALU.mult).then_inc(s_on, 1)

            def residual(at):
                if at.k % 8 == 7:
                    i = at.of(8)
                    ve.wait_ge(s_out, done(i))
                    h = row(s.h, i).rearrange("p (t two) -> p two t", two=2)
                    nc.vector.scalar_tensor_tensor(out=h, in0=p_out[:].rearrange("p (two t) -> p two t", two=2), scalar=col(s, "a0_bp"),
                                                   in1=h, op0=ALU.add, op1=ALU.add).then_inc(s_h, 1)

            staggered(nc.vector, 8 * NP, 16, (8, maximum), (3, normalise), (1, residual), (15, keys_by_head))


def route(nc, s):
    with ExitStack() as ctx:
        def sb(name, shape, dt=F32):
            return ctx.enter_context(nc.sbuf_tensor("ro_" + name, shape, dt))

        groups = NP * 4 * 2
        zt = [sb(f"zt{k}", [128, T]) for k in range(4)]
        logits, best, masked, picked, other = [sb(x, [128, groups, NE]) for x in ("logits", "best", "masked", "picked", "other")]
        first, second, top, total = [sb(x, [128, groups]) for x in ("first", "second", "top", "total")]
        p_l = [ctx.enter_context(nc.psum_tensor(f"ro_p{k}", [128, 4, 128], F32)) for k in range(4)]
        s_zt, s_l, s_ld, s_v, s_e = [ctx.enter_context(nc.semaphore("ro_" + x)) for x in ("s_zt", "s_l", "s_ld", "s_v", "s_e")]
        block = ctx.enter_context(nc.Block())

        def wide(t):
            return t[:].unsqueeze(2).broadcast_to([128, groups, NE])

        @block.gpsimd
        def _(pool):
            give_credits(pool, s_zt)

            def copy(at):
                pool.wait_ge(s_l, done(at.n - 4))
                pool_copy(nc, s, zt[at.k][:], row(s.z, at.n)).then_inc(s_zt, 1)

            staggered(nc.gpsimd, NP, 4, (0, copy))

        @block.tensor
        def _(te):
            give_credits(te, s_l)

            def product(at):
                te.wait_ge(s_zt, done(at.n))
                te.wait_ge(s_ld, done(at.n - 4))
                for c in range(4):
                    mm = nc.tensor.matmul(p_l[at.k][:, c, :], zt[at.k][:, c * 128:c * 128 + 128], s.moe_wr[:], start=True, stop=True)
                mm.then_inc(s_l, 1)

            staggered(nc.tensor, NP, 4, (0, product))

        @block.scalar
        def _(sc):
            sc.preload_act_table_set("natural_log_exp_and_others")
            sc.wait_ge(s_v, 11)
            nc.scalar.activation(masked[:], masked[:], ACT.Exp).then_inc(s_e, 1)

        @block.vector
        def _(ve):
            give_credits(ve, s_ld)
            all_logits = logits[:].rearrange("p (i g) e -> p i (g e)", i=NP)

            def fetch(at):
                ve.wait_ge(s_l, done(at.n))
                nc.vector.tensor_copy(row(all_logits, at.n).rearrange("p (c n) -> p c n", c=4), p_l[at.k][:, :, 0:2 * NE]).then_inc(s_ld, 1)

            staggered(nc.vector, NP, 4, (0, fetch))
            ve.wait_ge(s_ld, done(NP - 1))
            n = [0]

            def step(ins):
                ins.then_inc(s_v, 1)
                n[0] += 1
                ve.wait_ge(s_v, n[0])

            v = nc.vector
            rank = const(s, "rank").unsqueeze(1).broadcast_to([128, groups, NE])
            step(v.tensor_reduce(first[:], logits[:], AX, ALU.max))
            step(v.tensor_tensor(best[:], logits[:], wide(first), ALU.is_equal))
            step(v.tensor_tensor(best[:], best[:], rank, ALU.mult))
            step(v.tensor_reduce(top[:], best[:], AX, ALU.max))
            step(v.tensor_tensor(best[:], best[:], wide(top), ALU.is_equal))
            step(v.scalar_tensor_tensor(out=masked[:], in0=best[:], scalar=-3.0e38, in1=logits[:], op0=ALU.mult, op1=ALU.add))
            step(v.tensor_reduce(second[:], masked[:], AX, ALU.max))
            step(v.tensor_tensor(picked[:], masked[:], wide(second), ALU.is_equal))
            step(v.tensor_tensor(picked[:], picked[:], rank, ALU.mult))
            step(v.tensor_reduce(top[:], picked[:], AX, ALU.max))
            step(v.tensor_tensor(masked[:], logits[:], wide(first), ALU.subtract))
            step(v.tensor_tensor(picked[:], picked[:], wide(top), ALU.is_equal))
            step(v.tensor_tensor(picked[:], picked[:], best[:], ALU.add))
            ve.wait_ge(s_e, 1)
            step(v.tensor_tensor(other[:], picked[:], masked[:], ALU.mult))
            step(v.tensor_reduce(total[:], other[:], AX, ALU.add))
            step(v.reciprocal(total[:], total[:]))
            step(v.tensor_tensor(other[:], other[:], wide(total), ALU.mult))
            parts = s.combine[:].rearrange("p i c (b n) -> p (i c b) n", b=2)
            step(v.tensor_copy(parts[:, :, 0:NE], other[:]))
            step(v.tensor_tensor(parts[:, :, NE:2 * NE], other[:], parts[:, :, 0:NE].bitcast(F32), ALU.subtract))


def stack_high(nc, s, zs, zrow):
    return pool_copy(nc, s, zs[:], zrow.unsqueeze(1).broadcast_to([128, 2, T]))


def stack_low(nc, zs, zrow, b):
    own, other = slice(64 * b, 64 * b + 64), slice(64 - 64 * b, 128 - 64 * b)
    return nc.vector.tensor_tensor(zs[other, b, :], zrow[own, :], zs[own, b, :].bitcast(F32), ALU.subtract)


def mixture_of_experts(nc, s):
    with ExitStack() as ctx:
        def sb(name, shape, dt=F32, n=2):
            return [ctx.enter_context(nc.sbuf_tensor(f"me_{name}{k}", shape, dt)) for k in range(n)]

        def ps(name, n=2):
            return [ctx.enter_context(nc.psum_tensor(f"me_{name}{k}", [128, T], F32)) for k in range(n)]

        zs = sb("zs", [128, 2, T], F32R)
        ct_in, ct = sb("ctin", [128, 4 * 4 * NE]), sb("ct", [128, T], F32R)
        g, gw = sb("g", [128, T], n=4), sb("gw", [128, T], n=4)
        p_1, p_c, p_y, p_t = ps("p1"), ps("pc"), ps("py"), ps("pt", 1)[0]
        s_zero, s_ctin, s_high, s_low, s_hz, s_t, s_ct, s_w1, s_c, s_g, s_gw, s_w2, s_h = [
            ctx.enter_context(nc.semaphore("me_" + x)) for x in ("zero", "ctin", "high", "low", "hz", "t", "ct", "w1", "c", "g", "gw", "w2", "h")]
        block = ctx.enter_context(nc.Block())

        def where(at):
            return at.k % 8 // EP, at.k % EP

        @block.gpsimd
        def _(pool):
            for t in ct:
                nc.gpsimd.memset(t[:].bitcast(F32), 0.0).then_inc(s_zero, 1)
            give_credits(pool, s_ctin, s_high, s_hz)

            def prepare(at):
                if at.k % 8 == 0:
                    i, k = at.of(8), at.k // 8
                    pool.wait_ge(s_t, done(i - 2))
                    pool_copy(nc, s, ct_in[k][:], s.combine[:, bass.ds(i, 1), :, :].rearrange("p a b c -> p (a b c)").bitcast(F32)).then_inc(s_ctin, 1)
                    pool.wait_ge(s_w1, done(at.n - 9))
                    stack_high(nc, s, zs[k], row(s.z, i)).then_inc(s_high, 1)
                    nc.gpsimd.tensor_tensor(row(s.h, i), row(s.h, i), row(s.z, i), ALU.add).then_inc(s_hz, 1)

            staggered(nc.gpsimd, 8 * NP, 16, (0, prepare))

        @block.tensor
        def _(te):
            give_credits(te, s_t, s_w1, s_c, s_w2)
            te.wait_ge(s_zero, 2)

            def turn(at):
                if at.k % 8 == 0:
                    i = at.of(8)
                    te.wait_ge(s_ctin, done(i))
                    te.wait_ge(s_ct, done(i - 1))
                    for c in range(4):
                        mm = nc.tensor.transpose(p_t[0:4 * NE, c * 128:c * 128 + 128], ct_in[at.k // 8][:, c * 4 * NE:(c + 1) * 4 * NE], const(s, "ident"))
                    mm.then_inc(s_t, 1)

            def first(at):
                b, ep = where(at)
                if at.k % 8 == 0:
                    te.wait_ge(s_low, done(at.of(8)))
                te.wait_ge(s_g, done(at.n - 2))
                z = zs[at.k // 8][:, b, :]
                nc.tensor.matmul(p_1[at.k % 2][:], s.moe_w1h[:, ep, :], z, start=True, stop=False)
                nc.tensor.matmul(p_1[at.k % 2][:], s.moe_w1l[:, ep, :], z, start=False, stop=True).then_inc(s_w1, 1)

            def spread(at):
                b, ep = where(at)
                if at.k % 8 == 0:
                    te.wait_ge(s_ct, done(at.of(8)))
                te.wait_ge(s_gw, done(at.n - 2))
                nc.tensor.matmul(p_c[at.k % 2][:], s.pick[:, b, ep, :], ct[at.k // 8][:], start=True, stop=True).then_inc(s_c, 1)

            def bias(at):
                if at.k % 8 == 0:
                    te.wait_ge(s_h, done(at.of(8) - 2))
                    y = p_y[at.k // 8][:]
                    nc.tensor.matmul(y, s.moe_b2h[:], ct[at.k // 8][:], start=True, stop=False, skip_group_check=True)
                    nc.tensor.matmul(y, s.moe_b2l[:], ct[at.k // 8][:], start=False, stop=False, skip_group_check=True)

            def second(at):
                b, ep = where(at)
                te.wait_ge(s_gw, done(at.n))
                nc.tensor.matmul(p_y[at.k // 8][64 * b:64 * b + 64, :], s.moe_w2[:, ep, :], gw[at.k % 4][:], start=False, stop=(ep == EP - 1),
                                 skip_group_check=True).then_inc(s_w2, 1)

            staggered(nc.tensor, 8 * NP, 16, (4, first), (3, spread), (2, bias), (1, second), (10, turn))

        @block.scalar
        def _(sc):
            give_credits(sc, s_ct, s_g)

            def gelu(at):
                _, ep = where(at)
                sc.wait_ge(s_w1, done(at.n))
                sc.wait_ge(s_gw, done(at.n - 4))
                nc.scalar.activation(g[at.k % 4][:], p_1[at.k % 2][:], ACT.Gelu, bias=col(s, "moe_b1", ep)).then_inc(s_g, 1)

            def fetch(at):
                if at.k % 8 == 0:
                    sc.wait_ge(s_t, done(at.of(8)))
                    sc.wait_ge(s_c, done(at.n - 9))
                    sc.wait_ge(s_w2, done(at.n - 9))
                    nc.scalar.activation(ct[at.k // 8][0:4 * NE, :], p_t[0:4 * NE, :], ACT.Copy).then_inc(s_ct, 1)

            sc.wait_ge(s_zero, 2)
            staggered(nc.scalar, 8 * NP, 16, (3, gelu), (9, fetch))

        @block.vector
        def _(ve):
            give_credits(ve, s_low, s_gw, s_h)

            def low(at):
                if at.k % 8 == 0:
                    i = at.of(8)
                    ve.wait_ge(s_high, done(i))
                    stack_low(nc, zs[at.k // 8], row(s.z, i), 0)
                    stack_low(nc, zs[at.k // 8], row(s.z, i), 1).then_inc(s_low, 1)

            def weigh(at):
                ve.wait_ge(s_g, done(at.n))
                ve.wait_ge(s_c, done(at.n))
                ve.wait_ge(s_w2, done(at.n - 4))
                nc.vector.tensor_tensor(gw[at.k % 4][:], p_c[at.k % 2][:], g[at.k % 4][:], ALU.mult).then_inc(s_gw, 1)

            def residual(at):
                if at.k % 8 == 7:
                    i = at.of(8)
                    ve.wait_ge(s_w2, done(at.n))
                    ve.wait_ge(s_hz, done(i))
                    nc.vector.tensor_tensor(row(s.h, i), p_y[at.k // 8][:], row(s.h, i), ALU.add).then_inc(s_h, 1)

            staggered(nc.vector, 8 * NP, 16, (2, weigh), (0, residual), (8, low))


def decayed_attention(nc, s):
    with ExitStack() as ctx:
        def sb(name, shape, dt=F32, n=4):
            return [ctx.enter_context(nc.sbuf_tensor(f"da_{name}{k}", shape, dt)) for k in range(n)]

        def ps(name, n=1):
            return [ctx.enter_context(nc.psum_tensor(f"da_{name}{k}", [128, T], F32)) for k in range(n)]

        zt = sb("zt", [128, T])
        zs = sb("zs", [128, 2, T], F32R)
        qh, ql, kk = sb("qh", [128, T], F32R), sb("ql", [128, T], F32R), sb("k", [128, T], F32R)
        vt = [s.z[:, NP + k, :].rearrange("p (c n) -> p c n", c=4) for k in range(4)]
        width = [T - 128 * j for j in range(4)]
        free = s.z[:, NP + 4:NP + 10, :].rearrange("p a b -> p (a b)")
        sm = [[free[:, 3 * T * k + sum(width[:j]):3 * T * k + sum(width[:j + 1])] for j in range(4)] for k in range(2)]
        p_q, p_k, p_v, p_s, p_o = ps("pq")[0], ps("pk")[0], ps("pv")[0], ps("ps", 3), ps("po", 2)
        bank = [p_s[0][:, 0:width[0]], p_s[1][:, 0:width[1]], p_s[2][:, 0:width[2]], p_s[2][:, width[2]:width[2] + width[3]]]
        s_zt, s_high, s_low, s_qk, s_kh, s_kl, s_v, s_vt, s_s, s_sm, s_o, s_h, s_qh = [
            ctx.enter_context(nc.semaphore("da_" + x)) for x in ("s_zt", "high", "low", "qk", "kh", "kl", "v", "s_vt", "s", "sm", "o", "h", "s_qh")]
        block = ctx.enter_context(nc.Block())

        @block.gpsimd
        def _(pool):
            give_credits(pool, s_zt, s_high)

            def prepare(at):
                i = at.of(2)
                if at.k % 2 == 0:
                    pool.wait_ge(s_v, done(i - 4))
                    pool.wait_ge(s_qk, done(at.n - 7))
                    pool_copy(nc, s, zt[at.k // 2][:], row(s.z, i)).then_inc(s_zt, 1)
                    stack_high(nc, s, zs[at.k // 2], row(s.z, i)).then_inc(s_high, 1)

            staggered(nc.gpsimd, NB, 8, (0, prepare))

        @block.tensor
        def _(te):
            give_credits(te, s_qk, s_v, s_s, s_o)

            def queries_keys(at):
                te.wait_ge(s_low, done(at.n))
                te.wait_ge(s_kl, done(at.n - 1))
                z = zs[at.k // 2][:, at.k % 2, :]
                for c, p in enumerate((p_q, p_k)):
                    nc.tensor.matmul(p[:], s.a1_qkh[:, c, :], z, start=True, stop=False)
                    mm = nc.tensor.matmul(p[:], s.a1_qkl[:, c, :], z, start=False, stop=True)
                mm.then_inc(s_qk, 1)

            def values(at):
                if at.k % 2 == 0:
                    i = at.of(2)
                    te.wait_ge(s_zt, done(i))
                    te.wait_ge(s_vt, done(i - 1))
                    for c in range(4):
                        mm = nc.tensor.matmul(p_v[:, c * 128:c * 128 + 128], zt[at.k // 2][:, c * 128:c * 128 + 128], s.a1_wv[:], start=True, stop=True)
                    mm.then_inc(s_v, 1)

            def scores(at):
                te.wait_ge(s_kl, done(at.n))
                te.wait_ge(s_sm, done(4 * at.n - 1))
                for j in range(4):
                    keys = kk[at.k % 4][:, 128 * j:128 * j + 128]
                    nc.tensor.matmul(bank[j], keys, qh[at.k % 4][:, 128 * j:], start=True, stop=False, skip_group_check=True)
                    mm = nc.tensor.matmul(bank[j], keys, ql[at.k % 4][:, 128 * j:], start=False, stop=True, skip_group_check=True)
                    if j != 2:
                        mm.then_inc(s_s, 1)

            def outputs(at):
                b = at.k % 2
                te.wait_ge(s_sm, done(4 * at.n + 3))
                if b == 0:
                    te.wait_ge(s_vt, done(at.of(2)))
                    te.wait_ge(s_h, done(at.of(2) - 2))
                for j in range(4):
                    mm = nc.tensor.matmul(p_o[at.k // 2 % 2][64 * b:64 * b + 64, 128 * j:], vt[at.k // 2][:, j, 64 * b:64 * b + 64], sm[at.k % 2][j],
                                          start=(j == 0), stop=(j == 3), skip_group_check=True)
                mm.then_inc(s_o, 1)

            staggered(nc.tensor, NB, 8, (6, queries_keys), (6, values), (3, scores), (1, outputs))

        @block.scalar
        def _(sc):
            give_credits(sc, s_qh, s_kh)

            def high(at):
                sc.wait_ge(s_qk, done(at.n))
                sc.wait_ge(s_s, done(3 * at.n - 10))
                nc.scalar.activation(qh[at.k % 4][:], p_q[:], ACT.Identity, bias=col(s, "a1_bq")).then_inc(s_qh, 1)
                nc.scalar.activation(kk[at.k % 4][:], p_k[:], ACT.Identity, bias=col(s, "a1_bk")).then_inc(s_kh, 1)

            staggered(nc.scalar, NB, 8, (5, high))

        @block.vector
        def _(ve):
            give_credits(ve, s_low, s_kl, s_vt, s_sm, s_h)

            def low(at):
                ve.wait_ge(s_high, done(at.of(2)))
                stack_low(nc, zs[at.k // 2], row(s.z, at.of(2)), at.k % 2).then_inc(s_low, 1)

            def split(at):
                up = slice(64, 128)
                ve.wait_ge(s_qh, done(at.n))
                nc.vector.scalar_tensor_tensor(out=ql[at.k % 4][:], in0=p_q[:], scalar=col(s, "a1_bq"), in1=qh[at.k % 4][:].bitcast(F32),
                                               op0=ALU.add, op1=ALU.subtract)
                ve.wait_ge(s_kh, done(at.n))
                nc.vector.scalar_tensor_tensor(out=kk[at.k % 4][up, :], in0=p_k[up, :], scalar=s.cols[up, COLS["a1_bk"]:COLS["a1_bk"] + 1],
                                               in1=kk[at.k % 4][up, :].bitcast(F32), op0=ALU.add, op1=ALU.subtract).then_inc(s_kl, 1)

            def values(at):
                if at.k % 2 == 0:
                    ve.wait_ge(s_v, done(at.of(2)))
                    ve.wait_ge(s_o, done(at.n - 7))
                    nc.vector.tensor_tensor(vt[at.k // 2], p_v[:].rearrange("p (c n) -> p c n", c=4),
                                            s.a1_bv[:].rearrange("p a b -> p (a b)").unsqueeze(1).broadcast_to([128, 4, 128]), ALU.add).then_inc(s_vt, 1)

            def decay(at):
                ve.wait_ge(s_o, done(at.n - 2))
                for j in range(4):
                    ve.wait_ge(s_s, done(3 * at.n + min(j, 2)))
                    nc.vector.tensor_tensor(sm[at.k % 2][j], bank[j], const(s, "decay")[:, 0:width[j]], ALU.mult).then_inc(s_sm, 1)

            def residual(at):
                if at.k % 2 == 1:
                    ve.wait_ge(s_o, done(at.n))
                    h = row(s.h, at.of(2))
                    nc.vector.tensor_tensor(h, p_o[at.k // 2 % 2][:], h, ALU.add).then_inc(s_h, 1)

            staggered(nc.vector, NB, 8, (7, low), (5, split), (5, values), (2, decay), (0, residual))


def soft_router(nc, s):
    with ExitStack() as ctx:
        def sb(name, shape):
            return ctx.enter_context(nc.sbuf_tensor("sr_" + name, shape, F32))

        logits, w = sb("logits", [128, 4, NE]), sb("w", [128, 4, NE])
        top, total = sb("top", [128, 4]), sb("total", [128, 4])
        wide_w = sb("wide", [128, 4, NE, D])
        ps = [ctx.enter_context(nc.psum_tensor(f"sr_p{k}", [128, 4, 128], F32)) for k in range(6)]
        s_p, s_v, s_a = [ctx.enter_context(nc.semaphore("sr_" + x)) for x in ("pe", "dve", "act")]
        block = ctx.enter_context(nc.Block())

        @block.tensor
        def _(te):
            for c in range(4):
                nc.tensor.matmul(ps[0][:, c, :], s.feat[:, c * 128:c * 128 + 128], s.f1_wr[:], start=True, stop=True).then_inc(s_p, 1)
            te.wait_ge(s_v, 8)
            for ep in range(EP):
                for c in range(4):
                    nc.tensor.matmul(ps[1 + ep][:, c, :], wide_w[:, c, 2 * ep:2 * ep + 2, :].rearrange("p a b -> p (a b)"), const(s, "ident"),
                                     start=True, stop=True).then_inc(s_p, 1)
            for ep in range(EP):
                te.wait_ge(s_a, ep + 2)
                nc.tensor.matmul(ps[5][:].rearrange("p a b -> p (a b)"), s.f1_wdup[:, ep, :, :].rearrange("p a b -> p (a b)"), s.f1_w[:, ep, :],
                                 start=(ep == 0), stop=(ep == EP - 1)).then_inc(s_p, 1)

        @block.scalar
        def _(sc):
            sc.preload_act_table_set("natural_log_exp_and_others")
            sc.wait_ge(s_v, 4)
            nc.scalar.activation(w[:], logits[:], ACT.Exp).then_inc(s_a, 1)
            for ep in range(EP):
                sc.wait_ge(s_p, 4 + 4 * (ep + 1))
                nc.scalar.activation(s.f1_w[:, ep, :], ps[1 + ep][:].rearrange("p a b -> p (a b)"), ACT.Copy).then_inc(s_a, 1)
            sc.wait_ge(s_p, 24)
            nc.scalar.activation(s.f1_r, ps[5][:].rearrange("p a b -> p (a b)"), ACT.Copy).then_inc(s_a, 1)

        @block.vector
        def _(ve):
            n = [0]

            def step(ins):
                ins.then_inc(s_v, 1)
                n[0] += 1
                ve.wait_ge(s_v, n[0])

            def wide(t):
                return t[:].unsqueeze(2).broadcast_to([128, 4, NE])

            v = nc.vector
            ve.wait_ge(s_p, 4)
            step(v.tensor_scalar(logits[:], ps[0][:, :, 0:NE], 1.0 / NB, None, ALU.mult))
            step(v.tensor_tensor(logits[:], logits[:], s.f1_br[:].unsqueeze(1).broadcast_to([128, 4, NE]), ALU.add))
            step(v.tensor_reduce(top[:], logits[:], AX, ALU.max))
            step(v.tensor_tensor(logits[:], logits[:], wide(top), ALU.subtract))
            ve.wait_ge(s_a, 1)
            step(v.tensor_reduce(total[:], w[:], AX, ALU.add))
            step(v.reciprocal(total[:], total[:]))
            step(v.tensor_tensor(w[:], w[:], wide(total), ALU.mult))
            step(v.tensor_copy(wide_w[:].rearrange("p a b c -> p (a b) c"), w[:].rearrange("p a b -> p (a b)").unsqueeze(2).broadcast_to([128, 4 * NE, D])))


def soft_experts(nc, s, out):
    with ExitStack() as ctx:
        def sb(name, shape, dt=F32, n=2):
            return [ctx.enter_context(nc.sbuf_tensor(f"se_{name}{k}", shape, dt)) for k in range(n)]

        def ps(name, n=2):
            return [ctx.enter_context(nc.psum_tensor(f"se_{name}{k}", [128, T], F32)) for k in range(n)]

        zs = sb("zs", [128, 2, T], F32R)
        a1, a2 = sb("a1", [128, T], n=4), sb("a2", [128, T], n=4)
        res, rows = sb("res", [128, T]), sb("rows", [128, 2, 4, D])
        p_1, p_2, p_y, p_t = ps("p1"), ps("p2"), ps("py"), ps("pt", 1)[0]
        s_high, s_low, s_hr, s_w1, s_a1, s_w2, s_a2, s_wo, s_res, s_t, s_rows, *s_out = [
            ctx.enter_context(nc.semaphore("se_" + x)) for x in ("high", "low", "hr", "w1", "s_a1", "w2", "s_a2", "wo", "s_res", "t", "s_rows", "out0", "out1")]
        block = ctx.enter_context(nc.Block())

        def where(at):
            return at.k % 8 // EP, at.k % EP

        @block.gpsimd
        def _(pool):
            give_credits(pool, s_high, s_hr)

            def prepare(at):
                if at.k % 8 == 0:
                    i, k = at.of(8), at.k // 8
                    pool.wait_ge(s_w1, done(at.n - 9))
                    stack_high(nc, s, zs[k], row(s.z, i)).then_inc(s_high, 1)
                    nc.gpsimd.tensor_tensor(row(s.h, i), row(s.h, i), s.f1_r, ALU.add).then_inc(s_hr, 1)

            staggered(nc.gpsimd, 8 * NP, 16, (0, prepare))

        @block.tensor
        def _(te):
            give_credits(te, s_w1, s_w2, s_wo, s_t)

            def first(at):
                b, ep = where(at)
                if at.k % 8 == 0:
                    te.wait_ge(s_low, done(at.of(8)))
                te.wait_ge(s_a1, done(at.n - 2))
                z = zs[at.k // 8][:, b, :]
                nc.tensor.matmul(p_1[at.k % 2][:], s.f1_w1h[:, ep, :], z, start=True, stop=False)
                nc.tensor.matmul(p_1[at.k % 2][:], s.f1_w1l[:, ep, :], z, start=False, stop=True).then_inc(s_w1, 1)

            def second(at):
                _, ep = where(at)
                te.wait_ge(s_a1, done(at.n))
                te.wait_ge(s_a2, done(at.n - 2))
                nc.tensor.matmul(p_2[at.k % 2][:], s.f1_w2[:, ep, :], a1[at.k % 4][:], start=True, stop=True).then_inc(s_w2, 1)

            def third(at):
                b, ep = where(at)
                te.wait_ge(s_a2, done(at.n))
                if at.k % 8 == 0:
                    te.wait_ge(s_res, done(at.of(8) - 2))
                nc.tensor.matmul(p_y[at.k // 8][64 * b:64 * b + 64, :], s.f1_wo[:, ep, :], a2[at.k % 4][:], start=(ep == 0), stop=(ep == EP - 1),
                                 skip_group_check=True).then_inc(s_wo, 1)

            def turn(at):
                if at.k % 8 == 7:
                    i = at.of(8)
                    te.wait_ge(s_res, done(i))
                    te.wait_ge(s_rows, done(i - 1))
                    for c in range(4):
                        mm = nc.tensor.transpose(p_t[:, c * 128:c * 128 + 128], res[at.k // 8][:, c::4], const(s, "ident"))
                    mm.then_inc(s_t, 1)

            staggered(nc.tensor, 8 * NP, 16, (7, first), (5, second), (3, third), (1, turn))

        @block.scalar
        def _(sc):
            give_credits(sc, s_a1, s_rows)

            def relu(at):
                _, ep = where(at)
                sc.wait_ge(s_w1, done(at.n))
                sc.wait_ge(s_w2, done(at.n - 4))
                nc.scalar.activation(a1[at.k % 4][:], p_1[at.k % 2][:], ACT.Relu, scale=col(s, "f1_g1", ep), bias=col(s, "f1_be1", ep)).then_inc(s_a1, 1)

            def fetch(at):
                if at.k % 8 == 7:
                    i = at.of(8)
                    sc.wait_ge(s_t, done(i))
                    sc.wait_ge(s_out[at.k // 8], at.of(16) * 16 + 16)
                    nc.scalar.activation(rows[at.k // 8][:].rearrange("p b t c -> p t b c"), p_t[:].rearrange("p (t b c) -> p t b c", t=4, b=2),
                                         ACT.Copy).then_inc(s_rows, 1)

            staggered(nc.scalar, 8 * NP, 16, (6, relu), (0, fetch))

        @block.vector
        def _(ve):
            give_credits(ve, s_low, s_a2, s_res)

            def low(at):
                if at.k % 8 == 0:
                    i = at.of(8)
                    ve.wait_ge(s_high, done(i))
                    stack_low(nc, zs[at.k // 8], row(s.z, i), 0)
                    stack_low(nc, zs[at.k // 8], row(s.z, i), 1).then_inc(s_low, 1)

            def weigh(at):
                _, ep = where(at)
                ve.wait_ge(s_w2, done(at.n))
                ve.wait_ge(s_wo, done(at.n - 4))
                nc.vector.scalar_tensor_tensor(out=a2[at.k % 4][:], in0=p_2[at.k % 2][:], scalar=col(s, "f1_be2", ep), in1=s.f1_w[:, ep, :],
                                               op0=ALU.max, op1=ALU.mult).then_inc(s_a2, 1)

            def residual(at):
                if at.k % 8 == 7:
                    i = at.of(8)
                    ve.wait_ge(s_wo, done(at.n))
                    ve.wait_ge(s_hr, done(i))
                    ve.wait_ge(s_t, done(i - 2))
                    nc.vector.tensor_tensor(res[at.k // 8][:], p_y[at.k // 8][:], row(s.h, i), ALU.add).then_inc(s_res, 1)

            staggered(nc.vector, 8 * NP, 16, (4, weigh), (2, residual), (10, low))

        @block.sync
        def _(sp):
            for x in s_out:
                sp.sem_inc(x, 16)

            def store(at):
                sp.wait_ge(s_rows, done(at.n))
                sp.dma_start(out[bass.ds(at.n * 2, 2), :, :].rearrange("b (p t) c -> p b (t c)", t=4),
                             rows[at.k][:].rearrange("p b t c -> p b (t c)")).then_inc(s_out[at.k], 16)

            staggered(nc.sync, NP, 2, (0, store))
            for x in s_out:
                sp.wait_ge(x, 16 * (1 + NP // 2))





def build(nc, a, out):
    with ExitStack() as ctx:
        s = allocate(nc, ctx)
        prepare(nc, s, a)
        spectral_norm(nc, s, a)
        tokenizer_output(nc, s)
        layer_norm(nc, s, "ln0")
        neighbourhood_attention(nc, s)
        layer_norm(nc, s, "ln1")
        route(nc, s)
        mixture_of_experts(nc, s)

        layer_norm(nc, s, "ln2")
        decayed_attention(nc, s)

        layer_norm(nc, s, "ln3", features=True)
        soft_router(nc, s)
        soft_experts(nc, s, out)


_INS = ['x', 'L0_tok_freq_bands', 'L0_tok_w1', 'L0_tok_b1', 'L0_tok_gamma', 'L0_tok_beta', 'L0_tok_w2', 'L0_tok_b2',
        'L0_attn_w_qkv', 'L0_attn_b_qkv', 'L0_attn_w_proj', 'L0_attn_b_proj', 'L0_ffn_router_w', 'L0_ffn_w1', 'L0_ffn_b1',
        'L0_ffn_w2', 'L0_ffn_b2', 'L1_attn_Wqkv', 'L1_attn_bqkv', 'L1_ffn_Wr', 'L1_ffn_br', 'L1_ffn_W1', 'L1_ffn_b1',
        'L1_ffn_g1', 'L1_ffn_be1', 'L1_ffn_m1', 'L1_ffn_v1', 'L1_ffn_W2', 'L1_ffn_b2', 'L1_ffn_g2', 'L1_ffn_be2',
        'L1_ffn_m2', 'L1_ffn_v2', 'L1_ffn_Wo', 'L1_ffn_bo']


def kernel(**inputs):
    import concourse.bacc as bacc
    from concourse.bass_utils import run_bass_kernel_spmd

    nc = bacc.Bacc("TRN2", target_bir_lowering=False, num_devices=1)
    arrays, aps = {}, {}
    for name in _INS + ["const"]:
        array = constants() if name == "const" else np.ascontiguousarray(inputs[name])
        arrays[f"in_{name}"] = array
        aps[name] = nc.dram_tensor(f"in_{name}", array.shape, mybir.dt.from_np(array.dtype), kind="ExternalInput").ap()
    out = nc.dram_tensor("out", (NB, T, D), F32, kind="ExternalOutput").ap()
    build(nc, aps, out)
    r = run_bass_kernel_spmd(nc, [arrays], core_ids=[0])
    return r.results[0]["out"]
```

```python
from contextlib import ExitStack

import numpy as np
import concourse.bass as bass
from concourse import mybir

F32 = mybir.dt.float32
F32R = mybir.dt.float32r
BF16 = mybir.dt.bfloat16
I32 = mybir.dt.int32
ALU = mybir.AluOpType
ACT = mybir.ActivationFunctionType
AX = mybir.AxisListType.X

NB, T, D = 32, 512, 64
NP = NB // 2
HID = 2 * D
NF = D // 2
NE = 8
EP = NE // 2
NH, DH = 8, 8
KW, DIL = 31, 2
TG = T // DIL
QT = 32
NT = TG // QT
WIN = 64
LN_EPS = 1e-5
BN_EPS = 1e-3
NEG = -1.0e30
ALPHA = 0.99


def window_start(t):
    return min(max(t * QT - KW // 2, 0), TG - WIN)


CONST_PARTS = [("ident", 128), ("dft", 4 * 2 * NF), ("shift", T), ("center", 128), ("mean64", 128), ("mean128", 128),
               ("decay", T), ("winmask", 2 * WIN), ("headmask", NH), ("vmask", 18), ("rank", NE),
               ("pick", 2 * EP * 128)]
CONST_AT = {}
_at = 0
for _name, _n in CONST_PARTS:
    CONST_AT[_name] = (_at, _n)
    _at += _n
CONST_COLS = _at
FIRST_CONST = CONST_AT["center"][0]


def constants():
    c = {}
    c["ident"] = np.eye(128)
    block = np.kron(np.eye(2), np.full((D, D), 1.0 / D))
    c["center"] = np.eye(128) - block
    c["mean64"] = block
    c["mean128"] = np.full((128, 128), 1.0 / HID)
    t = np.arange(T)[:, None] * np.arange(NF)[None, :] % T * (2 * np.pi / T)
    dft = np.concatenate([np.cos(t), -np.sin(t)], 1)
    c["dft"] = dft.reshape(4, 128, 2 * NF).transpose(1, 0, 2).reshape(128, -1)
    step = np.float32(2.0 * np.pi / T)
    shift = (step * np.arange(T, dtype=np.float32)[None, :]) * np.arange(NF, dtype=np.float32)[:, None]
    shift = shift.astype(np.float64)
    c["shift"] = np.concatenate([np.cos(shift), np.sin(shift)] * 2, 0)
    k, q = np.arange(128)[:, None], np.arange(T)[None, :]
    c["decay"] = np.where(q >= k, np.power(float(np.float32(ALPHA)), np.maximum(q - k, 0)), 0.0) / np.sqrt(D)
    mask = np.full((2, 128, WIN), NEG)
    for half in range(2):
        for r in range(128):
            p = half * 128 + r
            first = min(max(p - KW // 2, 0), TG - KW) - window_start(p // QT)
            mask[half, r, first:first + KW] = 0.0
    c["winmask"] = mask.transpose(1, 0, 2).reshape(128, -1)
    c["headmask"] = np.kron(np.ones((2, 1)), np.kron(np.eye(NH), np.ones((DH, 1))))
    v = np.zeros((128, 18))
    v[:WIN, 0:8] = v[WIN:2 * WIN, 8:16] = 1.0
    v[:WIN, 16] = v[WIN:2 * WIN, 17] = 1.0
    c["vmask"] = v
    c["rank"] = np.broadcast_to(np.arange(NE, 0, -1), (128, NE))
    pick = np.zeros((128, 2, EP, 128))
    for b in range(2):
        for part in range(2):
            for e in range(NE):
                pick[(b * 2 + part) * NE + e, b, e // 2, (e % 2) * 64:(e % 2) * 64 + 64] = 1.0
    c["pick"] = pick.reshape(128, -1)
    return np.ascontiguousarray(np.concatenate([c[n] for n, _ in CONST_PARTS], 1).astype(np.float32))


class Buffers:
    pass


def allocate(nc, ctx):
    s = Buffers()

    def sb(name, shape, dt=F32):
        return ctx.enter_context(nc.sbuf_tensor(name, shape, dt))

    s.const = sb("const", [128, CONST_COLS])
    s.h = sb("h", [128, NP, T])
    s.z = sb("z", [128, NB, T])
    s.pick = sb("pick_r", [128, 2, EP, 128], F32R)
    s.winmask = sb("winmask_b", [128, 2, NH, WIN], BF16)
    s.ident_b = sb("ident_b", [128, 128], BF16)
    s.shift = sb("shift_r", [128, T], F32R)
    s.w1s = sb("tok_w1s", [128, HID])
    s.phase = sb("tok_phase", [128, NB])
    s.tok_bias = sb("tok_bias", [128, NB])
    s.tok_w2 = sb("tok_w2", [128, D])
    s.a0_qkh = sb("a0_qkh", [128, 128], F32R)
    s.a0_qkl = sb("a0_qkl", [128, 128], F32R)
    s.a0_wv = sb("a0_wv", [128, 128])
    s.a0_wp = sb("a0_wp", [128, 128])
    s.moe_wr = sb("moe_wr", [128, 128])
    s.moe_w1h = sb("moe_w1h", [128, EP, 128], F32R)
    s.moe_w1l = sb("moe_w1l", [128, EP, 128], F32R)
    s.moe_w2 = sb("moe_w2", [128, EP, D])
    s.moe_b2h = sb("moe_b2h", [128, 128], F32R)
    s.moe_b2l = sb("moe_b2l", [128, 128], F32R)
    s.a1_qkh = sb("a1_qkh", [128, 2, 128], F32R)
    s.a1_qkl = sb("a1_qkl", [128, 2, 128], F32R)
    s.a1_wv = sb("a1_wv", [128, 128])
    s.a1_bv = sb("a1_bv", [128, 2, D])
    s.f1_wr = sb("f1_wr", [128, 128])
    s.f1_br = sb("f1_br", [128, NE])
    s.f1_w1h = sb("f1_w1h", [128, EP, 128], F32R)
    s.f1_w1l = sb("f1_w1l", [128, EP, 128], F32R)
    s.f1_w2 = sb("f1_w2", [128, EP, 128])
    s.f1_wo = sb("f1_wo", [128, EP, D])
    s.f1_wdup = sb("f1_wdup", [128, EP, 2, D])
    s.f1_w = s.z[:, NP:NP + EP, :]
    s.f1_r = s.z[:, NP + EP, :]
    s.feat = sb("feat", [128, T])
    s.bn_diag = s.feat[:].rearrange("p (e n) -> p e n", e=EP)
    s.raw = sb("raw", [128, 2 * NE * D + 128 + 4 * D + EP * D + 2 * D + 3 * 2 * EP])
    at = 0

    def part(*shape):
        nonlocal at
        n = int(np.prod(shape))
        at += n
        return s.raw[:, at - n:at]

    s.raw_moe_w1, s.raw_f1_w1, s.raw_moe_b2, s.raw_a1_qk = part(NE, D), part(NE, D), part(128), part(2, 2, D)
    s.raw_bo, s.raw_a0_qk = part(EP, D), part(2 * D)
    s.bn_var, s.bn_scale, s.bn_shift = [part(2, EP).rearrange("p (k e) -> p k e", k=2) for _ in range(3)]
    s.loaded = ctx.enter_context(nc.semaphore("loaded"))
    s.bn_ready = ctx.enter_context(nc.semaphore("bn_ready"))
    s.eps = sb("eps", [128, 1])
    s.one = sb("one", [128, 1])
    s.cols = sb("cols", [128, 64])
    return s


COLS = {n: i for i, n in enumerate([
    "gamma", "beta", "tok_b2", "a0_bq", "a0_bk", "a0_bv", "a0_bp", "a1_bq", "a1_bk", "freq"])}
for _k, _n in enumerate(["moe_b1", "f1_b1", "f1_g1", "f1_be1", "f1_m1", "f1_v1", "f1_b2", "f1_g2", "f1_be2", "f1_m2", "f1_v2"]):
    COLS[_n] = 12 + EP * _k


def const(s, name, rows=128):
    at, n = CONST_AT[name]
    return s.const[0:rows, at:at + n]


def col(s, name, k=0):
    return s.cols[:, COLS[name] + k:COLS[name] + k + 1]


def cols4(s, name):
    return s.cols[:, COLS[name]:COLS[name] + EP]


def column(ap):
    return ap.rearrange("(p a) -> p a", a=1)


def later_loads(s, a):
    experts = lambda t, e: t.rearrange("p (e d) -> p e d", e=e)
    loads = []
    for e2 in range(2):
        n = 64 * e2
        hf = slice(n, n + 64)
        for name, src in [("tok_b2", a["L0_tok_b2"]), ("a0_bq", a["L0_attn_b_qkv"][0:D]), ("a0_bk", a["L0_attn_b_qkv"][D:2 * D]),
                          ("a0_bv", a["L0_attn_b_qkv"][2 * D:3 * D]), ("a0_bp", a["L0_attn_b_proj"]), ("a1_bq", a["L1_attn_bqkv"][0:D]),
                          ("a1_bk", a["L1_attn_bqkv"][D:2 * D])]:
            loads.append((s.cols[hf, COLS[name]:COLS[name] + 1], column(src)))
        for name, key in [("f1_v1", "L1_ffn_v1"), ("f1_v2", "L1_ffn_v2"), ("moe_b1", "L0_ffn_b1"), ("f1_b1", "L1_ffn_b1"), ("f1_g1", "L1_ffn_g1"),
                          ("f1_be1", "L1_ffn_be1"), ("f1_m1", "L1_ffn_m1"), ("f1_b2", "L1_ffn_b2"), ("f1_g2", "L1_ffn_g2"),
                          ("f1_be2", "L1_ffn_be2"), ("f1_m2", "L1_ffn_m2")]:
            loads.append((s.cols[hf, COLS[name]:COLS[name] + EP], a[key].rearrange("(p two) h -> two h p", two=2)[e2]))
        loads.append((s.raw_a0_qk[hf, :], a["L0_attn_w_qkv"][:, 0:2 * D]))
        loads.append((s.a0_wv[hf, hf], a["L0_attn_w_qkv"][:, 2 * D:3 * D]))
        loads.append((s.a0_wp[hf, hf], a["L0_attn_w_proj"]))
        loads.append((s.moe_wr[hf, NE * e2:NE * e2 + NE], a["L0_ffn_router_w"].rearrange("e d -> d e")))
        loads.append((experts(s.raw_moe_w1[hf, :], NE), a["L0_ffn_w1"].rearrange("e d h -> d e h")))
        loads.append((experts(s.raw_f1_w1[hf, :], NE), a["L1_ffn_W1"].rearrange("e d h -> d e h")))
        loads.append((s.a1_wv[hf, hf], a["L1_attn_Wqkv"][:, 2 * D:3 * D]))
        loads.append((s.f1_wr[hf, 0:NE], a["L1_ffn_Wr"]))
        qk = s.raw_a1_qk[hf, :].rearrange("p (n c e) -> p n c e", n=2, c=2)
        for c in range(2):
            loads.append((qk[:, :, c, :], a["L1_attn_Wqkv"][:, 0:2 * D].rearrange("d (n e) -> d n e", n=2)))
        loads.append((s.moe_w2[hf, :, :], a["L0_ffn_w2"].rearrange("(p two) h d -> two h p d", two=2)[e2]))
        loads.append((s.f1_w2[hf, :, hf], a["L1_ffn_W2"].rearrange("(p two) h d -> two h p d", two=2)[e2]))
        loads.append((s.f1_wo[hf, :, :], a["L1_ffn_Wo"].rearrange("(p two) h d -> two h p d", two=2)[e2]))
        loads.append((experts(s.raw_bo[n:n + 1, :], EP), a["L1_ffn_bo"].rearrange("(p two) d -> two p d", two=2)[e2:e2 + 1]))
        for part in range(2):
            r = (e2 * 2 + part) * NE
            loads.append((s.raw_moe_b2[r:r + NE, hf], a["L0_ffn_b2"]))
        loads.append((s.a1_bv[:, e2, :], a["L1_attn_bqkv"][2 * D:3 * D].partition_broadcast(128)))
    loads.append((s.f1_br[:], a["L1_ffn_br"].partition_broadcast(128)))
    return loads


def prepare(nc, s, a):
    with ExitStack() as ctx:
        def sb(name, shape, dt=F32):
            return ctx.enter_context(nc.sbuf_tensor(name, shape, dt))

        def sem(name):
            return ctx.enter_context(nc.semaphore(name))

        x_in = sb("x_in", [NB, T], I32)
        signal = sb("signal", [NB, T])
        signal_t = sb("signal_t", [128, 4, NB])
        spec = sb("spec", [NB, 2, NF])
        spec_sq = sb("spec_sq", [NB, 2, NF])
        power = sb("power", [NB, NF])
        is_zero = sb("is_zero", [NB, NF])
        mag = sb("mag", [NB, NF])
        inv = sb("inv", [NB, NF])
        sincos = sb("sincos", [NB, 4, NF])
        mag_t = sb("mag_t", [NF + 1, NB])
        w1m = sb("w1m", [NF + 1, HID])
        rowsum = sb("rowsum", [128, 2])
        ps = [ctx.enter_context(nc.psum_tensor(f"prep_ps{n}", [128, 512], F32)) for n in range(5)]

        zeroed, x_loaded, const_loaded, w1_loaded = sem("zeroed"), sem("x_loaded"), sem("const_loaded"), sem("w1_loaded")
        other_loaded = sem("other_loaded")
        dve, act, pe = sem("prep_dve"), sem("prep_act"), sem("prep_pe")
        block = ctx.enter_context(nc.Block())
        w1 = a["L0_tok_w1"]
        SIGNAL, SIGNAL_T, POWER, SINCOS, MAG_T = 1, 11, 17, 22, 24
        w1_loads = [(w1m[0:NF, :], w1[0:NF, :]), (w1m[NF:NF + 1, :], a["L0_tok_b1"].rearrange("(p n) -> p n", p=1))]
        w1_loads += [(s.w1s[32 * n:32 * n + 32, :], w1[NF:D, :]) for n in range(4)]
        w1_loads += [(s.cols[0:NF, COLS["freq"]:COLS["freq"] + 1], column(a["L0_tok_freq_bands"]))]
        others = [(s.const[:, FIRST_CONST:], a["const"][:, FIRST_CONST:]), (col(s, "gamma"), column(a["L0_tok_gamma"])),
                  (col(s, "beta"), column(a["L0_tok_beta"])), (s.tok_w2[:], a["L0_tok_w2"])]
        cleared = [s.cols, s.a0_wv, s.a0_wp, s.moe_wr, s.a1_wv, s.f1_wr, s.f1_w2, s.raw]

        @block.gpsimd
        def _(pool):
            for t in cleared:
                nc.gpsimd.memset(t[:], 0.0).then_inc(zeroed, 1)
            pool.wait_ge(zeroed, len(cleared))

        @block.sync
        def _(sp):
            sp.dma_start(x_in[:], a["x"]).then_inc(x_loaded, 16)
            for dst, src in w1_loads[:-1]:
                sp.dma_start(dst, src).then_inc(w1_loaded, 16)
            sp.wait_ge(other_loaded, 16 * len(others))

        @block.scalar
        def _(sc):
            sc.dma_start(s.const[:, 0:FIRST_CONST], a["const"][:, 0:FIRST_CONST]).then_inc(const_loaded, 16)
            sc.wait_ge(zeroed, 1)
            for dst, src in w1_loads[-1:]:
                sc.dma_start(dst, src, allow_slow_non_contiguous=True).then_inc(w1_loaded, 16)
            for dst, src in others:
                sc.dma_start(dst, src, allow_slow_non_contiguous=True).then_inc(other_loaded, 16)
            sc.preload_act_table_set("sqrt_and_others")
            sc.wait_ge(dve, POWER)
            nc.scalar.activation(mag[:], power[:], ACT.Sqrt).then_inc(act, 1)

        @block.tensor
        def _(te):
            te.wait_ge(const_loaded, 16)
            te.wait_ge(dve, SIGNAL)
            for c in range(4):
                nc.tensor.transpose(ps[0][:, c * NB:(c + 1) * NB], signal[:, c * 128:(c + 1) * 128],
                                    const(s, "ident", NB)[:, 0:NB]).then_inc(pe, 1)
            te.wait_ge(dve, SIGNAL_T)
            dft = const(s, "dft").rearrange("p (c n) -> p c n", c=4)
            for c in range(4):
                nc.tensor.matmul(ps[1][0:NB, 0:2 * NF], signal_t[:, c, :], dft[:, c, :],
                                 start=(c == 0), stop=(c == 3)).then_inc(pe, 1)
            te.wait_ge(dve, SINCOS)
            nc.tensor.transpose(ps[2][:, 0:NB], sincos[:].rearrange("p a b -> p (a b)"),
                                const(s, "ident", NB)[:, 0:NB]).then_inc(pe, 1)
            nc.tensor.transpose(ps[3][0:NF, 0:NB], mag[:], const(s, "ident", NB)[:, 0:NB]).then_inc(pe, 1)
            te.wait_ge(dve, MAG_T)
            nc.tensor.matmul(ps[4][:, 0:NB], w1m[:], mag_t[:], start=True, stop=True).then_inc(pe, 1)

        @block.vector
        def _(ve):
            n = [0]

            def step(ins):
                ins.then_inc(dve, 1)
                n[0] += 1
                ve.wait_ge(dve, n[0])

            v = nc.vector
            up = slice(64, 128)
            ve.wait_ge(x_loaded, 16)
            step(v.tensor_scalar(signal[:], x_in[:], 1.0 / 127.5, -1.0, ALU.mult, ALU.add))
            assert n[0] == SIGNAL
            step(v.memset(mag_t[:], 1.0))
            step(v.memset(s.eps[:], LN_EPS))
            step(v.memset(s.one[:], 1.0))
            ve.wait_ge(w1_loaded, 16 * len(w1_loads))
            step(v.tensor_reduce(rowsum[:, 0:1], s.w1s[:], AX, ALU.add))
            step(v.tensor_reduce(rowsum[0:NF + 1, 1:2], w1m[:], AX, ALU.add))
            step(v.tensor_scalar(rowsum[:, 0:1], rowsum[:, 0:1], 1.0 / HID, None, ALU.mult))
            step(v.tensor_scalar(rowsum[0:NF + 1, 1:2], rowsum[0:NF + 1, 1:2], 1.0 / HID, None, ALU.mult))
            step(v.tensor_scalar(s.w1s[:], s.w1s[:], rowsum[:, 0:1], None, ALU.subtract))
            step(v.tensor_scalar(w1m[:], w1m[:], rowsum[0:NF + 1, 1:2], None, ALU.subtract))
            ve.wait_ge(pe, 4)
            step(v.tensor_copy(signal_t[:].rearrange("p c b -> p (c b)"), ps[0][:, 0:4 * NB]))
            assert n[0] == SIGNAL_T
            ve.wait_ge(pe, 8)
            step(v.tensor_copy(spec[:].rearrange("p a b -> p (a b)"), ps[1][0:NB, 0:2 * NF]))
            re, im = spec[:, 0, :], spec[:, 1, :]
            step(v.tensor_tensor(spec_sq[:], spec[:], spec[:], ALU.mult))
            step(v.tensor_tensor(power[:], spec_sq[:, 0, :], spec_sq[:, 1, :], ALU.add))
            step(v.tensor_scalar(is_zero[:], power[:], 0.0, None, ALU.is_equal))
            step(v.tensor_tensor(re, re, is_zero[:], ALU.add))
            step(v.tensor_tensor(power[:], power[:], is_zero[:], ALU.add))
            assert n[0] == POWER
            step(v.tensor_copy(s.shift[:], const(s, "shift")))
            ve.wait_ge(act, 1)
            step(v.reciprocal(inv[:], mag[:]))
            step(v.tensor_tensor(sincos[:, 0::2, :], im.unsqueeze(1).broadcast_to([NB, 2, NF]),
                                 inv[:].unsqueeze(1).broadcast_to([NB, 2, NF]), ALU.mult))
            step(v.tensor_tensor(sincos[:, 1::2, :], re.unsqueeze(1).broadcast_to([NB, 2, NF]),
                                 inv[:].unsqueeze(1).broadcast_to([NB, 2, NF]), ALU.mult))
            step(v.tensor_tensor(mag[:], mag[:], is_zero[:], ALU.subtract))
            assert n[0] == SINCOS
            ve.wait_ge(pe, 9)
            step(v.tensor_copy(s.phase[:], ps[2][:, 0:NB]))
            ve.wait_ge(pe, 10)
            step(v.tensor_scalar(mag_t[0:NF, :], ps[3][0:NF, 0:NB], s.cols[0:NF, COLS["freq"]:COLS["freq"] + 1], None, ALU.mult))
            assert n[0] == MAG_T
            step(v.tensor_tensor(s.shift[up, :], const(s, "shift")[up, :], s.shift[up, :].bitcast(F32), ALU.subtract))
            ve.wait_ge(pe, 11)
            step(v.tensor_copy(s.tok_bias[:], ps[4][:, 0:NB]))


def derive_weights(nc, s, step):
    p = nc.gpsimd

    def product(out, x, y, op=ALU.mult):
        step(p.tensor_tensor(out, x, y, op))

    def split(high, low, whole):
        step(p.tensor_copy(high, whole))
        product(low, whole, high.bitcast(F32), ALU.subtract)

    def flat(t):
        return t[:].rearrange("p a b -> p (a b)")

    product(s.bn_shift, s.bn_scale, s.bn_scale)
    product(s.bn_shift, s.bn_shift, s.bn_var)
    step(p.tensor_scalar(s.bn_shift, s.bn_shift, -0.5, 1.5, ALU.mult, ALU.add))
    product(s.bn_scale, s.bn_scale, s.bn_shift)
    for k in range(2):
        m = f"{k + 1}"
        product(cols4(s, "f1_g" + m), cols4(s, "f1_g" + m), s.bn_scale[:, k, :])
        product(s.bn_shift[:, k, :], cols4(s, "f1_b" + m), cols4(s, "f1_m" + m), ALU.subtract)
        product(s.bn_shift[:, k, :], s.bn_shift[:, k, :], cols4(s, "f1_g" + m))
        product(cols4(s, "f1_be" + m), cols4(s, "f1_be" + m), s.bn_shift[:, k, :], ALU.add)
    product(s.bn_diag, const(s, "ident").unsqueeze(1).broadcast_to([128, EP, 128]), cols4(s, "f1_g2").unsqueeze(2).broadcast_to([128, EP, 128]))
    for c in range(2):
        product(s.f1_wdup[:, :, c, :], s.f1_wo[:], cols4(s, "f1_be2").unsqueeze(2).broadcast_to([128, EP, D]))
        product(s.f1_wdup[:, :, c, :], s.f1_wdup[:, :, c, :], s.raw_bo.rearrange("p (e d) -> p e d", e=EP), ALU.add)
    step(p.tensor_scalar(cols4(s, "f1_be2"), cols4(s, "f1_be2"), -1.0, None, ALU.mult))
    wm = const(s, "winmask").rearrange("p (a w) -> p a w", a=2)
    for hf in range(2):
        step(p.tensor_copy(s.winmask[:, hf, :, :], wm[:, hf, :].unsqueeze(1).broadcast_to([128, NH, WIN])))
    step(p.tensor_copy(s.ident_b[:], const(s, "ident")))
    split(s.a0_qkh[:], s.a0_qkl[:], s.raw_a0_qk)
    split(flat(s.moe_w1h), flat(s.moe_w1l), s.raw_moe_w1)
    split(s.moe_b2h[:], s.moe_b2l[:], s.raw_moe_b2)
    split(flat(s.a1_qkh), flat(s.a1_qkl), s.raw_a1_qk)
    split(flat(s.f1_w1h), flat(s.f1_w1l), s.raw_f1_w1)
    step(p.tensor_copy(s.pick[:].rearrange("p a b c -> p (a b c)"), const(s, "pick")))


BN_DIAG = 13


CREDITS = 16


def done(n):
    return n + (1 + CREDITS)


def give_credits(eng, *semaphores):
    for sem in semaphores:
        eng.sem_inc(sem, CREDITS)


def row(t, n):
    return t[:, bass.ds(n, 1), :].rearrange("p a b -> p (a b)")


class Step:

    def __init__(self, turn, offset, unroll):
        self.turn, self.offset, self.unroll = turn, offset, unroll
        self.n = turn * unroll + offset
        self.k = offset % unroll

    def of(self, size):
        return self.turn * (self.unroll // size) + self.offset // size


def staggered(eng, count, unroll, *stages):
    most = max(lead for lead, _ in stages)
    for n in range(-most, 0):
        for lead, stage in stages:
            if n + lead >= 0:
                stage(Step(0, n + lead, unroll))
    last = max(1, -(-most // unroll))
    turns = count // unroll - last
    with eng.Fori(0, turns) as turn:
        for k in range(unroll):
            for lead, stage in stages:
                stage(Step(turn, k + lead, unroll))
    for k in range(last * unroll):
        for lead, stage in stages:
            if k + lead < last * unroll:
                stage(Step(turns, k + lead, unroll))


def pool_copy(nc, s, out, in_):
    ones = s.one[:] if len(in_.shape) == 2 else s.one[:].unsqueeze(2)
    return nc.gpsimd.tensor_tensor(out, in_, ones.broadcast_to(in_.shape), ALU.mult)


def spectral_norm(nc, s, a):
    with ExitStack() as ctx:
        def sb(name, shape, dt=F32):
            return [ctx.enter_context(nc.sbuf_tensor(f"sn_{name}{k}", shape, dt)) for k in range(4)]

        def ps(name):
            return [ctx.enter_context(nc.psum_tensor(f"sn_{name}{k}", [128, T], F32)) for k in range(4)]

        def sem(name):
            return ctx.enter_context(nc.semaphore("sn_" + name))

        loads = later_loads(s, a)
        wh, wl = sb("wh", [128, HID], F32R), sb("wl", [128, HID], F32R)
        sq, ln, rstd = sb("sq", [128, T]), sb("ln", [128, T]), sb("rstd", [128, T])
        hid, var = ps("hid"), ps("var")
        s_wh, s_wl, s_hid, s_sq, s_var, s_ln, s_rstd, s_z = [sem(x) for x in ("wh", "wl", "hid", "sq", "var", "ln", "rstd", "z")]
        block = ctx.enter_context(nc.Block())

        @block.gpsimd
        def _(pool):
            give_credits(pool, s_wh)

            def weights(at):
                n, k = at.n, at.k
                phase = s.phase[:, bass.ds(n, 1)]
                pool.wait_ge(s_wl, done(n - 4))
                pool.wait_ge(s_hid, done(n - 4))
                nc.gpsimd.tensor_tensor(wh[k][:], s.w1s[:], phase.broadcast_to([128, HID]), ALU.mult).then_inc(s_wh, 1)

            staggered(nc.gpsimd, NB, 4, (0, weights))
            pool.wait_ge(s.loaded, 16 * len(loads))
            nc.gpsimd.tensor_scalar(s.bn_var[:, 0, :], cols4(s, "f1_v1"), BN_EPS, None, ALU.add).then_inc(s.bn_ready, 1)
            nc.gpsimd.tensor_scalar(s.bn_var[:, 1, :], cols4(s, "f1_v2"), BN_EPS, None, ALU.add).then_inc(s.bn_ready, 1)

        @block.sync
        def _(sp):
            for dst, src in loads:
                sp.dma_start(dst, src, allow_slow_non_contiguous=True).then_inc(s.loaded, 16)

        @block.tensor
        def _(te):
            give_credits(te, s_hid, s_var)

            def hidden(at):
                n, k = at.n, at.k
                te.wait_ge(s_wl, done(n))
                te.wait_ge(s_z, done(n - 4))
                nc.tensor.matmul(hid[k][:], wh[k][:], s.shift[:], start=True, stop=False)
                nc.tensor.matmul(hid[k][:], wl[k][:], s.shift[:], start=False, stop=True).then_inc(s_hid, 1)

            def variance(at):
                n, k = at.n, at.k
                te.wait_ge(s_sq, done(n))
                te.wait_ge(s_ln, done(n - 4))
                nc.tensor.matmul(var[k][:], const(s, "mean128"), sq[k][:], start=True, stop=True).then_inc(s_var, 1)

            staggered(nc.tensor, NB, 4, (2, variance), (4, hidden))

        @block.scalar
        def _(sc):
            sc.preload_act_table_set("natural_log_exp_and_others")
            give_credits(sc, s_sq, s_ln, s_rstd)

            def squares(at):
                n, k = at.n, at.k
                sc.wait_ge(s_hid, done(n))
                sc.wait_ge(s_var, done(n - 4))
                nc.scalar.activation(sq[k][:], hid[k][:], ACT.Square, bias=s.tok_bias[:, bass.ds(n, 1)]).then_inc(s_sq, 1)

            def logarithm(at):
                n, k = at.n, at.k
                sc.wait_ge(s_var, done(n))
                sc.wait_ge(s_rstd, done(n - 4))
                nc.scalar.activation(ln[k][:], var[k][:], ACT.Ln, bias=s.eps[:]).then_inc(s_ln, 1)

            def root(at):
                n, k = at.n, at.k
                sc.wait_ge(s_ln, done(n))
                sc.wait_ge(s_z, done(n - 4))
                nc.scalar.activation(rstd[k][:], ln[k][:], ACT.Exp, scale=-0.5).then_inc(s_rstd, 1)

            staggered(nc.scalar, NB, 4, (0, root), (1, logarithm), (3, squares))
            sc.wait_ge(s.bn_ready, 2)
            nc.scalar.activation(s.bn_scale, s.bn_var, ACT.Ln).then_inc(s.bn_ready, 1)
            sc.wait_ge(s.bn_ready, 3)
            nc.scalar.activation(s.bn_scale, s.bn_scale, ACT.Exp, scale=-0.5).then_inc(s.bn_ready, 1)

        @block.vector
        def _(ve):
            give_credits(ve, s_z, s_wl)

            def low(at):
                n, k = at.n, at.k
                ve.wait_ge(s_wh, done(n))
                ve.wait_ge(s_hid, done(n - 4))
                nc.vector.scalar_tensor_tensor(out=wl[k][:], in0=s.w1s[:], scalar=s.phase[:, bass.ds(n, 1)], in1=wh[k][:].bitcast(F32),
                                               op0=ALU.mult, op1=ALU.subtract).then_inc(s_wl, 1)

            def normalise(at):
                n, k = at.n, at.k
                ve.wait_ge(s_rstd, done(n))
                nc.vector.scalar_tensor_tensor(out=row(s.z, n), in0=hid[k][:], scalar=s.tok_bias[:, bass.ds(n, 1)],
                                               in1=rstd[k][:], op0=ALU.add, op1=ALU.mult).then_inc(s_z, 1)

            staggered(nc.vector, NB, 4, (4, low), (0, normalise))


def tokenizer_output(nc, s):
    with ExitStack() as ctx:
        g = [ctx.enter_context(nc.sbuf_tensor(f"to_g{k}", [128, 2, T], F32)) for k in range(4)]
        y = [ctx.enter_context(nc.psum_tensor(f"to_y{k}", [128, T], F32)) for k in range(4)]
        p_scale, p_bias = [ctx.enter_context(nc.psum_tensor("to_" + x, [128, 512], F32)) for x in ("scale", "bias")]
        s_g, s_y, s_h, s_derived, s_last, s_scaled = [ctx.enter_context(nc.semaphore("to_" + x)) for x in ("g", "y", "h", "derived", "last", "scaled")]
        block = ctx.enter_context(nc.Block())

        @block.scalar
        def _(sc):
            give_credits(sc, s_g)

            def gelu(at):
                sc.wait_ge(s_y, done(at.n - 4))
                nc.scalar.activation(g[at.k][:], s.z[:, bass.ds(at.n * 2, 2), :], ACT.Gelu, scale=col(s, "gamma"),
                                     bias=col(s, "beta")).then_inc(s_g, 1)

            staggered(nc.scalar, NP, 4, (0, gelu))

        @block.gpsimd
        def _(pool):
            n = [0]

            def step(ins):
                ins.then_inc(s_derived, 1)
                n[0] += 1
                pool.wait_ge(s_derived, n[0])

            derive_weights(nc, s, step)

        @block.tensor
        def _(te):
            give_credits(te, s_y)

            def product(at):
                te.wait_ge(s_g, done(at.n))
                te.wait_ge(s_h, done(at.n - 4))
                nc.tensor.matmul(y[at.k][0:64, :], s.tok_w2[:], g[at.k][:, 0, :], start=True, stop=True)
                nc.tensor.matmul(y[at.k][64:128, :], s.tok_w2[:], g[at.k][:, 1, :], start=True, stop=True).then_inc(s_y, 1)

            staggered(nc.tensor, NP, 4, (0, product))
            nc.tensor.matmul(p_bias[:, 0:1], s.a0_wp[:], col(s, "a0_bv"), start=True, stop=True).then_inc(s_last, 1)
            te.wait_ge(s_derived, BN_DIAG)
            nc.tensor.matmul(p_scale[:], const(s, "mean128"), s.feat[:], start=True, stop=True).then_inc(s_last, 1)

        @block.vector
        def _(ve):
            give_credits(ve, s_h)

            def bias(at):
                ve.wait_ge(s_y, done(at.n))
                nc.vector.tensor_scalar(row(s.h, at.n), y[at.k][:], col(s, "tok_b2"), None, ALU.add).then_inc(s_h, 1)

            staggered(nc.vector, NP, 4, (0, bias))
            ve.wait_ge(s_last, 1)
            nc.vector.tensor_tensor(col(s, "a0_bp"), p_bias[:, 0:1], col(s, "a0_bp"), ALU.add)
            ve.wait_ge(s_last, 2)
            w2 = s.f1_w2[:].rearrange("p a b -> p (a b)")
            nc.vector.scalar_tensor_tensor(out=w2, in0=p_scale[:], scalar=float(HID), in1=w2, op0=ALU.mult, op1=ALU.mult)
            nc.vector.memset(s.feat[:], 0.0).then_inc(s_scaled, 1)
            ve.wait_ge(s_scaled, 1)


def window_buffers(nc, ctx):
    q = [ctx.enter_context(nc.sbuf_tensor(f"na_q{k}", [128, 2, 2, TG], F32)) for k in range(2)]
    v = [ctx.enter_context(nc.sbuf_tensor(f"na_v{k}", [128, 2 * NT, 2, NH // 2, 18], F32))
         for k in range(2)]
    return q, v


def layer_norm(nc, s, tag, features=False, windows=None):
    with ExitStack() as ctx:
        def sb(name):
            return [ctx.enter_context(nc.sbuf_tensor(f"{tag}_{name}{k}", [128, T], F32)) for k in range(4)]

        sq, ln, rstd = sb("sq"), sb("ln"), sb("rstd")
        cen, var = [[ctx.enter_context(nc.psum_tensor(f"{tag}_{x}{k}", [128, T], F32)) for k in range(4)] for x in ("cen", "var")]
        s_cen, s_sq, s_var, s_ln, s_rstd, s_z, s_feat = [ctx.enter_context(nc.semaphore(f"{tag}_s_{x}"))
                                                         for x in ("cen", "sq", "var", "ln", "rstd", "z", "feat")]
        block = ctx.enter_context(nc.Block())

        @block.tensor
        def _(te):
            give_credits(te, s_cen, s_var)

            def centre(at):
                te.wait_ge(s_z, done(at.n - 4))
                nc.tensor.matmul(cen[at.k][:], const(s, "center"), row(s.h, at.n), start=True, stop=True).then_inc(s_cen, 1)

            def variance(at):
                te.wait_ge(s_sq, done(at.n))
                te.wait_ge(s_ln, done(at.n - 4))
                nc.tensor.matmul(var[at.k][:], const(s, "mean64"), sq[at.k][:], start=True, stop=True).then_inc(s_var, 1)

            staggered(nc.tensor, NP, 4, (2, variance), (4, centre))

        @block.scalar
        def _(sc):
            sc.preload_act_table_set("natural_log_exp_and_others")
            give_credits(sc, s_sq, s_ln, s_rstd)

            def squares(at):
                sc.wait_ge(s_cen, done(at.n))
                sc.wait_ge(s_var, done(at.n - 4))
                nc.scalar.activation(sq[at.k][:], cen[at.k][:], ACT.Square).then_inc(s_sq, 1)

            def logarithm(at):
                sc.wait_ge(s_var, done(at.n))
                sc.wait_ge(s_rstd, done(at.n - 4))
                nc.scalar.activation(ln[at.k][:], var[at.k][:], ACT.Ln, bias=s.eps[:]).then_inc(s_ln, 1)

            def root(at):
                sc.wait_ge(s_ln, done(at.n))
                sc.wait_ge(s_z, done(at.n - 4))
                nc.scalar.activation(rstd[at.k][:], ln[at.k][:], ACT.Exp, scale=-0.5).then_inc(s_rstd, 1)

            staggered(nc.scalar, NP, 4, (0, root), (1, logarithm), (3, squares))

        @block.vector
        def _(ve):
            give_credits(ve, s_z)

            def normalise(at):
                ve.wait_ge(s_rstd, done(at.n))
                nc.vector.tensor_tensor(row(s.z, at.n), cen[at.k][:], rstd[at.k][:], ALU.mult).then_inc(s_z, 1)

            staggered(nc.vector, NP, 4, (0, normalise))

        @block.gpsimd
        def _(pool):
            if windows:
                q, v = windows
                for t in (*q, *v):
                    nc.gpsimd.memset(t[:], 0.0).then_inc(s_feat, 1)
                pool.wait_ge(s_feat, 4)
                for t in v:
                    sums = t[:, :, :, :, 16:18].rearrange("p a b c d -> p (a b c) d")
                    nc.gpsimd.tensor_tensor(sums, sums, const(s, "vmask")[:, 16:18].unsqueeze(1).broadcast_to([128, 2 * NT * NH, 2]), ALU.add)\
                        .then_inc(s_feat, 1)
                pool.wait_ge(s_feat, 6)
            if features:
                give_credits(pool, s_feat)

                def add(at):
                    pool.wait_ge(s_z, done(at.n))
                    pool.wait_ge(s_feat, done(at.n - 1))
                    nc.gpsimd.tensor_tensor(s.feat[:], s.feat[:], row(s.z, at.n), ALU.add).then_inc(s_feat, 1)

                staggered(nc.gpsimd, NP, 4, (0, add))


def stack_high(nc, s, zs, zrow):
    return pool_copy(nc, s, zs[:], zrow.unsqueeze(1).broadcast_to([128, 2, T]))


def stack_low(nc, zs, zrow, b):
    own, other = slice(64 * b, 64 * b + 64), slice(64 - 64 * b, 128 - 64 * b)
    return nc.vector.tensor_tensor(zs[other, b, :], zrow[own, :], zs[own, b, :].bitcast(F32), ALU.subtract)


def neighbourhood_attention(nc, s, q, v):
    with ExitStack() as ctx:
        def sb(name, shape, dt=F32, n=2):
            return [ctx.enter_context(nc.sbuf_tensor(f"na_{name}{k}", shape, dt)) for k in range(n)]

        def ps(name, n=1):
            return [ctx.enter_context(nc.psum_tensor(f"na_{name}{k}", [128, 512], F32)) for k in range(n)]

        def sem(name):
            return ctx.enter_context(nc.semaphore("na_" + name))

        zt, zs = sb("zt", [128, T]), sb("zs", [128, 2, T], F32R)
        kk = sb("k", [128, 2, TG])
        kblk = [s.z[:, NP + NH * k:NP + NH * k + NH, :].rearrange("p h (two t) -> p h two t", two=2) for k in range(2)]
        diff, e = sb("diff", [128, NH * WIN]), sb("e", [128, NH * WIN])
        rowmax = sb("rowmax", [128, NH])
        et = sb("et", [128, NH // 2, 128])
        rden = sb("rden", [128, NH // 2, 2])
        on = sb("on", [128, 2, D])
        ot = sb("ot", [128, 2, TG])
        p_s, p_t, p_o, p_prep, p_out = ps("ps", 2), ps("pt", 2), ps("po", 2), ps("pprep")[0], ps("pout")[0]
        p_ot = p_out
        s_zt, s_high, s_low, s_prep, s_prepd, s_k, s_score, s_max, s_diff, s_e, s_et, s_etd, s_o, s_rden, s_on, s_ot, s_otd, s_out, s_h = [
            sem(x) for x in ("zt", "high", "low", "prep", "prepd", "k", "score", "max", "diff", "e", "et", "etd", "o", "rden", "on", "ot", "otd", "out", "h")]
        block = ctx.enter_context(nc.Block())
        PREP = 4

        def group(at):
            g = at.k % 8
            return g // 4, g // 2 % 2, g % 2

        def product(i, part):
            return i * PREP + part

        @block.gpsimd
        def _(pool):
            give_credits(pool, s_zt, s_high)

            def copy(at):
                if at.k % 8 == 0:
                    i = at.of(8)
                    pool.wait_ge(s_prep, done(product(i - 2, PREP - 1)))
                    stack_high(nc, s, zs[at.k // 8], row(s.z, i)).then_inc(s_high, 1)
                    pool_copy(nc, s, zt[at.k // 8][:], row(s.z, i)).then_inc(s_zt, 1)

            staggered(nc.gpsimd, 8 * NP, 16, (0, copy))

        @block.tensor
        def _(te):
            give_credits(te, s_prep, s_score, s_et, s_o, s_ot, s_out)

            def prepare_pair(at):
                if at.k % 2:
                    return
                part, b = at.k // 2 % PREP, at.k // 8
                i = at.of(8)
                if part == 0:
                    te.wait_ge(s_low, done(i))
                if part == 2:
                    te.wait_ge(s_zt, done(i))
                te.wait_ge(s_prepd, done(product(i, part) - 1))
                bank = p_prep
                if part < 2:
                    nc.tensor.matmul(bank[:], s.a0_qkh[:], zs[b][:, part, :], start=True, stop=False)
                    mm = nc.tensor.matmul(bank[:], s.a0_qkl[:], zs[b][:, part, :], start=False, stop=True)
                else:
                    for c in range(4):
                        for half in range(2):
                            first = part - 2 + DIL * window_start(4 * half + c)
                            window = zt[b][:, first:first + DIL * (WIN - 1) + 1:DIL]
                            mm = nc.tensor.matmul(bank[WIN * half:WIN * half + WIN, c * 128:c * 128 + 128], window, s.a0_wv[:],
                                                  start=True, stop=True, skip_group_check=True)
                mm.then_inc(s_prep, 1)

            def scores(at):
                par, half, b = group(at)
                te.wait_ge(s_diff, done(at.n - 2))
                if at.k % 8 == 0:
                    te.wait_ge(s_k, done(at.of(8)))
                bank = p_s[at.k % 2]
                nc.tensor.matmul(bank[:, 0:NH * WIN], s.ident_b[:], s.winmask[:, half, :, :], start=True, stop=False, skip_group_check=True)
                for c in range(4):
                    t = 4 * half + c
                    w = window_start(t)
                    mm = nc.tensor.matmul(bank[QT * c:QT * c + QT, 0:NH * WIN], q[at.k // 8][:, b, par, t * QT:t * QT + QT],
                                          kblk[at.k // 8][:, :, par, w:w + WIN], start=False, stop=True, skip_group_check=True)
                mm.then_inc(s_score, 1)

            def transposes(at):
                te.wait_ge(s_e, done(at.n))
                te.wait_ge(s_etd, done(at.n - 2))
                for c in range(NH // 2):
                    mm = nc.tensor.transpose(p_t[at.k % 2][0:2 * WIN, c * 128:c * 128 + 128],
                                             e[at.k % 2][:, c * 2 * WIN:(c + 1) * 2 * WIN], const(s, "ident"))
                mm.then_inc(s_et, 1)

            def values(at):
                par, half, b = group(at)
                te.wait_ge(s_etd, done(at.n))
                te.wait_ge(s_on, done(at.n - 2))
                for c in range(NH // 2):
                    for t in range(4):
                        mm = nc.tensor.matmul(p_o[at.k % 2][QT * t:QT * t + QT, c * 18:c * 18 + 18], et[at.k % 2][0:2 * WIN, c, QT * t:QT * t + QT],
                                              v[at.k // 8][0:2 * WIN, par * NT + 4 * half + t, b, c, :], start=True, stop=True)
                mm.then_inc(s_o, 1)

            def turn(at):
                if at.k % 2 == 1:
                    te.wait_ge(s_on, done(at.n))
                    te.wait_ge(s_otd, done(at.of(2) - 1))
                    if at.k % 8 == 1:
                        te.wait_ge(s_h, done(at.of(8) - 1))
                    nc.tensor.transpose(p_ot[:, 0:128], on[at.k // 2 % 2][:].rearrange("p a b -> p (a b)"), const(s, "ident")).then_inc(s_ot, 1)

            def project(at):
                if at.k % 8 == 7:
                    i = at.of(8)
                    te.wait_ge(s_otd, done(at.of(2)))
                    nc.tensor.matmul(p_out[:], s.a0_wp[:], ot[at.k // 8][:].rearrange("p a b -> p (a b)"), start=True, stop=True).then_inc(s_out, 1)

            staggered(nc.tensor, 8 * NP, 16, (6, transposes), (4, values), (1, project), (2, turn), (9, scores), (16, prepare_pair))

        @block.scalar
        def _(sc):
            sc.preload_act_table_set("natural_log_exp_and_others")
            give_credits(sc, s_e, s_etd, s_otd, s_prepd)

            def fetch_prepared(at):
                if at.k % 2:
                    return
                part, i, k = at.k // 2 % PREP, at.of(8), at.k // 8
                bank = p_prep
                sc.wait_ge(s_prep, done(product(i, part)))
                if part < 2:
                    if part == 0:
                        sc.wait_ge(s_k, done(i - 2))
                        sc.wait_ge(s_score, done(i * 8 - 9))
                    own = slice(64 * part, 64 * part + 64)
                    by_parity = bank[:].rearrange("p (t two) -> p two t", two=2)
                    nc.scalar.activation(q[k][own, part, :, :], by_parity[0:64], ACT.Identity, bias=s.cols[0:64, COLS["a0_bq"]:COLS["a0_bq"] + 1])
                    ins = nc.scalar.activation(kk[k][own, :, :], by_parity[64:128], ACT.Identity,
                                               bias=s.cols[64:128, COLS["a0_bk"]:COLS["a0_bk"] + 1])
                else:
                    if part == 2:
                        sc.wait_ge(s_o, done(i * 8 - 9))
                    for half in range(2):
                        first = (part - 2) * NT + 4 * half
                        for head in range(2):
                            values = bank[WIN * half:WIN * half + WIN, :].rearrange("p (a d) -> p a d", d=2 * DH)[:, :, DH * head:DH * head + DH]
                            out = v[k][WIN * head:WIN * head + WIN, first:first + 4, :, :, DH * head:DH * head + DH]
                            ins = nc.scalar.activation(out.rearrange("p a b c d -> p (a b c) d"), values, ACT.Copy)
                ins.then_inc(s_prepd, 1)

            def exponential(at):
                sc.wait_ge(s_diff, done(at.n))
                sc.wait_ge(s_et, done(at.n - 2))
                nc.scalar.activation(e[at.k % 2][:], diff[at.k % 2][:], ACT.Exp, scale=float(DH) ** -0.5).then_inc(s_e, 1)

            def fetch(at):
                sc.wait_ge(s_et, done(at.n))
                sc.wait_ge(s_o, done(at.n - 2))
                nc.scalar.activation(et[at.k % 2][0:2 * WIN, :, :].rearrange("p a b -> p (a b)"), p_t[at.k % 2][0:2 * WIN, :], ACT.Copy).then_inc(s_etd, 1)

            def fetch_output(at):
                if at.k % 2 == 1:
                    par, half, _ = group(at)
                    sc.wait_ge(s_ot, done(at.of(2)))
                    if at.k % 8 == 1:
                        sc.wait_ge(s_out, done(at.of(8) - 2))
                    nc.scalar.activation(ot[at.k // 8][:, par, half * 128:half * 128 + 128], p_ot[:, 0:128], ACT.Copy).then_inc(s_otd, 1)

            staggered(nc.scalar, 8 * NP, 16, (7, exponential), (5, fetch), (1, fetch_output), (15, fetch_prepared))

        @block.vector
        def _(ve):
            give_credits(ve, s_low, s_max, s_diff, s_k, s_rden, s_on, s_h)

            def low(at):
                if at.k % 8 == 0:
                    i = at.of(8)
                    ve.wait_ge(s_high, done(i))
                    stack_low(nc, zs[at.k // 8], row(s.z, i), 0)
                    stack_low(nc, zs[at.k // 8], row(s.z, i), 1).then_inc(s_low, 1)

            def keys_by_head(at):
                part, i, b = at.k % 8, at.of(8), at.k // 8
                if 3 <= part < 6:
                    if part == 3:
                        ve.wait_ge(s_prepd, done(product(i, 1)))
                        ve.wait_ge(s_score, done(i * 8 - 9))
                    for h in ((0, 1), (2, 3, 4), (5, 6, 7))[part - 3]:
                        ins = nc.vector.tensor_scalar(kblk[b][:, h, :, :], kk[b][:], const(s, "headmask")[:, h:h + 1], None, ALU.mult)
                    if part == 5:
                        ins.then_inc(s_k, 1)

            def maximum(at):
                ve.wait_ge(s_score, done(at.n))
                sc_ = p_s[at.k % 2][:, 0:NH * WIN].rearrange("p (h w) -> p h w", h=NH)
                nc.vector.tensor_reduce(rowmax[at.k % 2][:], sc_, AX, ALU.max).then_inc(s_max, 1)
                ve.wait_ge(s_max, done(at.n))
                ve.wait_ge(s_e, done(at.n - 2))
                nc.vector.tensor_tensor(diff[at.k % 2][:].rearrange("p (h w) -> p h w", h=NH), sc_,
                                        rowmax[at.k % 2][:].unsqueeze(2).broadcast_to([128, NH, WIN]), ALU.subtract).then_inc(s_diff, 1)

            def normalise(at):
                _, _, b = group(at)
                ve.wait_ge(s_o, done(at.n))
                o = p_o[at.k % 2][:, 0:72].rearrange("p (c d) -> p c d", c=NH // 2)
                nc.vector.reciprocal(rden[at.k % 2][:], o[:, :, 16:18]).then_inc(s_rden, 1)
                ve.wait_ge(s_rden, done(at.n))
                ve.wait_ge(s_ot, done(at.of(2) - 2))
                nc.vector.tensor_tensor(on[at.k // 2 % 2][:, b, :].rearrange("p (c h d) -> p c h d", c=NH // 2, h=2),
                                        o[:, :, 0:16].rearrange("p c (h d) -> p c h d", h=2),
                                        rden[at.k % 2][:].unsqueeze(3).broadcast_to([128, NH // 2, 2, DH]), ALU.mult).then_inc(s_on, 1)

            def residual(at):
                if at.k % 8 == 7:
                    i = at.of(8)
                    ve.wait_ge(s_out, done(i))
                    h = row(s.h, i).rearrange("p (t two) -> p two t", two=2)
                    nc.vector.scalar_tensor_tensor(out=h, in0=p_out[:].rearrange("p (two t) -> p two t", two=2), scalar=col(s, "a0_bp"),
                                                   in1=h, op0=ALU.add, op1=ALU.add).then_inc(s_h, 1)

            staggered(nc.vector, 8 * NP, 16, (16, low), (8, maximum), (15, keys_by_head), (3, normalise), (1, residual))


def mixture_of_experts(nc, s):
    with ExitStack() as ctx:
        def sb(name, shape, dt=F32, n=2):
            return [ctx.enter_context(nc.sbuf_tensor(f"me_{name}{k}", shape, dt)) for k in range(n)]

        def ps(name, n=2):
            return [ctx.enter_context(nc.psum_tensor(f"me_{name}{k}", [128, T], F32)) for k in range(n)]

        zs = sb("zs", [128, 2, T], F32R)
        groups = 2 * 4 * 2
        zr = sb("zr", [128, 2, T], n=1)[0]
        logits_t = sb("logits_t", [128, T], n=1)[0]
        logits, best, masked, picked, weights = [sb(x, [128, groups, NE], n=1)[0] for x in ("logits", "best", "masked", "picked", "weights")]
        high, first_of, second_of, top, gap, w_best, w_next = [
            sb(x, [128, groups] + ([NE] if x == "high" else []), F32R if x == "high" else F32, n=1)[0]
            for x in ("high", "first", "second", "top", "gap", "wbest", "wnext")]
        ct_in = sb("ctin", [128, 2, 4, 2 * 2 * NE], n=1)[0]
        ct = sb("ct", [128, T], F32R)
        g, gw = sb("g", [128, T], n=4), sb("gw", [128, T], n=4)
        p_1, p_c, p_y, p_t, p_r = ps("p1"), ps("pc"), ps("py"), ps("pt", 1)[0], ps("pr", 1)[0]
        s_zr, s_rl, s_lt, s_rt, s_route, s_gap, s_tanh, s_ctin = [ctx.enter_context(nc.semaphore("me_" + x)) for x in (
            "zr", "rl", "lt", "rt", "route", "gap", "tanh", "s_ctin")]
        ROUTE = 20
        s_zero, s_high, s_low, s_hz, s_t, s_ct, s_w1, s_c, s_g, s_gw, s_w2, s_h = [
            ctx.enter_context(nc.semaphore("me_" + x)) for x in ("zero", "high", "low", "hz", "t", "ct", "w1", "c", "g", "gw", "w2", "h")]
        block = ctx.enter_context(nc.Block())

        def where(at):
            return at.k % 8 // EP, at.k % EP

        @block.gpsimd
        def _(pool):
            nc.gpsimd.memset(logits_t[:], 0.0).then_inc(s_zero, 1)
            for t in ct:
                nc.gpsimd.memset(t[:].bitcast(F32), 0.0).then_inc(s_zero, 1)
            give_credits(pool, s_high, s_hz, s_zr)

            def router(at):
                if at.k == 0:
                    c = at.of(16)
                    pool.wait_ge(s_rl, done(c - 1))
                    pool_copy(nc, s, zr[:], s.z[:, bass.ds(c * 2, 2), :]).then_inc(s_zr, 1)

            def prepare(at):
                if at.k % 8 == 0:
                    i, k = at.of(8), at.k // 8
                    pool.wait_ge(s_w1, done(at.n - 9))
                    stack_high(nc, s, zs[k], row(s.z, i)).then_inc(s_high, 1)
                    nc.gpsimd.tensor_tensor(row(s.h, i), row(s.h, i), row(s.z, i), ALU.add).then_inc(s_hz, 1)

            staggered(nc.gpsimd, 8 * NP, 16, (24, router), (0, prepare))

        @block.tensor
        def _(te):
            give_credits(te, s_t, s_w1, s_c, s_w2, s_rl, s_rt)
            te.wait_ge(s_zero, 3)

            def logits_of(at):
                c = at.of(16)
                if at.k == 0:
                    te.wait_ge(s_zr, done(c))
                    te.wait_ge(s_route, ROUTE * c + (ROUTE * (CREDITS - 1) + 1))
                    for j in range(2):
                        mm = nc.tensor.matmul(p_r[32 * j:32 * j + 32, :], s.moe_wr[:, 0:32], zr[:, j, :], start=True, stop=True, skip_group_check=True)
                    mm.then_inc(s_rl, 1)
                if at.k == 2:
                    te.wait_ge(s_lt, done(c))
                    for tile in range(4):
                        mm = nc.tensor.transpose(p_r[:, tile * 128:tile * 128 + 128], logits_t[:, tile * 128:tile * 128 + 128], const(s, "ident"))
                    mm.then_inc(s_rt, 1)

            def turn(at):
                if at.k % 8 == 0:
                    i = at.of(8)
                    te.wait_ge(s_ctin, done(at.of(16)))
                    te.wait_ge(s_ct, done(i - 1))
                    for c in range(4):
                        mm = nc.tensor.transpose(p_t[0:4 * NE, c * 128:c * 128 + 128], ct_in[:, at.k // 8, c, :], const(s, "ident"))
                    mm.then_inc(s_t, 1)

            def first(at):
                b, ep = where(at)
                if at.k % 8 == 0:
                    te.wait_ge(s_low, done(at.of(8)))
                te.wait_ge(s_g, done(at.n - 2))
                z = zs[at.k // 8][:, b, :]
                nc.tensor.matmul(p_1[at.k % 2][:], s.moe_w1h[:, ep, :], z, start=True, stop=False)
                nc.tensor.matmul(p_1[at.k % 2][:], s.moe_w1l[:, ep, :], z, start=False, stop=True).then_inc(s_w1, 1)

            def spread(at):
                b, ep = where(at)
                if at.k % 8 == 0:
                    te.wait_ge(s_ct, done(at.of(8)))
                te.wait_ge(s_gw, done(at.n - 2))
                nc.tensor.matmul(p_c[at.k % 2][:], s.pick[:, b, ep, :], ct[at.k // 8][:], start=True, stop=True).then_inc(s_c, 1)

            def bias(at):
                if at.k % 8 == 0:
                    te.wait_ge(s_h, done(at.of(8) - 2))
                    y = p_y[at.k // 8][:]
                    nc.tensor.matmul(y, s.moe_b2h[:], ct[at.k // 8][:], start=True, stop=False, skip_group_check=True)
                    nc.tensor.matmul(y, s.moe_b2l[:], ct[at.k // 8][:], start=False, stop=False, skip_group_check=True)

            def second(at):
                b, ep = where(at)
                te.wait_ge(s_gw, done(at.n))
                nc.tensor.matmul(p_y[at.k // 8][64 * b:64 * b + 64, :], s.moe_w2[:, ep, :], gw[at.k % 4][:], start=False, stop=(ep == EP - 1),
                                 skip_group_check=True).then_inc(s_w2, 1)

            staggered(nc.tensor, 8 * NP, 16, (4, first), (3, spread), (2, bias), (1, second), (6, turn), (24, logits_of))

        @block.scalar
        def _(sc):
            give_credits(sc, s_ct, s_g, s_lt, s_tanh)

            def router(at):
                c = at.of(16)
                if at.k == 1:
                    sc.wait_ge(s_rl, done(c))
                    sc.wait_ge(s_rt, done(c - 1))
                    nc.scalar.activation(logits_t[0:64, :], p_r[0:64, :], ACT.Copy).then_inc(s_lt, 1)
                if at.k == 10:
                    sc.wait_ge(s_gap, done(c))
                    nc.scalar.activation(gap[:], gap[:], ACT.Tanh, scale=0.5).then_inc(s_tanh, 1)

            def gelu(at):
                _, ep = where(at)
                sc.wait_ge(s_w1, done(at.n))
                sc.wait_ge(s_gw, done(at.n - 4))
                nc.scalar.activation(g[at.k % 4][:], p_1[at.k % 2][:], ACT.Gelu, bias=col(s, "moe_b1", ep)).then_inc(s_g, 1)

            def fetch(at):
                if at.k % 8 == 0:
                    sc.wait_ge(s_t, done(at.of(8)))
                    sc.wait_ge(s_c, done(at.n - 9))
                    sc.wait_ge(s_w2, done(at.n - 9))
                    nc.scalar.activation(ct[at.k // 8][0:4 * NE, :], p_t[0:4 * NE, :], ACT.Copy).then_inc(s_ct, 1)

            sc.wait_ge(s_zero, 3)
            staggered(nc.scalar, 8 * NP, 16, (3, gelu), (5, fetch), (24, router))

        @block.vector
        def _(ve):
            give_credits(ve, s_low, s_gw, s_h, s_gap, s_ctin)
            ve.sem_inc(s_route, ROUTE * CREDITS)
            v = nc.vector

            def wide(x):
                return x[:].unsqueeze(2).broadcast_to([128, groups, NE])

            def router(at):
                c = at.of(16)
                start = ROUTE * c + ROUTE * CREDITS

                def link(m):
                    ve.wait_ge(s_route, start + m - 1)

                def linked(ins):
                    ins.then_inc(s_route, 1)

                rank = const(s, "rank").unsqueeze(1).broadcast_to([128, groups, NE])
                parts = ct_in[:].rearrange("p i c (b n) -> p (i c b) n", b=2)
                if at.k == 3:
                    ve.wait_ge(s_rt, done(c))
                    linked(v.tensor_copy(logits[:].rearrange("p (j c b) e -> p c j (b e)", j=2, c=4),
                                         p_r[:].rearrange("p (c j n) -> p c j n", c=4, j=4)[:, :, 0:2, 0:2 * NE]))
                if at.k == 4:
                    link(2)
                    linked(v.tensor_reduce(first_of[:], logits[:], AX, ALU.max))
                    link(3)
                    linked(v.tensor_tensor(best[:], logits[:], wide(first_of), ALU.is_equal))
                if at.k == 5:
                    link(4)
                    linked(v.tensor_tensor(best[:], best[:], rank, ALU.mult))
                    link(5)
                    linked(v.tensor_reduce(top[:], best[:], AX, ALU.max))
                if at.k == 6:
                    link(6)
                    linked(v.tensor_tensor(best[:], best[:], wide(top), ALU.is_equal))
                    link(7)
                    linked(v.scalar_tensor_tensor(out=masked[:], in0=best[:], scalar=-3.0e38, in1=logits[:], op0=ALU.mult, op1=ALU.add))
                if at.k == 7:
                    link(8)
                    linked(v.tensor_reduce(second_of[:], masked[:], AX, ALU.max))
                if at.k == 9:
                    link(9)
                    v.tensor_tensor(gap[:], first_of[:], second_of[:], ALU.subtract).then_inc(s_gap, 1)
                    linked(v.tensor_tensor(picked[:], masked[:], wide(second_of), ALU.is_equal))
                if at.k == 10:
                    link(10)
                    linked(v.tensor_tensor(picked[:], picked[:], rank, ALU.mult))
                    link(11)
                    linked(v.tensor_reduce(top[:], picked[:], AX, ALU.max))
                if at.k == 11:
                    link(12)
                    linked(v.tensor_tensor(picked[:], picked[:], wide(top), ALU.is_equal))
                    ve.wait_ge(s_tanh, done(c))
                    linked(v.tensor_scalar(w_best[:], gap[:], 0.5, 0.5, ALU.mult, ALU.add))
                if at.k == 12:
                    link(14)
                    linked(v.tensor_scalar(w_next[:], gap[:], -0.5, 0.5, ALU.mult, ALU.add))
                    link(15)
                    linked(v.tensor_tensor(best[:], best[:], wide(w_best), ALU.mult))
                if at.k == 13:
                    link(16)
                    linked(v.tensor_tensor(picked[:], picked[:], wide(w_next), ALU.mult))
                    link(17)
                    linked(v.tensor_tensor(weights[:], best[:], picked[:], ALU.add))
                if at.k == 14:
                    link(18)
                    linked(v.tensor_copy(high[:], weights[:]))
                    link(19)
                    ve.wait_ge(s_t, done(c * 2 - 1))
                    linked(v.tensor_copy(parts[:, :, 0:NE], high[:].bitcast(F32)))
                if at.k == 15:
                    link(20)
                    linked(v.tensor_tensor(parts[:, :, NE:2 * NE], weights[:], high[:].bitcast(F32), ALU.subtract))
                    link(21)
                    ve.sem_inc(s_ctin, 1)

            def low(at):
                if at.k % 8 == 0:
                    i = at.of(8)
                    ve.wait_ge(s_high, done(i))
                    stack_low(nc, zs[at.k // 8], row(s.z, i), 0)
                    stack_low(nc, zs[at.k // 8], row(s.z, i), 1).then_inc(s_low, 1)

            def weigh(at):
                ve.wait_ge(s_g, done(at.n))
                ve.wait_ge(s_c, done(at.n))
                ve.wait_ge(s_w2, done(at.n - 4))
                nc.vector.tensor_tensor(gw[at.k % 4][:], p_c[at.k % 2][:], g[at.k % 4][:], ALU.mult).then_inc(s_gw, 1)

            def residual(at):
                if at.k % 8 == 7:
                    i = at.of(8)
                    ve.wait_ge(s_w2, done(at.n))
                    ve.wait_ge(s_hz, done(i))
                    nc.vector.tensor_tensor(row(s.h, i), p_y[at.k // 8][:], row(s.h, i), ALU.add).then_inc(s_h, 1)

            staggered(nc.vector, 8 * NP, 16, (2, weigh), (0, residual), (8, low), (24, router))


def decayed_attention(nc, s):
    with ExitStack() as ctx:
        def sb(name, shape, dt=F32, n=4):
            return [ctx.enter_context(nc.sbuf_tensor(f"da_{name}{k}", shape, dt)) for k in range(n)]

        def ps(name, n=1):
            return [ctx.enter_context(nc.psum_tensor(f"da_{name}{k}", [128, T], F32)) for k in range(n)]

        zt = sb("zt", [128, T])
        zs = sb("zs", [128, 2, T], F32R)
        qh, ql, kk = sb("qh", [128, T], F32R), sb("ql", [128, T], F32R), sb("k", [128, T], F32R)
        vt = [s.z[:, NP + k, :].rearrange("p (c n) -> p c n", c=4) for k in range(4)]
        width = [T - 128 * j for j in range(4)]
        free = s.z[:, NP + 4:NP + 10, :].rearrange("p a b -> p (a b)")
        sm = [[free[:, 3 * T * k + sum(width[:j]):3 * T * k + sum(width[:j + 1])] for j in range(4)] for k in range(2)]
        p_q, p_k, p_v, p_s, p_o = ps("pq")[0], ps("pk")[0], ps("pv")[0], ps("ps", 3), ps("po", 2)
        bank = [p_s[0][:, 0:width[0]], p_s[1][:, 0:width[1]], p_s[2][:, 0:width[2]], p_s[2][:, width[2]:width[2] + width[3]]]
        s_zt, s_high, s_low, s_q, s_k, s_ql, s_kh, s_kl, s_v, s_vt, s_s, s_sm, s_o, s_h, s_qh = [
            ctx.enter_context(nc.semaphore("da_" + x)) for x in ("s_zt", "high", "low", "q", "k", "ql", "kh", "kl", "v", "s_vt", "s", "sm", "o", "h", "s_qh")]
        block = ctx.enter_context(nc.Block())

        @block.gpsimd
        def _(pool):
            give_credits(pool, s_zt, s_high)

            def prepare(at):
                i = at.of(2)
                if at.k % 2 == 0:
                    pool.wait_ge(s_v, done(i - 4))
                    pool.wait_ge(s_k, done(at.n - 7))
                    pool_copy(nc, s, zt[at.k // 2][:], row(s.z, i)).then_inc(s_zt, 1)
                    stack_high(nc, s, zs[at.k // 2], row(s.z, i)).then_inc(s_high, 1)

            staggered(nc.gpsimd, NB, 8, (0, prepare))

        @block.tensor
        def _(te):
            give_credits(te, s_q, s_k, s_v, s_s, s_o)

            def queries_keys(at):
                te.wait_ge(s_low, done(at.n))
                z = zs[at.k // 2][:, at.k % 2, :]
                te.wait_ge(s_ql, done(at.n - 1))
                nc.tensor.matmul(p_q[:], s.a1_qkh[:, 0, :], z, start=True, stop=False)
                nc.tensor.matmul(p_q[:], s.a1_qkl[:, 0, :], z, start=False, stop=True).then_inc(s_q, 1)
                te.wait_ge(s_kl, done(at.n - 1))
                nc.tensor.matmul(p_k[:], s.a1_qkh[:, 1, :], z, start=True, stop=False)
                nc.tensor.matmul(p_k[:], s.a1_qkl[:, 1, :], z, start=False, stop=True).then_inc(s_k, 1)

            def values(at):
                if at.k % 2 == 0:
                    i = at.of(2)
                    te.wait_ge(s_zt, done(i))
                    te.wait_ge(s_vt, done(i - 1))
                    for c in range(4):
                        mm = nc.tensor.matmul(p_v[:, c * 128:c * 128 + 128], zt[at.k // 2][:, c * 128:c * 128 + 128], s.a1_wv[:], start=True, stop=True)
                    mm.then_inc(s_v, 1)

            def scores(at):
                te.wait_ge(s_kl, done(at.n))
                for j in range(4):
                    if j < 3:
                        te.wait_ge(s_sm, done(4 * at.n + (-4, -3, -1)[j]))
                    keys = kk[at.k % 4][:, 128 * j:128 * j + 128]
                    nc.tensor.matmul(bank[j], keys, qh[at.k % 4][:, 128 * j:], start=True, stop=False, skip_group_check=True)
                    mm = nc.tensor.matmul(bank[j], keys, ql[at.k % 4][:, 128 * j:], start=False, stop=True, skip_group_check=True)
                    if j != 2:
                        mm.then_inc(s_s, 1)

            def outputs(at):
                b = at.k % 2
                te.wait_ge(s_sm, done(4 * at.n + 3))
                if b == 0:
                    te.wait_ge(s_vt, done(at.of(2)))
                    te.wait_ge(s_h, done(at.of(2) - 2))
                for j in range(4):
                    mm = nc.tensor.matmul(p_o[at.k // 2 % 2][64 * b:64 * b + 64, 128 * j:], vt[at.k // 2][:, j, 64 * b:64 * b + 64], sm[at.k % 2][j],
                                          start=(j == 0), stop=(j == 3), skip_group_check=True)
                mm.then_inc(s_o, 1)

            staggered(nc.tensor, NB, 8, (1, outputs), (3, scores), (6, queries_keys), (6, values))

        @block.scalar
        def _(sc):
            give_credits(sc, s_qh, s_kh)

            def high(at):
                sc.wait_ge(s_q, done(at.n))
                sc.wait_ge(s_s, done(3 * at.n - 10))
                nc.scalar.activation(qh[at.k % 4][:], p_q[:], ACT.Identity, bias=col(s, "a1_bq")).then_inc(s_qh, 1)
                sc.wait_ge(s_k, done(at.n))
                nc.scalar.activation(kk[at.k % 4][:], p_k[:], ACT.Identity, bias=col(s, "a1_bk")).then_inc(s_kh, 1)

            staggered(nc.scalar, NB, 8, (5, high))

        @block.vector
        def _(ve):
            give_credits(ve, s_low, s_ql, s_kl, s_vt, s_sm, s_h)

            def low(at):
                ve.wait_ge(s_high, done(at.of(2)))
                stack_low(nc, zs[at.k // 2], row(s.z, at.of(2)), at.k % 2).then_inc(s_low, 1)

            def split(at):
                up = slice(64, 128)
                ve.wait_ge(s_qh, done(at.n))
                nc.vector.scalar_tensor_tensor(out=ql[at.k % 4][:], in0=p_q[:], scalar=col(s, "a1_bq"), in1=qh[at.k % 4][:].bitcast(F32),
                                               op0=ALU.add, op1=ALU.subtract).then_inc(s_ql, 1)
                ve.wait_ge(s_kh, done(at.n))
                nc.vector.scalar_tensor_tensor(out=kk[at.k % 4][up, :], in0=p_k[up, :], scalar=s.cols[up, COLS["a1_bk"]:COLS["a1_bk"] + 1],
                                               in1=kk[at.k % 4][up, :].bitcast(F32), op0=ALU.add, op1=ALU.subtract).then_inc(s_kl, 1)

            def values(at):
                if at.k % 2 == 0:
                    ve.wait_ge(s_v, done(at.of(2)))
                    ve.wait_ge(s_o, done(at.n - 7))
                    nc.vector.tensor_tensor(vt[at.k // 2], p_v[:].rearrange("p (c n) -> p c n", c=4),
                                            s.a1_bv[:].rearrange("p a b -> p (a b)").unsqueeze(1).broadcast_to([128, 4, 128]), ALU.add).then_inc(s_vt, 1)

            def decay(at):
                ve.wait_ge(s_o, done(at.n - 2))
                for j in range(4):
                    ve.wait_ge(s_s, done(3 * at.n + min(j, 2)))
                    nc.vector.tensor_tensor(sm[at.k % 2][j], bank[j], const(s, "decay")[:, 0:width[j]], ALU.mult).then_inc(s_sm, 1)

            def residual(at):
                if at.k % 2 == 1:
                    ve.wait_ge(s_o, done(at.n))
                    h = row(s.h, at.of(2))
                    nc.vector.tensor_tensor(h, p_o[at.k // 2 % 2][:], h, ALU.add).then_inc(s_h, 1)

            staggered(nc.vector, NB, 8, (2, decay), (5, split), (7, low), (5, values), (0, residual))


def soft_router(nc, s):
    with ExitStack() as ctx:
        def sb(name, shape):
            return ctx.enter_context(nc.sbuf_tensor("sr_" + name, shape, F32))

        logits, w = sb("logits", [128, 4, NE]), sb("w", [128, 4, NE])
        top, total = sb("top", [128, 4]), sb("total", [128, 4])
        wide_w = sb("wide", [128, 4, NE, D])
        ps = [ctx.enter_context(nc.psum_tensor(f"sr_p{k}", [128, 4, 128], F32)) for k in range(6)]
        s_p, s_v, s_a = [ctx.enter_context(nc.semaphore("sr_" + x)) for x in ("pe", "dve", "act")]
        block = ctx.enter_context(nc.Block())

        @block.tensor
        def _(te):
            for c in range(4):
                nc.tensor.matmul(ps[0][:, c, :], s.feat[:, c * 128:c * 128 + 128], s.f1_wr[:], start=True, stop=True).then_inc(s_p, 1)
            te.wait_ge(s_v, 8)
            for ep in range(EP):
                for c in range(4):
                    nc.tensor.matmul(ps[1 + ep][:, c, :], wide_w[:, c, 2 * ep:2 * ep + 2, :].rearrange("p a b -> p (a b)"), const(s, "ident"),
                                     start=True, stop=True).then_inc(s_p, 1)
            for ep in range(EP):
                te.wait_ge(s_a, ep + 2)
                nc.tensor.matmul(ps[5][:].rearrange("p a b -> p (a b)"), s.f1_wdup[:, ep, :, :].rearrange("p a b -> p (a b)"), s.f1_w[:, ep, :],
                                 start=(ep == 0), stop=(ep == EP - 1)).then_inc(s_p, 1)

        @block.scalar
        def _(sc):
            sc.preload_act_table_set("natural_log_exp_and_others")
            sc.wait_ge(s_v, 4)
            nc.scalar.activation(w[:], logits[:], ACT.Exp).then_inc(s_a, 1)
            for ep in range(EP):
                sc.wait_ge(s_p, 4 + 4 * (ep + 1))
                nc.scalar.activation(s.f1_w[:, ep, :], ps[1 + ep][:].rearrange("p a b -> p (a b)"), ACT.Copy).then_inc(s_a, 1)
            sc.wait_ge(s_p, 24)
            nc.scalar.activation(s.f1_r, ps[5][:].rearrange("p a b -> p (a b)"), ACT.Copy).then_inc(s_a, 1)

        @block.vector
        def _(ve):
            n = [0]

            def step(ins):
                ins.then_inc(s_v, 1)
                n[0] += 1
                ve.wait_ge(s_v, n[0])

            def wide(t):
                return t[:].unsqueeze(2).broadcast_to([128, 4, NE])

            v = nc.vector
            ve.wait_ge(s_p, 4)
            step(v.tensor_scalar(logits[:], ps[0][:, :, 0:NE], 1.0 / NB, None, ALU.mult))
            step(v.tensor_tensor(logits[:], logits[:], s.f1_br[:].unsqueeze(1).broadcast_to([128, 4, NE]), ALU.add))
            step(v.tensor_reduce(top[:], logits[:], AX, ALU.max))
            step(v.tensor_tensor(logits[:], logits[:], wide(top), ALU.subtract))
            ve.wait_ge(s_a, 1)
            step(v.tensor_reduce(total[:], w[:], AX, ALU.add))
            step(v.reciprocal(total[:], total[:]))
            step(v.tensor_tensor(w[:], w[:], wide(total), ALU.mult))
            step(v.tensor_copy(wide_w[:].rearrange("p a b c -> p (a b) c"), w[:].rearrange("p a b -> p (a b)").unsqueeze(2).broadcast_to([128, 4 * NE, D])))


def soft_experts(nc, s, out):
    with ExitStack() as ctx:
        def sb(name, shape, dt=F32, n=2):
            return [ctx.enter_context(nc.sbuf_tensor(f"se_{name}{k}", shape, dt)) for k in range(n)]

        def ps(name, n=2):
            return [ctx.enter_context(nc.psum_tensor(f"se_{name}{k}", [128, T], F32)) for k in range(n)]

        zs = sb("zs", [128, 2, T], F32R)
        w2h, w2l = [sb("w2" + x, [128, EP, 128], F32R, n=1)[0] for x in "hl"]
        a1, a1h, a1l = sb("a1", [128, T]), sb("a1h", [128, T], F32R, n=4), sb("a1l", [128, T], F32R, n=4)
        a2 = sb("a2", [128, T], n=4)
        res, rows = sb("res", [128, T]), sb("rows", [128, 2, 4, D])
        p_1, p_2, p_y, p_t = ps("p1"), ps("p2"), ps("py"), ps("pt", 1)[0]
        s_high, s_low, s_hr, s_split, s_w1, s_a1, s_a1h, s_a1l, s_w2, s_a2, s_wo, s_res, s_t, s_rows, *s_out = [
            ctx.enter_context(nc.semaphore("se_" + x)) for x in ("high", "low", "hr", "split", "w1", "s_a1", "s_a1h", "s_a1l", "w2", "s_a2", "wo", "s_res", "t", "s_rows", "out0", "out1")]
        block = ctx.enter_context(nc.Block())

        def where(at):
            return at.k % 8 // EP, at.k % EP

        @block.gpsimd
        def _(pool):
            give_credits(pool, s_high, s_hr)

            def prepare(at):
                if at.k % 8 == 0:
                    i, k = at.of(8), at.k // 8
                    pool.wait_ge(s_w1, done(at.n - 9))
                    stack_high(nc, s, zs[k], row(s.z, i)).then_inc(s_high, 1)
                    nc.gpsimd.tensor_tensor(row(s.h, i), row(s.h, i), s.f1_r, ALU.add).then_inc(s_hr, 1)

            staggered(nc.gpsimd, 8 * NP, 16, (0, prepare))

        @block.tensor
        def _(te):
            give_credits(te, s_w1, s_w2, s_wo, s_t)
            te.wait_ge(s_split, 2)

            def first(at):
                b, ep = where(at)
                if at.k % 8 == 0:
                    te.wait_ge(s_low, done(at.of(8)))
                te.wait_ge(s_a1h, done(at.n - 2))
                z = zs[at.k // 8][:, b, :]
                nc.tensor.matmul(p_1[at.k % 2][:], s.f1_w1h[:, ep, :], z, start=True, stop=False)
                nc.tensor.matmul(p_1[at.k % 2][:], s.f1_w1l[:, ep, :], z, start=False, stop=True).then_inc(s_w1, 1)

            def second(at):
                _, ep = where(at)
                te.wait_ge(s_a1l, done(at.n))
                te.wait_ge(s_a2, done(at.n - 2))
                nc.tensor.matmul(p_2[at.k % 2][:], w2h[:, ep, :], a1h[at.k % 4][:], start=True, stop=False)
                nc.tensor.matmul(p_2[at.k % 2][:], w2l[:, ep, :], a1h[at.k % 4][:], start=False, stop=False)
                nc.tensor.matmul(p_2[at.k % 2][:], w2h[:, ep, :], a1l[at.k % 4][:], start=False, stop=True).then_inc(s_w2, 1)

            def third(at):
                b, ep = where(at)
                te.wait_ge(s_a2, done(at.n))
                if at.k % 8 == 0:
                    te.wait_ge(s_res, done(at.of(8) - 2))
                nc.tensor.matmul(p_y[at.k // 8][64 * b:64 * b + 64, :], s.f1_wo[:, ep, :], a2[at.k % 4][:], start=(ep == 0), stop=(ep == EP - 1),
                                 skip_group_check=True).then_inc(s_wo, 1)

            def turn(at):
                if at.k % 8 == 7:
                    i = at.of(8)
                    te.wait_ge(s_res, done(i))
                    te.wait_ge(s_rows, done(i - 1))
                    for c in range(4):
                        mm = nc.tensor.transpose(p_t[:, c * 128:c * 128 + 128], res[at.k // 8][:, c::4], const(s, "ident"))
                    mm.then_inc(s_t, 1)

            staggered(nc.tensor, 8 * NP, 16, (8, first), (5, second), (3, third), (1, turn))

        @block.scalar
        def _(sc):
            give_credits(sc, s_a1, s_a1h, s_rows)
            nc.scalar.activation(w2h[:], s.f1_w2[:], ACT.Copy).then_inc(s_split, 1)

            def relu(at):
                _, ep = where(at)
                sc.wait_ge(s_w1, done(at.n))
                sc.wait_ge(s_a1l, done(at.n - 2))
                sc.wait_ge(s_w2, done(at.n - 4))
                scale, shift = col(s, "f1_g1", ep), col(s, "f1_be1", ep)
                nc.scalar.activation(a1[at.k % 2][:], p_1[at.k % 2][:], ACT.Relu, scale=scale, bias=shift).then_inc(s_a1, 1)
                nc.scalar.activation(a1h[at.k % 4][:], p_1[at.k % 2][:], ACT.Relu, scale=scale, bias=shift).then_inc(s_a1h, 1)

            def fetch(at):
                if at.k % 8 == 7:
                    i = at.of(8)
                    sc.wait_ge(s_t, done(i))
                    sc.wait_ge(s_out[at.k // 8], at.of(16) * 16 + 16)
                    nc.scalar.activation(rows[at.k // 8][:].rearrange("p b t c -> p t b c"), p_t[:].rearrange("p (t b c) -> p t b c", t=4, b=2),
                                         ACT.Copy).then_inc(s_rows, 1)

            staggered(nc.scalar, 8 * NP, 16, (7, relu), (0, fetch))

        @block.vector
        def _(ve):
            give_credits(ve, s_low, s_a1l, s_a2, s_res)
            ve.wait_ge(s_split, 1)
            nc.vector.tensor_tensor(w2l[:], s.f1_w2[:], w2h[:].bitcast(F32), ALU.subtract).then_inc(s_split, 1)

            def low(at):
                if at.k % 8 == 0:
                    i = at.of(8)
                    ve.wait_ge(s_high, done(i))
                    stack_low(nc, zs[at.k // 8], row(s.z, i), 0)
                    stack_low(nc, zs[at.k // 8], row(s.z, i), 1).then_inc(s_low, 1)

            def split(at):
                ve.wait_ge(s_a1, done(at.n))
                ve.wait_ge(s_a1h, done(at.n))
                ve.wait_ge(s_w2, done(at.n - 4))
                nc.vector.tensor_tensor(a1l[at.k % 4][:], a1[at.k % 2][:], a1h[at.k % 4][:].bitcast(F32), ALU.subtract).then_inc(s_a1l, 1)

            def weigh(at):
                _, ep = where(at)
                ve.wait_ge(s_w2, done(at.n))
                ve.wait_ge(s_wo, done(at.n - 4))
                nc.vector.scalar_tensor_tensor(out=a2[at.k % 4][:], in0=p_2[at.k % 2][:], scalar=col(s, "f1_be2", ep), in1=s.f1_w[:, ep, :],
                                               op0=ALU.max, op1=ALU.mult).then_inc(s_a2, 1)

            def residual(at):
                if at.k % 8 == 7:
                    i = at.of(8)
                    ve.wait_ge(s_wo, done(at.n))
                    ve.wait_ge(s_hr, done(i))
                    ve.wait_ge(s_t, done(i - 2))
                    nc.vector.tensor_tensor(res[at.k // 8][:], p_y[at.k // 8][:], row(s.h, i), ALU.add).then_inc(s_res, 1)

            staggered(nc.vector, 8 * NP, 16, (6, split), (4, weigh), (2, residual), (11, low))

        @block.sync
        def _(sp):
            for x in s_out:
                sp.sem_inc(x, 16)

            def store(at):
                sp.wait_ge(s_rows, done(at.n))
                sp.dma_start(out[bass.ds(at.n * 2, 2), :, :].rearrange("b (p t) c -> p b (t c)", t=4),
                             rows[at.k][:].rearrange("p b t c -> p b (t c)")).then_inc(s_out[at.k], 16)

            staggered(nc.sync, NP, 2, (0, store))
            for x in s_out:
                sp.wait_ge(x, 16 * (1 + NP // 2))


def build(nc, a, out):
    with ExitStack() as ctx:
        s = allocate(nc, ctx)
        prepare(nc, s, a)
        spectral_norm(nc, s, a)
        tokenizer_output(nc, s)
        with ExitStack() as inner:
            q, v = window_buffers(nc, inner)
            layer_norm(nc, s, "ln0", windows=(q, v))
            neighbourhood_attention(nc, s, q, v)
        layer_norm(nc, s, "ln1")
        mixture_of_experts(nc, s)
        layer_norm(nc, s, "ln2")
        decayed_attention(nc, s)
        layer_norm(nc, s, "ln3", features=True)
        soft_router(nc, s)
        soft_experts(nc, s, out)


_INS = ['x', 'L0_tok_freq_bands', 'L0_tok_w1', 'L0_tok_b1', 'L0_tok_gamma', 'L0_tok_beta', 'L0_tok_w2', 'L0_tok_b2',
        'L0_attn_w_qkv', 'L0_attn_b_qkv', 'L0_attn_w_proj', 'L0_attn_b_proj', 'L0_ffn_router_w', 'L0_ffn_w1', 'L0_ffn_b1',
        'L0_ffn_w2', 'L0_ffn_b2', 'L1_attn_Wqkv', 'L1_attn_bqkv', 'L1_ffn_Wr', 'L1_ffn_br', 'L1_ffn_W1', 'L1_ffn_b1',
        'L1_ffn_g1', 'L1_ffn_be1', 'L1_ffn_m1', 'L1_ffn_v1', 'L1_ffn_W2', 'L1_ffn_b2', 'L1_ffn_g2', 'L1_ffn_be2',
        'L1_ffn_m2', 'L1_ffn_v2', 'L1_ffn_Wo', 'L1_ffn_bo']


def kernel(**inputs):
    import concourse.bacc as bacc
    from concourse.bass_utils import run_bass_kernel_spmd

    nc = bacc.Bacc("TRN2", target_bir_lowering=False, num_devices=1)
    arrays, aps = {}, {}
    for name in _INS + ["const"]:
        array = constants() if name == "const" else np.ascontiguousarray(inputs[name])
        arrays[f"in_{name}"] = array
        aps[name] = nc.dram_tensor(f"in_{name}", array.shape, mybir.dt.from_np(array.dtype), kind="ExternalInput").ap()
    out = nc.dram_tensor("out", (NB, T, D), F32, kind="ExternalOutput").ap()
    build(nc, aps, out)
    r = run_bass_kernel_spmd(nc, [arrays], core_ids=[0])
    return r.results[0]["out"]
```
